# Optimizing a Trainium2 kernel written in Bass

```python
import numpy as np
import jax
import jax.numpy as jnp

def _softmax(x, axis=-1):
    return jax.nn.softmax(x, axis=axis)

def _gelu(x):
    return jax.nn.gelu(x, approximate=True)

def _silu(x):
    return jax.nn.silu(x)

def _sigmoid(x):
    return jax.nn.sigmoid(x)

def _layernorm(x, axis=-1, eps=1e-05):
    m = jnp.mean(x, axis=axis, keepdims=True)
    v = jnp.var(x, axis=axis, keepdims=True)
    return (x - m) / jnp.sqrt(v + eps)

def _scatter_add(tgt, idx, src, axis=0):
    return tgt.at[idx].add(src)

def _segment_sum(src, seg, n):
    return jax.ops.segment_sum(src, seg, n)
kernel_name = 'mk_adaln_d2_jaxref_r4_5eec66'

def setup_inputs(seed: int=0):
    np.random.seed(seed)
    _w = jnp.asarray

    def _L0_attn_setup():
        import jax, jax.numpy as jnp
        import numpy as np
        H = 256
        F = 1024
        B, S = (4, 1024)
        EPS = 1e-05

        def _layernorm(x, scale, bias):
            mu = jnp.mean(x, axis=-1, keepdims=True)
            var = jnp.var(x, axis=-1, keepdims=True)
            return (x - mu) * jax.lax.rsqrt(var + EPS) * scale + bias
        key = jax.random.key(seed)
        ks = jax.random.split(key, 4)
        x = jax.random.normal(ks[0], (B, S, H), dtype=jnp.float32)
        W_ret = jax.random.normal(ks[1], (H, H), dtype=jnp.float32) * 0.02
        b_ret = jnp.zeros((H,), dtype=jnp.float32)
        ln1_scale = jnp.ones((H,), dtype=jnp.float32)
        ln1_bias = jnp.zeros((H,), dtype=jnp.float32)
        W1 = jax.random.normal(ks[2], (H, F), dtype=jnp.float32) * 0.02
        b1 = jnp.zeros((F,), dtype=jnp.float32)
        W2 = jax.random.normal(ks[3], (F, H), dtype=jnp.float32) * 0.02
        b2 = jnp.zeros((H,), dtype=jnp.float32)
        ln2_scale = jnp.ones((H,), dtype=jnp.float32)
        ln2_bias = jnp.zeros((H,), dtype=jnp.float32)
        return {'x': x, 'W_ret': W_ret, 'b_ret': b_ret, 'ln1_scale': ln1_scale, 'ln1_bias': ln1_bias, 'W1': W1, 'b1': b1, 'W2': W2, 'b2': b2, 'ln2_scale': ln2_scale, 'ln2_bias': ln2_bias}
    _L0_attn_in = _L0_attn_setup()

    def _L0_ffn_setup():
        import jax, jax.numpy as jnp
        import numpy as np
        DIM = 256

        def _reference_tuple_inner(x, W_r, W_k, W_v, mu_r, mu_k):
            B, T, C = x.shape
            x_prev = jnp.concatenate([jnp.zeros((B, 1, C), x.dtype), x[:, :-1, :]], axis=1)
            xr = mu_r * x + (1.0 - mu_r) * x_prev
            xk = mu_k * x + (1.0 - mu_k) * x_prev
            r = jax.nn.sigmoid(jnp.einsum('btc,dc->btd', xr, W_r))
            k = jnp.einsum('btc,dc->btd', xk, W_k)
            k_act = jnp.square(jax.nn.relu(k))
            out = r * jnp.einsum('btc,dc->btd', k_act, W_v)
            new_state = x[:, -1, :]
            return (out, new_state)
        key = jax.random.key(seed)
        ks = jax.random.split(key, 6)
        B, T, C = (8, 512, DIM)
        x = jax.random.normal(ks[0], (B, T, C), dtype=jnp.float32)
        s = 1.0 / np.sqrt(C)
        W_r = jax.random.uniform(ks[1], (C, C), jnp.float32, -s, s)
        W_k = jax.random.uniform(ks[2], (C, C), jnp.float32, -s, s)
        W_v = jax.random.uniform(ks[3], (C, C), jnp.float32, -s, s)
        mu_r = jax.random.uniform(ks[4], (C,), jnp.float32)
        mu_k = jax.random.uniform(ks[5], (C,), jnp.float32)
        return {'x': x, 'W_r': W_r, 'W_k': W_k, 'W_v': W_v, 'mu_r': mu_r, 'mu_k': mu_k}
    _L0_ffn_in = _L0_ffn_setup()
    _L0_c = _w((lambda *s: np.random.randn(*s).astype(np.float32) * 0.05)(16, 256))
    _L0_wmod = _w((lambda *s: np.random.randn(*s).astype(np.float32) * 0.05)(256, 6 * 256) * 256 ** (-0.5))

    def _L1_attn_setup():
        import jax, jax.numpy as jnp
        import numpy as np
        B, T, C = (4, 512, 256)
        N_HEADS = 16
        HEAD_DIM = C // N_HEADS

        def rotary_embedding(seq_len, dim, dtype=jnp.float32):
            pos = jnp.arange(seq_len, dtype=dtype)[:, None]
            i = jnp.arange(0, dim, 2, dtype=dtype)[None, :]
            theta = pos / jnp.power(10000.0, i / dim)
            return (jnp.cos(theta), jnp.sin(theta))

        def apply_rotary(x, cos, sin):
            d = x.shape[-1]
            x1, x2 = (x[..., :d // 2], x[..., d // 2:])
            rotated = jnp.concatenate([-x2, x1], axis=-1)
            cos = jnp.concatenate([cos, cos], axis=-1)[None, :, None, :]
            sin = jnp.concatenate([sin, sin], axis=-1)[None, :, None, :]
            return x * cos + rotated * sin
        key = jax.random.key(seed)
        k1, k2, k3 = jax.random.split(key, 3)
        x = jax.random.normal(k1, (B, T, C), dtype=jnp.float32)
        w_qkv = jax.random.normal(k2, (C, 3 * C), dtype=jnp.float32) / np.sqrt(C)
        w_out = jax.random.normal(k3, (C, C), dtype=jnp.float32) / np.sqrt(C)
        return {'x': x, 'w_qkv': w_qkv, 'w_out': w_out}
    _L1_attn_in = _L1_attn_setup()

    def _L1_ffn_setup():
        import jax, jax.numpy as jnp
        import numpy as np
        D_MODEL = 256
        N_HEAD = 16
        HEAD_DIM = D_MODEL // N_HEAD
        D_FF = 1024
        N_EXPERTS = 4
        EPS = 1e-05

        def _layer_norm(x, gamma, beta):
            mu = jnp.mean(x, axis=-1, keepdims=True)
            var = jnp.mean((x - mu) ** 2, axis=-1, keepdims=True)
            return (x - mu) / jnp.sqrt(var + EPS) * gamma + beta
        key = jax.random.key(seed)
        ks = jax.random.split(key, 20)
        f32 = jnp.float32
        sc = 1.0 / np.sqrt(D_MODEL)
        scf = 1.0 / np.sqrt(D_FF)
        return {'src': jax.random.normal(ks[0], (4, 128, D_MODEL), f32), 'Wq': jax.random.normal(ks[1], (D_MODEL, D_MODEL), f32) * sc, 'bq': jnp.zeros((D_MODEL,), f32), 'Wk': jax.random.normal(ks[2], (D_MODEL, D_MODEL), f32) * sc, 'bk': jnp.zeros((D_MODEL,), f32), 'Wv': jax.random.normal(ks[3], (D_MODEL, D_MODEL), f32) * sc, 'bv': jnp.zeros((D_MODEL,), f32), 'Wo': jax.random.normal(ks[4], (D_MODEL, D_MODEL), f32) * sc, 'bo': jnp.zeros((D_MODEL,), f32), 'router_w': jax.random.normal(ks[5], (D_MODEL, 1), f32) * 0.05, 'router_b': jnp.zeros((1,), f32), 'W1': jax.random.normal(ks[6], (N_EXPERTS, D_MODEL, D_FF), f32) * sc, 'b1': jnp.zeros((N_EXPERTS, D_FF), f32), 'W2': jax.random.normal(ks[7], (N_EXPERTS, D_FF, D_MODEL), f32) * scf, 'b2': jnp.zeros((N_EXPERTS, D_MODEL), f32), 'ln1_g': jnp.ones((D_MODEL,), f32), 'ln1_b': jnp.zeros((D_MODEL,), f32), 'ln2_g': jnp.ones((D_MODEL,), f32), 'ln2_b': jnp.zeros((D_MODEL,), f32)}
    _L1_ffn_in = _L1_ffn_setup()
    _L1_c = _w((lambda *s: np.random.randn(*s).astype(np.float32) * 0.05)(16, 256))
    _L1_wmod = _w((lambda *s: np.random.randn(*s).astype(np.float32) * 0.05)(256, 6 * 256) * 256 ** (-0.5))
    _d = {'L0_attn_x': _L0_attn_in['x'], 'L0_attn_W_ret': _L0_attn_in['W_ret'], 'L0_attn_b_ret': _L0_attn_in['b_ret'], 'L0_attn_ln1_scale': _L0_attn_in['ln1_scale'], 'L0_attn_ln1_bias': _L0_attn_in['ln1_bias'], 'L0_attn_W1': _L0_attn_in['W1'], 'L0_attn_b1': _L0_attn_in['b1'], 'L0_attn_W2': _L0_attn_in['W2'], 'L0_attn_b2': _L0_attn_in['b2'], 'L0_attn_ln2_scale': _L0_attn_in['ln2_scale'], 'L0_attn_ln2_bias': _L0_attn_in['ln2_bias'], 'L0_ffn_W_r': _L0_ffn_in['W_r'], 'L0_ffn_W_k': _L0_ffn_in['W_k'], 'L0_ffn_W_v': _L0_ffn_in['W_v'], 'L0_ffn_mu_r': _L0_ffn_in['mu_r'], 'L0_ffn_mu_k': _L0_ffn_in['mu_k'], 'L0_c': _L0_c, 'L0_wmod': _L0_wmod, 'L1_attn_w_qkv': _L1_attn_in['w_qkv'], 'L1_attn_w_out': _L1_attn_in['w_out'], 'L1_ffn_Wq': _L1_ffn_in['Wq'], 'L1_ffn_bq': _L1_ffn_in['bq'], 'L1_ffn_Wk': _L1_ffn_in['Wk'], 'L1_ffn_bk': _L1_ffn_in['bk'], 'L1_ffn_Wv': _L1_ffn_in['Wv'], 'L1_ffn_bv': _L1_ffn_in['bv'], 'L1_ffn_Wo': _L1_ffn_in['Wo'], 'L1_ffn_bo': _L1_ffn_in['bo'], 'L1_ffn_router_w': _L1_ffn_in['router_w'], 'L1_ffn_router_b': _L1_ffn_in['router_b'], 'L1_ffn_W1': _L1_ffn_in['W1'], 'L1_ffn_b1': _L1_ffn_in['b1'], 'L1_ffn_W2': _L1_ffn_in['W2'], 'L1_ffn_b2': _L1_ffn_in['b2'], 'L1_ffn_ln1_g': _L1_ffn_in['ln1_g'], 'L1_ffn_ln1_b': _L1_ffn_in['ln1_b'], 'L1_ffn_ln2_g': _L1_ffn_in['ln2_g'], 'L1_ffn_ln2_b': _L1_ffn_in['ln2_b'], 'L1_c': _L1_c, 'L1_wmod': _L1_wmod}
    _x0 = _d['L0_attn_x']
    _d['L0_attn_x'] = jax.random.normal(jax.random.fold_in(jax.random.key(seed), 1), (16, 512, 256), dtype=_x0.dtype)
    del _x0
    return _d

def reference(L0_attn_x, L0_attn_W_ret, L0_attn_b_ret, L0_attn_ln1_scale, L0_attn_ln1_bias, L0_attn_W1, L0_attn_b1, L0_attn_W2, L0_attn_b2, L0_attn_ln2_scale, L0_attn_ln2_bias, L0_ffn_W_r, L0_ffn_W_k, L0_ffn_W_v, L0_ffn_mu_r, L0_ffn_mu_k, L0_c, L0_wmod, L1_attn_w_qkv, L1_attn_w_out, L1_ffn_Wq, L1_ffn_bq, L1_ffn_Wk, L1_ffn_bk, L1_ffn_Wv, L1_ffn_bv, L1_ffn_Wo, L1_ffn_bo, L1_ffn_router_w, L1_ffn_router_b, L1_ffn_W1, L1_ffn_b1, L1_ffn_W2, L1_ffn_b2, L1_ffn_ln1_g, L1_ffn_ln1_b, L1_ffn_ln2_g, L1_ffn_ln2_b, L1_c, L1_wmod):

    def _L0_attn_ref(x, W_ret, b_ret, ln1_scale, ln1_bias, W1, b1, W2, b2, ln2_scale, ln2_bias):
        import jax, jax.numpy as jnp
        import numpy as np
        H = 256
        F = 1024
        B, S = (4, 1024)
        EPS = 1e-05

        def _layernorm(x, scale, bias):
            mu = jnp.mean(x, axis=-1, keepdims=True)
            var = jnp.var(x, axis=-1, keepdims=True)
            return (x - mu) * jax.lax.rsqrt(var + EPS) * scale + bias
        sig = jax.nn.sigmoid(jnp.einsum('bsh,hk->bsk', x, W_ret) + b_ret)

        def ema_step(carry, s_t):
            xi = 0.5 * s_t + 0.5 * carry
            return (xi, xi)
        _, ret = jax.lax.scan(ema_step, jnp.zeros((x.shape[0], x.shape[2]), x.dtype), jnp.transpose(sig, (1, 0, 2)))
        retention_output = jnp.transpose(ret, (1, 0, 2))
        h = _layernorm(x + retention_output, ln1_scale, ln1_bias)
        ffn = jnp.einsum('bsf,fh->bsh', jax.nn.gelu(jnp.einsum('bsh,hf->bsf', h, W1) + b1), W2) + b2
        out = _layernorm(h + ffn, ln2_scale, ln2_bias)
        return out

    def _L0_ffn_ref(x, W_r, W_k, W_v, mu_r, mu_k):
        import jax, jax.numpy as jnp
        import numpy as np
        DIM = 256

        def _reference_tuple_inner(x, W_r, W_k, W_v, mu_r, mu_k):
            B, T, C = x.shape
            x_prev = jnp.concatenate([jnp.zeros((B, 1, C), x.dtype), x[:, :-1, :]], axis=1)
            xr = mu_r * x + (1.0 - mu_r) * x_prev
            xk = mu_k * x + (1.0 - mu_k) * x_prev
            r = jax.nn.sigmoid(jnp.einsum('btc,dc->btd', xr, W_r))
            k = jnp.einsum('btc,dc->btd', xk, W_k)
            k_act = jnp.square(jax.nn.relu(k))
            out = r * jnp.einsum('btc,dc->btd', k_act, W_v)
            new_state = x[:, -1, :]
            return (out, new_state)
        return _reference_tuple_inner(x, W_r, W_k, W_v, mu_r, mu_k)[0]

    def _L1_attn_ref(x, w_qkv, w_out):
        import jax, jax.numpy as jnp
        import numpy as np
        B, T, C = (4, 512, 256)
        N_HEADS = 16
        HEAD_DIM = C // N_HEADS

        def rotary_embedding(seq_len, dim, dtype=jnp.float32):
            pos = jnp.arange(seq_len, dtype=dtype)[:, None]
            i = jnp.arange(0, dim, 2, dtype=dtype)[None, :]
            theta = pos / jnp.power(10000.0, i / dim)
            return (jnp.cos(theta), jnp.sin(theta))

        def apply_rotary(x, cos, sin):
            d = x.shape[-1]
            x1, x2 = (x[..., :d // 2], x[..., d // 2:])
            rotated = jnp.concatenate([-x2, x1], axis=-1)
            cos = jnp.concatenate([cos, cos], axis=-1)[None, :, None, :]
            sin = jnp.concatenate([sin, sin], axis=-1)[None, :, None, :]
            return x * cos + rotated * sin
        b, t, c = x.shape
        qkv = jnp.einsum('btc,cd->btd', x, w_qkv)
        q, k, v = jnp.split(qkv, 3, axis=-1)
        q = q.reshape(b, t, N_HEADS, HEAD_DIM)
        k = k.reshape(b, t, N_HEADS, HEAD_DIM)
        v = v.reshape(b, t, N_HEADS, HEAD_DIM)
        cos, sin = rotary_embedding(t, HEAD_DIM, dtype=x.dtype)
        q = apply_rotary(q, cos, sin)
        k = apply_rotary(k, cos, sin)
        scale = jnp.sqrt(jnp.asarray(HEAD_DIM, dtype=x.dtype))
        attn = jnp.einsum('bqhd,bkhd->bhqk', q, k) / scale
        mask = jnp.tril(jnp.ones((t, t), dtype=jnp.bool_))
        attn = jnp.where(mask[None, None, :, :], attn, jnp.asarray(-1000000000.0, dtype=x.dtype))
        attn = jax.nn.softmax(attn, axis=-1)
        out = jnp.einsum('bhqk,bkhd->bqhd', attn, v).reshape(b, t, c)
        return jnp.einsum('btc,cd->btd', out, w_out)

    def _L1_ffn_ref(src, Wq, bq, Wk, bk, Wv, bv, Wo, bo, router_w, router_b, W1, b1, W2, b2, ln1_g, ln1_b, ln2_g, ln2_b):
        import jax, jax.numpy as jnp
        import numpy as np
        D_MODEL = 256
        N_HEAD = 16
        HEAD_DIM = D_MODEL // N_HEAD
        D_FF = 1024
        N_EXPERTS = 4
        EPS = 1e-05

        def _layer_norm(x, gamma, beta):
            mu = jnp.mean(x, axis=-1, keepdims=True)
            var = jnp.mean((x - mu) ** 2, axis=-1, keepdims=True)
            return (x - mu) / jnp.sqrt(var + EPS) * gamma + beta
        B, T, _ = src.shape
        q = (src @ Wq + bq).reshape(B, T, N_HEAD, HEAD_DIM)
        k = (src @ Wk + bk).reshape(B, T, N_HEAD, HEAD_DIM)
        v = (src @ Wv + bv).reshape(B, T, N_HEAD, HEAD_DIM)
        scale = HEAD_DIM ** (-0.5)
        scores = jnp.einsum('bqhd,bkhd->bhqk', q, k) * scale
        probs = jax.nn.softmax(scores, axis=-1)
        attn = jnp.einsum('bhqk,bkhd->bqhd', probs, v).reshape(B, T, D_MODEL)
        attn = attn @ Wo + bo
        x = _layer_norm(src + attn, ln1_g, ln1_b)
        keys = (x @ router_w + router_b)[..., 0]
        expert_idx = jnp.remainder(jnp.floor(keys).astype(jnp.int32), N_EXPERTS)
        ff_out = jnp.zeros_like(x)
        for e in range(N_EXPERTS):
            h = jax.nn.relu(x @ W1[e] + b1[e])
            y = h @ W2[e] + b2[e]
            ff_out = ff_out + jnp.where((expert_idx == e)[..., None], y, 0.0)
        return _layer_norm(x + ff_out, ln2_g, ln2_b)
    x = L0_attn_x
    mod = (_silu(L0_c) @ L0_wmod).reshape(L0_c.shape[0], 6, 1, -1)
    sa, ca, ga, sb, cb, gb = (mod[:, 0], mod[:, 1], mod[:, 2], mod[:, 3], mod[:, 4], mod[:, 5])
    ga = (2 * (ga >= 0) - 1) * jnp.maximum(jnp.abs(ga), 0.25)
    gb = (2 * (gb >= 0) - 1) * jnp.maximum(jnp.abs(gb), 0.25)
    h = _layernorm(x, axis=-1) * (1 + ca) + sa
    x = x + ga * _L0_attn_ref(h, L0_attn_W_ret, L0_attn_b_ret, L0_attn_ln1_scale, L0_attn_ln1_bias, L0_attn_W1, L0_attn_b1, L0_attn_W2, L0_attn_b2, L0_attn_ln2_scale, L0_attn_ln2_bias)
    h = _layernorm(x, axis=-1) * (1 + cb) + sb
    x = x + gb * _L0_ffn_ref(h, L0_ffn_W_r, L0_ffn_W_k, L0_ffn_W_v, L0_ffn_mu_r, L0_ffn_mu_k)
    mod = (_silu(L1_c) @ L1_wmod).reshape(L1_c.shape[0], 6, 1, -1)
    sa, ca, ga, sb, cb, gb = (mod[:, 0], mod[:, 1], mod[:, 2], mod[:, 3], mod[:, 4], mod[:, 5])
    ga = (2 * (ga >= 0) - 1) * jnp.maximum(jnp.abs(ga), 0.25)
    gb = (2 * (gb >= 0) - 1) * jnp.maximum(jnp.abs(gb), 0.25)
    h = _layernorm(x, axis=-1) * (1 + ca) + sa
    x = x + ga * _L1_attn_ref(h, L1_attn_w_qkv, L1_attn_w_out)
    h = _layernorm(x, axis=-1) * (1 + cb) + sb
    x = x + gb * _L1_ffn_ref(h, L1_ffn_Wq, L1_ffn_bq, L1_ffn_Wk, L1_ffn_bk, L1_ffn_Wv, L1_ffn_bv, L1_ffn_Wo, L1_ffn_bo, L1_ffn_router_w, L1_ffn_router_b, L1_ffn_W1, L1_ffn_b1, L1_ffn_W2, L1_ffn_b2, L1_ffn_ln1_g, L1_ffn_ln1_b, L1_ffn_ln2_g, L1_ffn_ln2_b)
    return x

_drawn_inputs = setup_inputs


def setup_inputs(seed=0):
    import zlib

    import numpy as np

    out = dict(_drawn_inputs(seed))
    spreads = {'L0_attn_b_ret': (0.0, 0.455),
     'L0_attn_ln1_scale': (1.0, 0.2),
     'L0_attn_ln1_bias': (0.0, 0.1),
     'L0_attn_b1': (0.0, 0.415),
     'L0_attn_b2': (0.0, 0.1),
     'L0_attn_ln2_scale': (1.0, 0.2),
     'L0_attn_ln2_bias': (0.0, 0.1),
     'L1_ffn_bq': (0.0, 0.419),
     'L1_ffn_bk': (0.0, 0.8),
     'L1_ffn_bv': (0.0, 0.284),
     'L1_ffn_bo': (0.0, 0.1),
     'L1_ffn_b1': (0.0, 0.58),
     'L1_ffn_b2': (0.0, 0.401),
     'L1_ffn_ln1_g': (1.0, 0.2),
     'L1_ffn_ln1_b': (0.0, 0.1),
     'L1_ffn_ln2_g': (1.0, 0.2),
     'L1_ffn_ln2_b': (0.0, 0.327)}
    factors = {'L0_attn_W_ret': 3.066, 'L0_ffn_W_r': 5.473, 'L0_ffn_mu_r': 8.0, 'L0_ffn_mu_k': 3.067}
    for name, (base, spread) in spreads.items():
        noise = np.random.default_rng([zlib.crc32(name.encode()), seed]).standard_normal(out[name].shape)
        drawn = base * np.exp(spread * noise) if base else spread * noise
        out[name] = jnp.asarray(drawn.astype(out[name].dtype))
    for name, factor in factors.items():
        out[name] = (out[name] * factor).astype(out[name].dtype)
    return out
```

```python
import concourse.bass as bass
from concourse import mybir
from concourse.alu_op_type import AluOpType as ALU
from contextlib import ExitStack

F32 = mybir.dt.float32
BF16 = mybir.dt.bfloat16
ACT = mybir.ActivationFunctionType
AX = mybir.AxisListType

P = 128
C = 256
CB = C // P
T = 512
J = T // P
FF = 1024
FB = FF // P
NE = 4
NH = 16
HD = C // NH
EPS = 1e-5
KS = 3 * 2 * HD
G4 = 4

COLS = {}
for _name, _n in (("b_ret", 2), ("ln1_scale", 2), ("ln1_bias", 2), ("b1", 8), ("mu_r", 2), ("mu_k", 2),
                  ("bq", 2), ("bk", 2), ("l1_ln1_g", 2), ("l1_ln1_b", 2), ("router_b", 1)):
    COLS[_name] = sum(n for _, n in COLS.values()) if COLS else 0
    COLS[_name] = (COLS[_name], _n)
NCOLS = sum(n for _, n in COLS.values())
ROWS = ("ln1_scale", "ln1_bias", "b2", "ln2_scale", "ln2_bias",
        "bv", "bo", "l1_ln1_g", "l1_ln1_b", "router_w", "l1_ln2_g", "l1_ln2_b")
SA, CA, GA, SB, CBM, GB = range(6)
MROWS = ((0, GA), (0, GB), (1, GA), (1, GB), (1, CBM), (1, SB))


class Core:
    pass


def col(k, name, i=0):
    first, _ = COLS[name]
    return k.cols[:, first + i:first + i + 1]


def over_tiles(ap):
    return ap.unsqueeze(1).to_broadcast([P, J, C])


def setup_phase(nc, k, d):
    with ExitStack() as ctx:
        sb = lambda n, s, t=F32: ctx.enter_context(nc.sbuf_tensor("set_" + n, s, t))
        sem = lambda n: nc.alloc_semaphore("set_" + n)
        B = k.B
        wmod = [sb(f"wmod{l}", [P, CB, 6 * C]) for l in range(2)]
        cT = sb("cT", [P, 2, CB, B])
        sg = sb("sg", [P, 2, CB, B])
        rowmod = sb("rowmod", [B, len(MROWS), C])
        mask = sb("mask", [P, P])
        t_sign = sb("t_sign", [B, C])
        t_abs = sb("t_abs", [B, C])
        colps = [ctx.enter_context(nc.psum_tensor(f"colps{l}", [P, 12, B], F32)) for l in range(2)]
        rowps = [ctx.enter_context(nc.psum_tensor(f"rowps{i}", [B, C], F32)) for i in range(len(MROWS))]
        loaded, c_loaded, sig_done, silu_done = sem("loaded"), sem("c_loaded"), sem("sig_done"), sem("silu_done")
        colmod_ready, rowmod_ready = sem("colmod_ready"), sem("rowmod_ready")
        cols_done, step, rows_done, stored = sem("cols_done"), sem("step"), sem("rows_done"), sem("stored")
        block = ctx.enter_context(nc.Block())

        @block.sync
        def _(sp):
            for l in range(2):
                sp.dma_start(cT[:, l], d[f"cT{l}"].rearrange("(k p) b -> p k b", p=P)).then_inc(c_loaded, 16)
            for l in range(2):
                sp.dma_start(wmod[l][:], d[f"wmod{l}"].rearrange("(k p) n -> p k n", p=P)).then_inc(loaded, 16)
            sp.dma_start(k.cols[:], d["cols"]).then_inc(loaded, 16)
            sp.dma_start(k.ident[:], d["ident"]).then_inc(loaded, 16)
            sp.dma_start(mask[:], d["mask"]).then_inc(loaded, 16)
            sp.wait_ge(rows_done, 1)
            sp.dma_start(k.mrows_dram.rearrange("r b c -> b r c"), rowmod[:]).then_inc(stored, 16)
            sp.wait_ge(stored, 16)
            sp.wait_ge(loaded, 80)

        @block.scalar
        def _(act):
            act.wait_ge(c_loaded, 32)
            nc.scalar.activation(sg[:], cT[:], ACT.Sigmoid).then_inc(sig_done, 1)

        @block.tensor
        def _(pe):
            pe.wait_ge(loaded, 80)
            pe.wait_ge(silu_done, 1)
            for l in range(2):
                for m in range(12):
                    for kb in range(CB):
                        last = nc.tensor.matmul(colps[l][:, m, :], wmod[l][:, kb, m * P:(m + 1) * P], sg[:, l, kb, :],
                                                start=(kb == 0), stop=(kb == CB - 1))
            last.then_inc(colmod_ready, 1)
            for i, (l, part) in enumerate(MROWS):
                for kb in range(CB):
                    last = nc.tensor.matmul(rowps[i][:], sg[:, l, kb, :], wmod[l][:, kb, part * C:(part + 1) * C],
                                            start=(kb == 0), stop=(kb == CB - 1))
            last.then_inc(rowmod_ready, 1)

        @block.vector
        def _(dve):
            dve.wait_ge(loaded, 80)
            dve.wait_ge(sig_done, 1)
            nc.vector.tensor_tensor(sg[:], sg[:], cT[:], ALU.mult).then_inc(silu_done, 1)
            dve.wait_ge(colmod_ready, 1)
            for l in range(2):
                for m in range(12):
                    plus = 1.0 if m // 2 in (CA, CBM) else 0.0
                    nc.vector.tensor_scalar(k.mod[:, l, m, :], colps[l][:, m, :], plus, None, ALU.add)
            nc.vector.tensor_copy(k.ident_bf[:], k.ident[:])
            nc.vector.tensor_copy(k.mask_bf[:], mask[:])
            nc.vector.memset(k.half[:], 0.5).then_inc(cols_done, 1)
            dve.wait_ge(rowmod_ready, 1)
            steps = [0]

            def follow(instruction):
                steps[0] += 1
                instruction.then_inc(step, 1)
                dve.wait_ge(step, steps[0])

            for i, (l, part) in enumerate(MROWS):
                if part in (GA, GB):
                    follow(nc.vector.tensor_scalar(t_sign[:], rowps[i][:], 0.0, 2.0, ALU.is_ge, ALU.mult))
                    follow(nc.vector.tensor_scalar(t_sign[:], t_sign[:], -1.0, None, ALU.add))
                    follow(nc.vector.tensor_tensor(t_abs[:], t_sign[:], rowps[i][:], ALU.mult))
                    follow(nc.vector.scalar_tensor_tensor(rowmod[:, i, :], t_abs[:], 0.25, t_sign[:],
                                                          ALU.max, ALU.mult))
                else:
                    nc.vector.tensor_scalar(rowmod[:, i, :], rowps[i][:], 1.0 if part == CBM else 0.0, None, ALU.add)
            nc.vector.tensor_copy(t_sign[:], t_abs[:]).then_inc(rows_done, 1)


class Norm:

    def __init__(self, nc, ctx, name):
        self.stats = ctx.enter_context(nc.sbuf_tensor(f"{name}_stats", [P, J, 6], F32))
        self.mv = ctx.enter_context(nc.sbuf_tensor(f"{name}_mv", [P, J, 2], F32))
        self.pause = ctx.enter_context(nc.sbuf_tensor(f"{name}_pause", [P, 1], F32))
        self.ve = ctx.enter_context(nc.sbuf_tensor(f"{name}_ve", [P, J], F32))
        self.rstd = ctx.enter_context(nc.sbuf_tensor(f"{name}_rstd", [P, J], F32))
        self.stats_ready = nc.alloc_semaphore(f"{name}_stats_ready")
        self.mv_ready = nc.alloc_semaphore(f"{name}_mv_ready")
        self.ve_ready = nc.alloc_semaphore(f"{name}_ve_ready")
        self.rstd_ready = nc.alloc_semaphore(f"{name}_rstd_ready")

    def moments(self, nc, dve, tile, b):
        for j in range(J):
            last = nc.vector.bn_stats(self.stats[:, j, :], tile(j))
        last.then_inc(self.stats_ready, 1)
        dve.wait_ge(self.stats_ready, b + 1)
        nc.vector.memset(self.pause[:], 0.0)
        for j in range(J):
            last = nc.vector.bn_aggr(self.mv[:, j, :], self.stats[:, j, :])
        last.then_inc(self.mv_ready, 1)

    def rsqrt(self, nc, k, pool, b):
        pool.wait_ge(self.mv_ready, b + 1)
        nc.gpsimd.tensor_tensor(self.ve[:], self.mv[:, :, 1], k.eps[:], ALU.add).then_inc(self.ve_ready, 1)
        pool.wait_ge(self.ve_ready, b + 1)
        nc.gpsimd.tensor_tensor(self.rstd[:], self.ve[:], k.minus_half[:], ALU.pow).then_inc(self.rstd_ready, 1)

    def apply(self, nc, dve, out, tile, b):
        dve.wait_ge(self.rstd_ready, b + 1)
        for j in range(J):
            last = nc.vector.tensor_scalar(out[:, j, :], tile(j), self.mv[:, j, 0:1], self.rstd[:, j:j + 1],
                                           ALU.subtract, ALU.mult)
        return last


def to_channels(nc, k, out, z):
    for cb in range(CB):
        for j in range(J):
            last = nc.tensor.transpose(out[:, cb, j * P:(j + 1) * P], z[:, j, cb * P:(cb + 1) * P], k.ident[:])
    return last


def retention_phase(nc, k, d):
    with ExitStack() as ctx:
        sb = lambda n, s, t=F32: ctx.enter_context(nc.sbuf_tensor("ret_" + n, s, t))
        sem = lambda n: nc.alloc_semaphore("ret_" + n)
        B = k.B
        w_ret = sb("w_ret", [P, CB, C])
        w1 = sb("w1", [P, CB, FF])
        w2 = sb("w2", [P, FB, C])
        rowb = {n: sb(f"rowb_{n}", [P, C]) for n in ("ln1_scale", "ln1_bias", "b2", "ln2_scale", "ln2_bias")}
        hbias = sb("hbias", [P, C])
        gate = sb("gate", [P, C])
        gate_scale = sb("gate_scale", [P, C])
        gate_bias = sb("gate_bias", [P, C])
        half_b_ret = sb("half_b_ret", [P, CB])
        z0 = sb("z0", [P, J, C])
        hT = sb("hT", [P, CB, T])
        sT = sb("sT", [P, CB, T])
        tT = sb("tT", [P, CB, T])
        z1 = sb("z1", [P, J, C])
        h1T = sb("h1T", [P, CB, T])
        h1b = sb("h1b", [P, J, C])
        gT = sb("gT", [P, FB, T])
        t2 = sb("t2", [P, J, C])
        ln0, ln1, ln2 = (Norm(nc, ctx, "ret_" + n) for n in ("ln0", "ln1", "ln2"))
        ps = lambda n, s: ctx.enter_context(nc.psum_tensor("ret_" + n, s, F32))
        psA = ps("psA", [P, 2, T])
        psB = ps("psB", [P, 2, T])
        psF = ps("psF", [P, 2, T])
        psY = ps("psY", [P, J, C])
        weights, rows, x_loaded, gate_loaded = sem("weights"), sem("rows"), sem("x_loaded"), sem("gate_loaded")
        init, hbias_done = sem("init"), sem("hbias_done")
        z0_done, zT_done, hT_done, pre_done = sem("z0_done"), sem("zT_done"), sem("hT_done"), sem("pre_done")
        tanh_done, s_done, scan_done, tT_done = sem("tanh_done"), sem("s_done"), sem("scan_done"), sem("tT_done")
        tok_done, z1_done, z1T_done, h1T_done = sem("tok_done"), sem("z1_done"), sem("z1T_done"), sem("h1T_done")
        h1g_done, h1b_done, ffn1_done, gelu_done = sem("h1g_done"), sem("h1b_done"), sem("ffn1_done"), sem("gelu_done")
        y_done, t2_done, z2_done, gate_done = sem("y_done"), sem("t2_done"), sem("z2_done"), sem("gate_done")
        zg_done, out_done, x_done = sem("zg_done"), sem("out_done"), sem("x_done")
        block = ctx.enter_context(nc.Block())

        @block.sync
        def _(sp):
            for ap, src in ((w_ret, "W_ret"), (w1, "W1"), (w2, "W2")):
                sp.dma_start(ap[:], d[src].rearrange("(k p) n -> p k n", p=P)).then_inc(weights, 16)
            for n, ap in rowb.items():
                sp.dma_start(ap[:], d["rows"][ROWS.index(n)].partition_broadcast(P)).then_inc(rows, 16)
            with sp.Fori(0, B) as b:
                sp.wait_ge(x_loaded, 16 * b)
                sp.dma_start(k.x[:, bass.ds(b * J, J), :],
                             d["x"][bass.ds(b * J, J)].rearrange("j p c -> p j c")).then_inc(x_loaded, 16)
                sp.wait_ge(gate_done, b)
                sp.dma_start(gate[:], k.mrows_dram[0, b].partition_broadcast(P)).then_inc(gate_loaded, 16)

        @block.vector
        def _(dve):
            def norm0(b):
                dve.wait_ge(x_loaded, 16 * b + 16)
                tile = lambda j: k.x[:, b * J + j, :]
                ln0.moments(nc, dve, tile, b)
                dve.wait_ge(zT_done, b)
                ln0.apply(nc, dve, z0, tile, b).then_inc(z0_done, 1)

            def retention(b):
                dve.wait_ge(s_done, b + 1)
                dve.wait_ge(tok_done, b)
                for cb in range(CB):
                    last = nc.vector.tensor_tensor_scan(tT[:, cb, :], k.half[:], sT[:, cb, :], 0.0, ALU.mult, ALU.add)
                last.then_inc(scan_done, 1)
                dve.wait_ge(scan_done, b + 1)
                nc.vector.scalar_tensor_tensor(tT[:], tT[:], 0.5, hT[:], ALU.mult, ALU.add).then_inc(tT_done, 1)

            def norm1(b):
                dve.wait_ge(tok_done, b + 1)
                tile = lambda j: psA[:, j // 2, (j % 2) * C:(j % 2 + 1) * C]
                ln1.moments(nc, dve, tile, b)
                dve.wait_ge(z1T_done, b)
                dve.wait_ge(h1b_done, b)
                ln1.apply(nc, dve, z1, tile, b).then_inc(z1_done, 1)

            def norm2(b):
                dve.wait_ge(y_done, J * b + J)
                dve.wait_ge(h1b_done, b + 1)
                dve.wait_ge(x_done, b)
                nc.vector.tensor_tensor(t2[:], psY[:], h1b[:], ALU.add).then_inc(t2_done, 1)
                dve.wait_ge(t2_done, b + 1)
                tile = lambda j: t2[:, j, :]
                ln2.moments(nc, dve, tile, b)
                ln2.apply(nc, dve, t2, tile, b).then_inc(z2_done, 1)

            def residual(b):
                dve.wait_ge(out_done, b + 1)
                xb = k.x[:, bass.ds(b * J, J), :]
                nc.vector.tensor_tensor(xb, xb, t2[:], ALU.add).then_inc(x_done, 1)

            dve.wait_ge(rows, 16 * len(rowb))
            nc.vector.tensor_scalar(half_b_ret[:], k.cols[:, COLS["b_ret"][0]:COLS["b_ret"][0] + CB], 0.5, None,
                                    ALU.mult)
            nc.vector.tensor_tensor(hbias[:], rowb["ln1_bias"][:], rowb["b2"][:], ALU.add).then_inc(init, 1)
            norm0(0)
            retention(0)
            norm1(0)
            if True:
                with dve.Fori(0, B - 1) as b:
                    norm0(b + 1)
                    retention(b + 1)
                    norm1(b + 1)
                    norm2(b)
                    residual(b)
            norm2(B - 1)
            residual(B - 1)

        @block.gpsimd
        def _(pool):
            def add_bias(b):
                pool.wait_ge(z1_done, b + 1)
                pool.wait_ge(t2_done, b)
                nc.gpsimd.tensor_tensor(h1b[:], z1[:], over_tiles(rowb["ln1_scale"][:]), ALU.mult).then_inc(h1g_done, 1)
                pool.wait_ge(h1g_done, b + 1)
                nc.gpsimd.tensor_tensor(h1b[:], h1b[:], over_tiles(hbias[:]), ALU.add).then_inc(h1b_done, 1)

            def gates(b):
                pool.wait_ge(gate_loaded, 16 * b + 16)
                pool.wait_ge(out_done, b)
                nc.gpsimd.tensor_tensor(gate_scale[:], gate[:], rowb["ln2_scale"][:], ALU.mult)
                nc.gpsimd.tensor_tensor(gate_bias[:], gate[:], rowb["ln2_bias"][:], ALU.mult).then_inc(gate_done, 1)

            def scale_out(b):
                pool.wait_ge(z2_done, b + 1)
                pool.wait_ge(gate_done, b + 1)
                nc.gpsimd.tensor_tensor(t2[:], t2[:], over_tiles(gate_scale[:]), ALU.mult).then_inc(zg_done, 1)
                pool.wait_ge(zg_done, b + 1)
                nc.gpsimd.tensor_tensor(t2[:], t2[:], over_tiles(gate_bias[:]), ALU.add).then_inc(out_done, 1)

            pool.wait_ge(init, 1)
            ln0.rsqrt(nc, k, pool, 0)
            ln1.rsqrt(nc, k, pool, 0)
            add_bias(0)
            if True:
                with pool.Fori(0, B - 1) as b:
                    gates(b)
                    ln0.rsqrt(nc, k, pool, b + 1)
                    ln1.rsqrt(nc, k, pool, b + 1)
                    ln2.rsqrt(nc, k, pool, b)
                    scale_out(b)
                    add_bias(b + 1)
            gates(B - 1)
            ln2.rsqrt(nc, k, pool, B - 1)
            scale_out(B - 1)

        @block.tensor
        def _(pe):
            def transpose_h(b):
                pe.wait_ge(z0_done, b + 1)
                pe.wait_ge(z1_done, b)
                to_channels(nc, k, psA, z0).then_inc(zT_done, 1)

            def retention_product(b):
                pe.wait_ge(hT_done, b + 1)
                pe.wait_ge(h1T_done, b)
                for db in range(CB):
                    for cb in range(CB):
                        last = nc.tensor.matmul(psB[:, db, :], w_ret[:, cb, db * P:(db + 1) * P], hT[:, cb, :],
                                                start=(cb == 0), stop=(cb == CB - 1))
                last.then_inc(pre_done, 1)

            def transpose_back(b):
                pe.wait_ge(tT_done, b + 1)
                for j in range(J):
                    for cb in range(CB):
                        last = nc.tensor.transpose(psA[:, j // 2, (j % 2) * C + cb * P:(j % 2) * C + (cb + 1) * P],
                                                   tT[:, cb, j * P:(j + 1) * P], k.ident[:])
                last.then_inc(tok_done, 1)

            def transpose_h1(b):
                pe.wait_ge(z1_done, b + 1)
                pe.wait_ge(tanh_done, b + 1)
                to_channels(nc, k, psB, z1).then_inc(z1T_done, 1)

            def hidden(b, blocks):
                for f in blocks:
                    if f == 0:
                        pe.wait_ge(h1T_done, b + 1)
                    pe.wait_ge(gelu_done, FB * b + max(f - 1, 0))
                    for cb in range(CB):
                        last = nc.tensor.matmul(psF[:, f % 2, :], w1[:, cb, f * P:(f + 1) * P], h1T[:, cb, :],
                                                start=(cb == 0), stop=(cb == CB - 1))
                    last.then_inc(ffn1_done, 1)

            def output(b, tiles):
                for j in tiles:
                    if j == 0:
                        pe.wait_ge(gelu_done, FB * b + FB)
                        pe.wait_ge(t2_done, b)
                    for f in range(FB):
                        last = nc.tensor.matmul(psY[:, j, :], gT[:, f, j * P:(j + 1) * P], w2[:, f, :],
                                                start=(f == 0), stop=(f == FB - 1))
                    last.then_inc(y_done, 1)

            pe.wait_ge(weights, 48)
            transpose_h(0)
            retention_product(0)
            transpose_back(0)
            transpose_h1(0)
            if True:
                with pe.Fori(0, B - 1) as b:
                    hidden(b, range(0, 5))
                    transpose_h(b + 1)
                    hidden(b, range(5, 6))
                    retention_product(b + 1)
                    hidden(b, range(6, 8))
                    output(b, range(0, 1))
                    transpose_back(b + 1)
                    output(b, range(1, 3))
                    transpose_h1(b + 1)
                    output(b, range(3, 4))
            hidden(B - 1, range(FB))
            output(B - 1, range(J))

        @block.scalar
        def _(act):
            def modulate(b):
                act.wait_ge(zT_done, b + 1)
                act.wait_ge(tT_done, b)
                for cb in range(CB):
                    last = nc.scalar.activation(hT[:, cb, :], psA[:, cb, :], ACT.Identity,
                                                scale=k.mod[:, 0, CA * CB + cb, bass.ds(b, 1)],
                                                bias=k.mod[:, 0, SA * CB + cb, bass.ds(b, 1)])
                last.then_inc(hT_done, 1)

            def sigmoid(b):
                act.wait_ge(pre_done, b + 1)
                for cb in range(CB):
                    last = nc.scalar.activation(sT[:, cb, :], psB[:, cb, :], ACT.Tanh, scale=0.5,
                                                bias=half_b_ret[:, cb:cb + 1])
                last.then_inc(tanh_done, 1)
                act.wait_ge(tanh_done, b + 1)
                nc.scalar.activation(sT[:], sT[:], ACT.Copy, scale=0.5, bias=0.5).then_inc(s_done, 1)

            def scale_h1(b):
                act.wait_ge(z1T_done, b + 1)
                act.wait_ge(ffn1_done, FB * b)
                for cb in range(CB):
                    last = nc.scalar.activation(h1T[:, cb, :], psB[:, cb, :], ACT.Identity,
                                                scale=col(k, "ln1_scale", cb), bias=col(k, "ln1_bias", cb))
                last.then_inc(h1T_done, 1)

            def gelu(b, blocks):
                for f in blocks:
                    if f == 0:
                        act.wait_ge(y_done, J * b)
                    act.wait_ge(ffn1_done, FB * b + f + 1)
                    nc.scalar.activation(gT[:, f, :], psF[:, f % 2, :], ACT.Gelu_apprx_tanh,
                                         bias=col(k, "b1", f)).then_inc(gelu_done, 1)

            act.wait_ge(init, 1)
            modulate(0)
            sigmoid(0)
            scale_h1(0)
            if True:
                with act.Fori(0, B - 1) as b:
                    gelu(b, range(0, 5))
                    modulate(b + 1)
                    gelu(b, range(5, 6))
                    sigmoid(b + 1)
                    gelu(b, range(6, 8))
                    scale_h1(b + 1)
            gelu(B - 1, range(FB))


def channel_mix_phase(nc, k, d):
    with ExitStack() as ctx:
        sb = lambda n, s, t=F32: ctx.enter_context(nc.sbuf_tensor("mix_" + n, s, t))
        sem = lambda n: nc.alloc_semaphore("mix_" + n)
        ps = lambda n, s: ctx.enter_context(nc.psum_tensor("mix_" + n, s, F32))
        B = k.B
        wr, wk, wv = sb("wr", [P, CB, C]), sb("wk", [P, CB, C]), sb("wv", [P, CB, C])
        gate = sb("gate", [P, C])
        z = sb("z", [P, J, C])
        hT = sb("hT", [P, CB, 1 + T])
        dT = sb("dT", [P, CB, T])
        xkT, xrT = sb("xkT", [P, CB, T]), sb("xrT", [P, CB, T])
        kT = sb("kT", [P, CB, T])
        r = sb("r", [P, J, C])
        o = sb("o", [P, J, C])
        ln = Norm(nc, ctx, "mix_ln")
        psA, psK = ps("psA", [P, CB, T]), ps("psK", [P, CB, T])
        psR, psV = ps("psR", [P, J, C]), ps("psV", [P, J, C])
        weights, gate_loaded, zero_done = sem("weights"), sem("gate_loaded"), sem("zero_done")
        z_done, zT_done, hT_done, d_done = sem("z_done"), sem("zT_done"), sem("hT_done"), sem("d_done")
        xk_done, xr_done, k_done, relu_done = sem("xk_done"), sem("xr_done"), sem("k_done"), sem("relu_done")
        sq_done, r_done, sig_done, rg_done = sem("sq_done"), sem("r_done"), sem("sig_done"), sem("rg_done")
        v_done, o_done, x_done = sem("v_done"), sem("o_done"), sem("x_done")
        block = ctx.enter_context(nc.Block())

        @block.sync
        def _(sp):
            for ap, src in ((wr, "W_rT"), (wk, "W_kT"), (wv, "W_vT")):
                sp.dma_start(ap[:], d[src].rearrange("(k p) n -> p k n", p=P)).then_inc(weights, 16)
            with sp.Fori(0, B) as b:
                sp.wait_ge(rg_done, b)
                sp.dma_start(gate[:], k.mrows_dram[1, b].partition_broadcast(P)).then_inc(gate_loaded, 16)

        @block.vector
        def _(dve):
            def norm(b):
                tile = lambda j: k.x[:, b * J + j, :]
                ln.moments(nc, dve, tile, b)
                dve.wait_ge(zT_done, b)
                ln.apply(nc, dve, z, tile, b).then_inc(z_done, 1)

            def mix(b):
                dve.wait_ge(hT_done, b + 1)
                now, before = hT[:, :, 1:1 + T], hT[:, :, 0:T]
                nc.vector.tensor_tensor(dT[:], now, before, ALU.subtract).then_inc(d_done, 1)
                dve.wait_ge(d_done, b + 1)
                dve.wait_ge(k_done, b)
                for cb in range(CB):
                    last = nc.vector.scalar_tensor_tensor(xkT[:, cb, :], dT[:, cb, :], col(k, "mu_k", cb),
                                                          hT[:, cb, 0:T], ALU.mult, ALU.add)
                last.then_inc(xk_done, 1)
                dve.wait_ge(r_done, b)
                for cb in range(CB):
                    last = nc.vector.scalar_tensor_tensor(xrT[:, cb, :], dT[:, cb, :], col(k, "mu_r", cb),
                                                          hT[:, cb, 0:T], ALU.mult, ALU.add)
                last.then_inc(xr_done, 1)

            def output(b):
                dve.wait_ge(v_done, b + 1)
                dve.wait_ge(rg_done, b + 1)
                dve.wait_ge(x_done, b)
                nc.vector.tensor_tensor(o[:], psV[:], r[:], ALU.mult).then_inc(o_done, 1)
                dve.wait_ge(o_done, b + 1)
                xb = k.x[:, bass.ds(b * J, J), :]
                nc.vector.tensor_tensor(xb, xb, o[:], ALU.add).then_inc(x_done, 1)

            nc.vector.memset(hT[:, :, 0:1], 0.0).then_inc(zero_done, 1)
            dve.wait_ge(zero_done, 1)
            norm(0)
            mix(0)
            if True:
                with dve.Fori(0, B - 1) as b:
                    norm(b + 1)
                    mix(b + 1)
                    output(b)
            output(B - 1)

        @block.gpsimd
        def _(pool):
            def gate_r(b):
                pool.wait_ge(sig_done, b + 1)
                pool.wait_ge(gate_loaded, 16 * b + 16)
                nc.gpsimd.tensor_tensor(r[:], r[:], over_tiles(gate[:]), ALU.mult).then_inc(rg_done, 1)

            ln.rsqrt(nc, k, pool, 0)
            if True:
                with pool.Fori(0, B - 1) as b:
                    ln.rsqrt(nc, k, pool, b + 1)
                    gate_r(b)
            gate_r(B - 1)

        @block.tensor
        def _(pe):
            def transpose_h(b):
                pe.wait_ge(z_done, b + 1)
                pe.wait_ge(hT_done, b)
                to_channels(nc, k, psA, z).then_inc(zT_done, 1)

            def key(b):
                pe.wait_ge(xk_done, b + 1)
                pe.wait_ge(relu_done, b)
                for db in range(CB):
                    for cb in range(CB):
                        last = nc.tensor.matmul(psK[:, db, :], wk[:, cb, db * P:(db + 1) * P], xkT[:, cb, :],
                                                start=(cb == 0), stop=(cb == CB - 1))
                last.then_inc(k_done, 1)

            def by_tokens(out, xT, w):
                for j in range(J):
                    for cb in range(CB):
                        last = nc.tensor.matmul(out[:, j, :], xT[:, cb, j * P:(j + 1) * P], w[:, cb, :],
                                                start=(cb == 0), stop=(cb == CB - 1))
                return last

            def receptance(b):
                pe.wait_ge(xr_done, b + 1)
                pe.wait_ge(sig_done, b)
                by_tokens(psR, xrT, wr).then_inc(r_done, 1)

            def value(b):
                pe.wait_ge(sq_done, b + 1)
                pe.wait_ge(o_done, b)
                by_tokens(psV, kT, wv).then_inc(v_done, 1)

            pe.wait_ge(weights, 48)
            transpose_h(0)
            if True:
                with pe.Fori(0, B - 1) as b:
                    key(b)
                    transpose_h(b + 1)
                    receptance(b)
                    value(b)
            key(B - 1)
            receptance(B - 1)
            value(B - 1)

        @block.scalar
        def _(act):
            def modulate(b):
                act.wait_ge(zT_done, b + 1)
                act.wait_ge(xr_done, b)
                for cb in range(CB):
                    last = nc.scalar.activation(hT[:, cb, 1:1 + T], psA[:, cb, :], ACT.Identity,
                                                scale=k.mod[:, 0, CBM * CB + cb, bass.ds(b, 1)],
                                                bias=k.mod[:, 0, SB * CB + cb, bass.ds(b, 1)])
                last.then_inc(hT_done, 1)

            def activate(b):
                act.wait_ge(k_done, b + 1)
                act.wait_ge(v_done, b)
                nc.scalar.activation(kT[:], psK[:], ACT.Relu).then_inc(relu_done, 1)
                act.wait_ge(relu_done, b + 1)
                nc.scalar.activation(kT[:], kT[:], ACT.Square).then_inc(sq_done, 1)
                act.wait_ge(r_done, b + 1)
                act.wait_ge(o_done, b)
                nc.scalar.activation(r[:], psR[:], ACT.Sigmoid).then_inc(sig_done, 1)

            act.wait_ge(zero_done, 1)
            modulate(0)
            if True:
                with act.Fori(0, B - 1) as b:
                    modulate(b + 1)
                    activate(b)
            activate(B - 1)


def rotary_qkv_phase(nc, k, d):
    with ExitStack() as ctx:
        sb = lambda n, s, t=F32: ctx.enter_context(nc.sbuf_tensor("rot_" + n, s, t))
        sem = lambda n: nc.alloc_semaphore("rot_" + n)
        ps = lambda n, s: ctx.enter_context(nc.psum_tensor("rot_" + n, s, F32))
        B = k.B
        w = sb("w_qkv", [P, CB, 3 * C])
        cos, sin = sb("cos", [P, J, HD]), sb("sin", [P, J, HD])
        z = sb("z", [P, J, C])
        hT = sb("hT", [P, CB, T])
        by_cos, by_sin = sb("by_cos", [P, 2, 2 * C]), sb("by_sin", [P, 2, 2 * C])
        rot = sb("rot", [P, J, 2 * C])
        rest = sb("rest", [P, 2, T])
        parts = sb("parts", [P, 3, 2 * CB, T], BF16)
        v = sb("v", [P, J, C])
        ln = Norm(nc, ctx, "rot_ln")
        psA = ps("psA", [P, CB, T])
        psQK = ps("psQK", [P, 2, 2 * C])
        psV = ps("psV", [P, 2, T])[:, :, 0:C]
        psT = ps("psT", [P, 2, T])
        weights, z_done, zT_done, hT_done = sem("weights"), sem("z_done"), sem("zT_done"), sem("hT_done")
        qk_done, v_done, prod_done, rot_done = sem("qk_done"), sem("v_done"), sem("prod_done"), sem("rot_done")
        vcopy_done, rT_done, hi_done = sem("vcopy_done"), sem("rT_done"), sem("hi_done")
        rest_done, mid_done, lo_done = sem("rest_done"), sem("mid_done"), sem("lo_done")
        parts_stored, v_stored = sem("parts_stored"), sem("v_stored")
        block = ctx.enter_context(nc.Block())
        NB = 2 * CB

        @block.sync
        def _(sp):
            sp.dma_start(w[:], d["w_qkv"].rearrange("(k p) n -> p k n", p=P)).then_inc(weights, 16)
            sp.dma_start(cos[:], d["cos"]).then_inc(weights, 16)
            sp.dma_start(sin[:], d["sin"]).then_inc(weights, 16)
            with sp.Fori(0, B) as b:
                sp.wait_ge(v_stored, 16 * b)
                sp.wait_ge(vcopy_done, J * b + J)
                sp.dma_start(k.v_dram[b], v[:]).then_inc(v_stored, 16)
                sp.wait_ge(parts_stored, 16 * b)
                sp.wait_ge(hi_done, NB * b + NB)
                sp.wait_ge(mid_done, NB * b + NB)
                sp.wait_ge(lo_done, NB * b + NB)
                sp.dma_start(k.parts_dram[b].rearrange("s n p t -> p s n t"), parts[:]).then_inc(parts_stored, 16)
            sp.wait_ge(v_stored, 16 * B)
            sp.wait_ge(parts_stored, 16 * B)

        @block.vector
        def _(dve):
            def norm(b):
                tile = lambda j: k.x[:, b * J + j, :]
                ln.moments(nc, dve, tile, b)
                dve.wait_ge(zT_done, b)
                ln.apply(nc, dve, z, tile, b).then_inc(z_done, 1)

            def rotate(b):
                for j in range(J):
                    i = j % 2
                    dve.wait_ge(qk_done, J * b + j + 1)
                    dve.wait_ge(rot_done, J * b + max(j - 1, 0))
                    heads = psQK[:, i, :].rearrange("p (h e) -> p h e", e=HD)
                    nc.vector.tensor_tensor(by_cos[:, i, :].rearrange("p (h e) -> p h e", e=HD), heads,
                                            cos[:, j, :].unsqueeze(1).to_broadcast([P, 2 * NH, HD]), ALU.mult)
                    out = by_sin[:, i, :].rearrange("p (h e) -> p h e", e=HD)
                    H2 = HD // 2
                    for half in range(2):
                        own, other = slice(half * H2, half * H2 + H2), slice(H2 - half * H2, HD - half * H2)
                        last = nc.vector.tensor_tensor(out[:, :, own], heads[:, :, other],
                                                       sin[:, j, own].unsqueeze(1).to_broadcast([P, 2 * NH, H2]),
                                                       ALU.mult)
                    last.then_inc(prod_done, 1)

            def split(b):
                for n in range(NB):
                    dve.wait_ge(hi_done, NB * b + n + 1)
                    dve.wait_ge(lo_done, NB * b + max(n - 1, 0))
                    nc.vector.tensor_tensor(rest[:, n % 2, :], psT[:, n % 2, :], parts[:, 0, n, :],
                                            ALU.subtract).then_inc(rest_done, 1)

            norm(0)
            with dve.Fori(0, B - 1) as b:
                rotate(b)
                norm(b + 1)
                split(b)
            rotate(B - 1)
            split(B - 1)

        @block.gpsimd
        def _(pool):
            def add_rotated(b):
                for j in range(J):
                    pool.wait_ge(prod_done, J * b + j + 1)
                    if j == 0:
                        pool.wait_ge(rT_done, NB * b)
                    nc.gpsimd.tensor_tensor(rot[:, j, :], by_cos[:, j % 2, :], by_sin[:, j % 2, :],
                                            ALU.add).then_inc(rot_done, 1)

            def low_parts(b):
                for n in range(NB):
                    pool.wait_ge(mid_done, NB * b + n + 1)
                    nc.gpsimd.tensor_tensor(parts[:, 2, n, :], rest[:, n % 2, :], parts[:, 1, n, :],
                                            ALU.subtract).then_inc(lo_done, 1)

            ln.rsqrt(nc, k, pool, 0)
            with pool.Fori(0, B - 1) as b:
                add_rotated(b)
                ln.rsqrt(nc, k, pool, b + 1)
                low_parts(b)
            add_rotated(B - 1)
            low_parts(B - 1)

        @block.tensor
        def _(pe):
            def transpose_h(b):
                pe.wait_ge(z_done, b + 1)
                pe.wait_ge(hT_done, b)
                to_channels(nc, k, psA, z).then_inc(zT_done, 1)

            def project(b):
                pe.wait_ge(hT_done, b + 1)
                for j in range(J):
                    tok = slice(j * P, (j + 1) * P)
                    pe.wait_ge(prod_done, J * b + max(j - 1, 0))
                    for cb in range(CB):
                        last = nc.tensor.matmul(psQK[:, j % 2, :], hT[:, cb, tok], w[:, cb, 0:2 * C],
                                                start=(cb == 0), stop=(cb == CB - 1))
                    last.then_inc(qk_done, 1)
                    pe.wait_ge(vcopy_done, J * b + max(j - 1, 0))
                    for cb in range(CB):
                        last = nc.tensor.matmul(psV[:, j % 2, :], hT[:, cb, tok], w[:, cb, 2 * C:3 * C],
                                                start=(cb == 0), stop=(cb == CB - 1))
                    last.then_inc(v_done, 1)

            def transpose_rotated(b):
                pe.wait_ge(rot_done, J * b + J)
                for n in range(NB):
                    pe.wait_ge(rest_done, NB * b + max(n - 1, 0))
                    for j in range(J):
                        last = nc.tensor.transpose(psT[:, n % 2, j * P:(j + 1) * P], rot[:, j, n * P:(n + 1) * P],
                                                   k.ident[:])
                    last.then_inc(rT_done, 1)

            pe.wait_ge(weights, 48)
            transpose_h(0)
            project(0)
            with pe.Fori(0, B - 1) as b:
                transpose_h(b + 1)
                transpose_rotated(b)
                project(b + 1)
            transpose_rotated(B - 1)

        @block.scalar
        def _(act):
            def modulate(b):
                act.wait_ge(zT_done, b + 1)
                act.wait_ge(v_done, J * b)
                for cb in range(CB):
                    last = nc.scalar.activation(hT[:, cb, :], psA[:, cb, :], ACT.Identity,
                                                scale=k.mod[:, 1, CA * CB + cb, bass.ds(b, 1)],
                                                bias=k.mod[:, 1, SA * CB + cb, bass.ds(b, 1)])
                last.then_inc(hT_done, 1)

            def copy_v(b):
                act.wait_ge(v_stored, 16 * b)
                for j in range(J):
                    act.wait_ge(v_done, J * b + j + 1)
                    nc.scalar.activation(v[:, j, :], psV[:, j % 2, :], ACT.Copy).then_inc(vcopy_done, 1)

            def split(b):
                act.wait_ge(parts_stored, 16 * b)
                for n in range(NB):
                    act.wait_ge(rT_done, NB * b + n + 1)
                    nc.scalar.activation(parts[:, 0, n, :], psT[:, n % 2, :], ACT.Copy).then_inc(hi_done, 1)
                    act.wait_ge(rest_done, NB * b + n + 1)
                    nc.scalar.activation(parts[:, 1, n, :], rest[:, n % 2, :], ACT.Copy).then_inc(mid_done, 1)

            modulate(0)
            copy_v(0)
            with act.Fori(0, B - 1) as b:
                modulate(b + 1)
                split(b)
                copy_v(b + 1)
            split(B - 1)


def attention_phase(nc, k, tag, causal):
    with ExitStack() as ctx:
        sb = lambda n, s, t=F32: ctx.enter_context(nc.sbuf_tensor(f"{tag}_{n}", s, t))
        sem = lambda n: nc.alloc_semaphore(f"{tag}_{n}")
        ps = lambda n, s: ctx.enter_context(nc.psum_tensor(f"{tag}_{n}", s, F32))
        B = k.B
        half_B = B // 2
        U = NH // G4 * J
        GR = NH // G4
        Q_PARTS, K_PARTS = (0, 0, 1, 0, 2, 1), (0, 1, 0, 2, 0, 1)
        LOADS = len(Q_PARTS) + len(K_PARTS)
        KX = KS + 2
        VW = 2 * HD
        qs = [sb(f"qs{i}", [P, NH, T], BF16) for i in range(2)]
        ks = [sb(f"ks{i}", [P, NH, T], BF16) for i in range(2)]
        vd = [sb(f"vd{i}", [P, J, C]) for i in range(2)]
        vp = [sb(f"vp{i}", [P, J, NH, VW]) for i in range(2)]
        pT = sb("pT", [P, 2, G4, T])
        mx = sb("mx", [P, J, NH])
        mrow = sb("mrow", [NH, 2, T], BF16)
        o_sb = sb("o_sb", [P, T])
        rec = sb("rec", [P, J, G4])
        att = sb("att", [P, J, C])
        one, pause = sb("one", [P, 1]), sb("pause", [P, 1])
        psS = ps("psS", [P, 2, T])
        psT = ps("psT", [P, 2, 2, T])
        psO = ps("psO", [P, T])
        psM = ps("psM", [P, T])
        stack_loaded = [[sem(f"stack_loaded{i}_{g}") for g in range(GR)] for i in range(2)]
        v_loaded = [sem(f"v_loaded{i}") for i in range(2)]
        m_loaded = [sem(f"m_loaded{i}") for i in range(2)]
        ones_done, k_ones, v_exp = sem("ones_done"), sem("k_ones"), sem("v_exp")
        s_done, max_done, mT_done, mhi_done, mrow_done = (sem("s_done"), sem("max_done"), sem("mT_done"),
                                                          sem("mhi_done"), sem("mrow_done"))
        st_done, exp_done, sel_done, pv_done = sem("st_done"), sem("exp_done"), sem("sel_done"), sem("pv_done")
        evac_done, oT_done, rec_done, att_done = sem("evac_done"), sem("oT_done"), sem("rec_done"), sem("att_done")
        att_stored = sem("att_stored")
        block = ctx.enter_context(nc.Block())

        heads_of = lambda u: [u] if u < U - 2 else ([u, u + 1] if u == U - 2 else [])
        first_q = lambda kt: kt * P if causal else 0
        seen = lambda qt: (qt + 1) * P if causal else T

        @block.sync
        def _(sp):
            def load_group(b, p, g):
                for dst, qk, which in ((qs[p], 0, Q_PARTS), (ks[p], 1, K_PARTS)):
                    for n, part in enumerate(which):
                        src = k.parts_dram[b, part, qk * CB:(qk + 1) * CB].rearrange("n p t -> (n p) t")
                        src = src[g * G4 * HD:(g + 1) * G4 * HD].rearrange("(h e) t -> e h t", e=HD)
                        sp.dma_start(dst[n * HD:(n + 1) * HD, g * G4:(g + 1) * G4, :], src
                                     ).then_inc(stack_loaded[p][g], 16)

            def load_v(b, p):
                sp.dma_start(vd[p][:], k.v_dram[b]).then_inc(v_loaded[p], 16)

            def load_maxima(b, p):
                sp.wait_ge(mrow_done, b + 1)
                for n in range(2):
                    sp.dma_start(qs[p][KS + n:KS + n + 1, :, :].rearrange("o h t -> o (h t)"), mrow[:, n, :]
                                 ).then_inc(m_loaded[p], 16)

            def store(b):
                sp.wait_ge(att_done, GR * b + GR)
                sp.dma_start(k.att_dram[b], att[:]).then_inc(att_stored, 16)

            def step(b, p, last_two=False, last=False):
                for g in range(GR):
                    if g == GR - 1 and not last:
                        load_maxima(b + 1, 1 - p)
                    if not last_two:
                        sp.wait_ge(pv_done, U * b + J * (g + 1))
                        load_group(b + 2, p, g)
                if not last_two:
                    sp.wait_ge(v_exp, b + 1)
                    load_v(b + 2, p)
                store(b)

            for p in range(2):
                for g in range(GR):
                    load_group(p, p, g)
                load_v(p, p)
            load_maxima(0, 0)
            if half_B > 1:
                with sp.Fori(0, half_B - 1) as i:
                    for p in range(2):
                        step(2 * i + p, p)
            step(B - 2, 0, last_two=True)
            step(B - 1, 1, last_two=True, last=True)
            sp.wait_ge(att_stored, 16 * B)

        @block.tensor
        def _(pe):
            def scores_by_queries(b, i, p, heads):
                for h in heads:
                    if h % G4 == 0:
                        pe.wait_ge(stack_loaded[p][h // G4], 16 * LOADS * (i + 1))
                    for qt in range(J):
                        n = J * h + qt
                        pe.wait_ge(max_done, J * NH * b + max(n - 1, 0))
                        out = psS[:, qt % 2, 0:seen(qt)]
                        last = nc.tensor.matmul(out, qs[p][0:KS, h, qt * P:(qt + 1) * P], ks[p][0:KS, h, 0:seen(qt)],
                                                start=True, stop=not causal)
                        if causal:
                            last = nc.tensor.matmul(psS[:, qt % 2, qt * P:(qt + 1) * P], k.ident_bf[:], k.mask_bf[:],
                                                    start=False, stop=True)
                        last.then_inc(s_done, 1)

            def transpose_maxima(b):
                pe.wait_ge(max_done, J * NH * (b + 1))
                for j in range(J):
                    last = nc.tensor.transpose(psM[0:NH, j * P:(j + 1) * P], mx[:, j, :], k.ident[:])
                last.then_inc(mT_done, 1)

            def scores_by_keys(b, p, u):
                g, kt = divmod(u, J)
                for pr in range(2):
                    pe.wait_ge(exp_done, 2 * U * b + max(2 * u + pr - 1, 0))
                    for n in range(2):
                        h = G4 * g + 2 * pr + n
                        last = nc.tensor.matmul(psT[:, pr, n, first_q(kt):T], ks[p][0:KX, h, kt * P:(kt + 1) * P],
                                                qs[p][0:KX, h, first_q(kt):T], start=True, stop=True)
                    last.then_inc(st_done, 1)

            def values(b, p, u):
                g, kt = divmod(u, J)
                if causal:
                    pe.wait_ge(sel_done, U * b + u + 1)
                else:
                    pe.wait_ge(exp_done, 2 * U * b + 2 * u + 2)
                if u == 0:
                    pe.wait_ge(v_exp, b + 1)
                if kt == 0:
                    pe.wait_ge(evac_done, GR * b + g)
                for n in range(G4):
                    last = nc.tensor.matmul(psO[VW * n:VW * (n + 1), first_q(kt):T], vp[p][:, kt, G4 * g + n, :],
                                            pT[:, u % 2, n, first_q(kt):T], start=(kt == 0), stop=(kt == J - 1))
                last.then_inc(pv_done, 1)

            def transpose_outputs(b, g):
                pe.wait_ge(evac_done, GR * b + g + 1)
                for j in range(J):
                    last = nc.tensor.transpose(psM[:, j * P:(j + 1) * P], o_sb[:, j * P:(j + 1) * P], k.ident[:])
                last.then_inc(oT_done, 1)

            def step(b, i, p, last=False):
                for u in range(U):
                    if u == 0:
                        pe.wait_ge(m_loaded[p], 32 * (i + 1))
                    scores_by_keys(b, p, u)
                    if not last:
                        scores_by_queries(b + 1, i + p, 1 - p, heads_of(u))
                    if u > 0:
                        values(b, p, u - 1)
                    if u % J == 2 and u > J:
                        if u == J + 2:
                            pe.wait_ge(mrow_done, b + 1)
                        pe.wait_ge(att_done, GR * b + u // J - 1)
                        transpose_outputs(b, u // J - 1)
                    if u == U - 1 and not last:
                        pe.wait_ge(att_done, GR * b + GR - 1)
                        transpose_maxima(b + 1)
                values(b, p, U - 1)
                if not last:
                    pe.wait_ge(mrow_done, b + 2)
                else:
                    pe.wait_ge(att_done, GR * b + GR - 1)
                transpose_outputs(b, GR - 1)

            pe.wait_ge(k_ones, 1)
            scores_by_queries(0, 0, 0, range(NH))
            transpose_maxima(0)
            if half_B > 1:
                with pe.Fori(0, half_B - 1) as i:
                    for p in range(2):
                        step(2 * i + p, i, p)
            step(B - 2, half_B - 1, 0)
            step(B - 1, half_B - 1, 1, last=True)

        @block.scalar
        def _(act):
            def exponentials(b, u):
                kt = u % J
                for pr in range(2):
                    act.wait_ge(st_done, 2 * U * b + 2 * u + pr + 1)
                    if pr == 0:
                        act.wait_ge(pv_done, U * b + max(u - 1, 0))
                    nc.scalar.activation(pT[:, u % 2, 2 * pr:2 * pr + 2, first_q(kt):T], psT[:, pr, :, first_q(kt):T],
                                         ACT.Exp, scale=HD ** -0.5).then_inc(exp_done, 1)

            def read_outputs(b, g):
                act.wait_ge(pv_done, U * b + J * (g + 1))
                act.wait_ge(oT_done, GR * b + g)
                nc.scalar.activation(o_sb[:], psO[:], ACT.Copy).then_inc(evac_done, 1)

            def negate_maxima(b, i, p):
                if i is not None:
                    act.wait_ge(m_loaded[p], 32 * (i + 1))
                act.wait_ge(mT_done, b + 1)
                nc.scalar.activation(mrow[:, 0, :], psM[0:NH, :], ACT.Copy, scale=-1.0).then_inc(mhi_done, 1)

            def step(b, i, p, last=False):
                for u in range(U):
                    exponentials(b, u)
                    if u % J == 0 and u > 0:
                        read_outputs(b, u // J - 1)
                if not last:
                    negate_maxima(b + 1, i, p)
                read_outputs(b, GR - 1)

            negate_maxima(0, None, None)
            if half_B > 1:
                with act.Fori(0, half_B - 1) as i:
                    for p in range(2):
                        step(2 * i + p, i, p)
            step(B - 2, half_B - 1, 0)
            step(B - 1, half_B - 1, 1, last=True)

        @block.vector
        def _(dve):
            def maxima(b, heads):
                for h in heads:
                    if h == 0:
                        dve.wait_ge(mT_done, b)
                    for qt in range(J):
                        dve.wait_ge(s_done, J * NH * b + J * h + qt + 1)
                        nc.vector.reduce_max(mx[:, qt, h:h + 1], psS[:, qt % 2, 0:seen(qt)], axis=AX.X
                                             ).then_inc(max_done, 1)

            def second_part(b):
                dve.wait_ge(mhi_done, b + 1)
                nc.vector.scalar_tensor_tensor(mrow[:, 1, :], psM[0:NH, :], -1.0, mrow[:, 0, :],
                                               ALU.mult, ALU.subtract).then_inc(mrow_done, 1)

            def normalize(b, g):
                heads = psM[:].rearrange("p (j h e) -> p j h e", j=J, e=VW)
                dve.wait_ge(oT_done, GR * b + g + 1)
                nc.vector.reciprocal(rec[:], heads[:, :, :, HD]).then_inc(rec_done, 1)
                dve.wait_ge(rec_done, GR * b + g + 1)
                if g == 0:
                    dve.wait_ge(att_stored, 16 * b)
                out = att[:].rearrange("p j (h e) -> p j h e", e=HD)[:, :, G4 * g:G4 * (g + 1), :]
                nc.vector.tensor_tensor(out, heads[:, :, :, 0:HD], rec[:].unsqueeze(3).to_broadcast([P, J, G4, HD]),
                                        ALU.mult).then_inc(att_done, 1)

            def step(b, last=False):
                for u in range(U):
                    if not last:
                        maxima(b + 1, heads_of(u))
                    if u % J == 2 and u > J:
                        normalize(b, u // J - 1)
                if not last:
                    second_part(b + 1)
                normalize(b, GR - 1)

            for p in range(2):
                last = nc.vector.memset(ks[p][KS:KX, :, :], 1.0)
            last.then_inc(k_ones, 1)
            maxima(0, range(NH))
            second_part(0)
            if half_B > 1:
                with dve.Fori(0, half_B - 1) as i:
                    for p in range(2):
                        step(2 * i + p)
            step(B - 2)
            step(B - 1, last=True)

        @block.gpsimd
        def _(pool):
            def expand_v(b, i, p):
                pool.wait_ge(v_loaded[p], 16 * (i + 1))
                heads = vd[p][:].rearrange("p j (h e) -> p j h e", e=HD)
                nc.gpsimd.tensor_tensor(vp[p][:, :, :, 0:HD], heads, one[:].unsqueeze(2).unsqueeze(3).to_broadcast(
                    [P, J, NH, HD]), ALU.mult).then_inc(v_exp, 1)

            def mask(b, u):
                kt = u % J
                pool.wait_ge(exp_done, 2 * U * b + 2 * u + 2)
                diagonal = pT[:, u % 2, :, kt * P:(kt + 1) * P]
                pool.wait_ge(sel_done, U * b + u)
                nc.gpsimd.tensor_tensor(pause[:], one[:], one[:], ALU.add)
                nc.gpsimd.affine_select(diagonal, diagonal, pattern=[[0, G4], [1, P]], compare_op=ALU.is_ge, fill=0.0,
                                        base=0, channel_multiplier=-1).then_inc(sel_done, 1)

            def step(b, i, p, last=False):
                if not last:
                    pool.wait_ge(pv_done, U * b)
                    expand_v(b + 1, i + p, 1 - p)
                if causal:
                    for u in range(U):
                        mask(b, u)

            for p in range(2):
                nc.gpsimd.memset(vp[p][:, :, :, HD:VW], 1.0)
            nc.gpsimd.memset(one[:], 1.0).then_inc(ones_done, 1)
            pool.wait_ge(ones_done, 1)
            expand_v(0, 0, 0)
            if half_B > 1:
                with pool.Fori(0, half_B - 1) as i:
                    for p in range(2):
                        step(2 * i + p, i, p)
            step(B - 2, half_B - 1, 0)
            step(B - 1, half_B - 1, 1, last=True)


def output_and_qkv_phase(nc, k, d):
    with ExitStack() as ctx:
        sb = lambda n, s, t=F32: ctx.enter_context(nc.sbuf_tensor("mid_" + n, s, t))
        sem = lambda n: nc.alloc_semaphore("mid_" + n)
        ps = lambda n, s: ctx.enter_context(nc.psum_tensor("mid_" + n, s, F32))
        B = k.B
        NB = 2 * CB
        wo, wq, wk, wv = sb("wo", [P, CB, C]), sb("wq", [P, CB, C]), sb("wk", [P, CB, C]), sb("wv", [P, CB, C])
        bv = sb("bv", [P, C])
        gate = sb("gate", [P, C])
        att = sb("att", [P, J, C])
        aT = sb("aT", [P, CB, T])
        y = sb("y", [P, J, C])
        z = sb("z", [P, J, C])
        hT = sb("hT", [P, CB, T])
        rest = sb("rest", [P, 2, T])
        parts = sb("parts", [P, 3, NB, T], BF16)
        v = sb("v", [P, J, C])
        ln = Norm(nc, ctx, "mid_ln")
        psA, psY, psV = ps("psA", [P, CB, T]), ps("psY", [P, J, C]), ps("psV", [P, J, C])
        psQ = ps("psQ", [P, 2, T])
        weights, gate_loaded, att_loaded = sem("weights"), sem("gate_loaded"), sem("att_loaded")
        aT_ps, aT_done, y_done, yg_done, x_done = sem("aT_ps"), sem("aT_done"), sem("y_done"), sem("yg_done"), sem("x_done")
        z_done, zT_done, hT_done, q_done = sem("z_done"), sem("zT_done"), sem("hT_done"), sem("q_done")
        hi_done, rest_done, mid_done, lo_done = sem("hi_done"), sem("rest_done"), sem("mid_done"), sem("lo_done")
        v_done, vb_done, v_stored, parts_stored = sem("v_done"), sem("vb_done"), sem("v_stored"), sem("parts_stored")
        block = ctx.enter_context(nc.Block())
        bias = lambda n: col(k, "bq" if n < CB else "bk", n % CB)

        @block.sync
        def _(sp):
            for ap, src in ((wo, "w_out"), (wq, "Wq"), (wk, "Wk"), (wv, "Wv")):
                sp.dma_start(ap[:], d[src].rearrange("(k p) n -> p k n", p=P)).then_inc(weights, 16)
            sp.dma_start(bv[:], d["rows"][ROWS.index("bv")].partition_broadcast(P)).then_inc(weights, 16)

            def load(b):
                sp.wait_ge(yg_done, b)
                sp.dma_start(gate[:], k.mrows_dram[2, b].partition_broadcast(P)).then_inc(gate_loaded, 16)
                sp.dma_start(att[:], k.att_dram[b]).then_inc(att_loaded, 16)

            def store(b):
                sp.wait_ge(v_stored, 16 * b)
                sp.wait_ge(vb_done, b + 1)
                sp.dma_start(k.v_dram[b], v[:]).then_inc(v_stored, 16)
                sp.wait_ge(parts_stored, 16 * b)
                sp.wait_ge(mid_done, NB * b + NB)
                sp.wait_ge(lo_done, NB * b + NB)
                sp.dma_start(k.parts_dram[b].rearrange("s n p t -> p s n t"), parts[:]).then_inc(parts_stored, 16)

            load(0)
            with sp.Fori(0, B - 1) as b:
                load(b + 1)
                store(b)
            store(B - 1)
            sp.wait_ge(v_stored, 16 * B)
            sp.wait_ge(parts_stored, 16 * B)

        @block.tensor
        def _(pe):
            def project_out(b):
                pe.wait_ge(att_loaded, 16 * b + 16)
                pe.wait_ge(hT_done, b)
                to_channels(nc, k, psA, att).then_inc(aT_ps, 1)
                pe.wait_ge(aT_done, b + 1)
                pe.wait_ge(yg_done, b)
                for j in range(J):
                    for cb in range(CB):
                        last = nc.tensor.matmul(psY[:, j, :], aT[:, cb, j * P:(j + 1) * P], wo[:, cb, :],
                                                start=(cb == 0), stop=(cb == CB - 1))
                last.then_inc(y_done, 1)

            def transpose_h(b):
                pe.wait_ge(z_done, b + 1)
                to_channels(nc, k, psA, z).then_inc(zT_done, 1)

            def project_v(b):
                pe.wait_ge(hT_done, b + 1)
                pe.wait_ge(vb_done, b)
                for j in range(J):
                    for cb in range(CB):
                        last = nc.tensor.matmul(psV[:, j, :], hT[:, cb, j * P:(j + 1) * P], wv[:, cb, :],
                                                start=(cb == 0), stop=(cb == CB - 1))
                last.then_inc(v_done, 1)

            def project_qk(b):
                for n in range(NB):
                    w = wq if n < CB else wk
                    pe.wait_ge(rest_done, NB * b + max(n - 1, 0))
                    for cb in range(CB):
                        last = nc.tensor.matmul(psQ[:, n % 2, :], w[:, cb, (n % CB) * P:(n % CB + 1) * P],
                                                hT[:, cb, :], start=(cb == 0), stop=(cb == CB - 1))
                    last.then_inc(q_done, 1)

            pe.wait_ge(weights, 80)
            project_out(0)
            transpose_h(0)
            with pe.Fori(0, B - 1) as b:
                project_v(b)
                project_out(b + 1)
                project_qk(b)
                transpose_h(b + 1)
            project_v(B - 1)
            project_qk(B - 1)

        @block.scalar
        def _(act):
            def copy_attention(b):
                act.wait_ge(aT_ps, b + 1)
                act.wait_ge(y_done, b)
                nc.scalar.activation(aT[:], psA[:], ACT.Copy).then_inc(aT_done, 1)

            def modulate(b):
                act.wait_ge(zT_done, b + 1)
                act.wait_ge(v_done, b)
                act.wait_ge(q_done, NB * b)
                for cb in range(CB):
                    last = nc.scalar.activation(hT[:, cb, :], psA[:, cb, :], ACT.Identity,
                                                scale=k.mod[:, 1, CBM * CB + cb, bass.ds(b, 1)],
                                                bias=k.mod[:, 1, SB * CB + cb, bass.ds(b, 1)])
                last.then_inc(hT_done, 1)

            def split(b):
                act.wait_ge(parts_stored, 16 * b)
                for n in range(NB):
                    act.wait_ge(q_done, NB * b + n + 1)
                    nc.scalar.activation(parts[:, 0, n, :], psQ[:, n % 2, :], ACT.Identity, bias=bias(n)
                                         ).then_inc(hi_done, 1)
                    act.wait_ge(rest_done, NB * b + n + 1)
                    nc.scalar.activation(parts[:, 1, n, :], rest[:, n % 2, :], ACT.Copy).then_inc(mid_done, 1)

            copy_attention(0)
            modulate(0)
            with act.Fori(0, B - 1) as b:
                copy_attention(b + 1)
                split(b)
                modulate(b + 1)
            split(B - 1)

        @block.vector
        def _(dve):
            def residual(b):
                dve.wait_ge(y_done, b + 1)
                dve.wait_ge(gate_loaded, 16 * b + 16)
                dve.wait_ge(x_done, b)
                nc.vector.tensor_tensor(y[:], psY[:], over_tiles(gate[:]), ALU.mult).then_inc(yg_done, 1)
                dve.wait_ge(yg_done, b + 1)
                xb = k.x[:, bass.ds(b * J, J), :]
                nc.vector.tensor_tensor(xb, xb, y[:], ALU.add).then_inc(x_done, 1)
                dve.wait_ge(x_done, b + 1)
                nc.vector.memset(ln.pause[:], 0.0)
                tile = lambda j: k.x[:, b * J + j, :]
                ln.moments(nc, dve, tile, b)
                dve.wait_ge(zT_done, b)
                ln.apply(nc, dve, z, tile, b).then_inc(z_done, 1)

            def add_bias(b):
                dve.wait_ge(v_done, b + 1)
                dve.wait_ge(v_stored, 16 * b)
                nc.vector.tensor_tensor(v[:], psV[:], over_tiles(bv[:]), ALU.add).then_inc(vb_done, 1)

            def split(b, blocks):
                for n in blocks:
                    dve.wait_ge(hi_done, NB * b + n + 1)
                    dve.wait_ge(lo_done, NB * b + max(n - 1, 0))
                    nc.vector.scalar_tensor_tensor(rest[:, n % 2, :], psQ[:, n % 2, :], bias(n), parts[:, 0, n, :],
                                                   ALU.add, ALU.subtract).then_inc(rest_done, 1)

            dve.wait_ge(weights, 80)
            residual(0)
            with dve.Fori(0, B - 1) as b:
                add_bias(b)
                split(b, range(0, 2))
                residual(b + 1)
                split(b, range(2, NB))
            add_bias(B - 1)
            split(B - 1, range(NB))

        @block.gpsimd
        def _(pool):
            def low_parts(b, blocks):
                for n in blocks:
                    pool.wait_ge(mid_done, NB * b + n + 1)
                    if n == 0:
                        pool.wait_ge(parts_stored, 16 * b)
                    nc.gpsimd.tensor_tensor(parts[:, 2, n, :], rest[:, n % 2, :], parts[:, 1, n, :],
                                            ALU.subtract).then_inc(lo_done, 1)

            ln.rsqrt(nc, k, pool, 0)
            with pool.Fori(0, B - 1) as b:
                low_parts(b, range(0, 2))
                ln.rsqrt(nc, k, pool, b + 1)
                low_parts(b, range(2, NB))
            low_parts(B - 1, range(NB))


ROW_X1, ROW_X, ROW_GATE, ROW_ID, ROW = 0, C, 2 * C, 3 * C, 3 * C + 4
I32 = mybir.dt.int32


def route_phase(nc, k, d):
    with ExitStack() as ctx:
        sb = lambda n, s, t=F32: ctx.enter_context(nc.sbuf_tensor("rou_" + n, s, t))
        sem = lambda n: nc.alloc_semaphore("rou_" + n)
        ps = lambda n, s: ctx.enter_context(nc.psum_tensor("rou_" + n, s, F32))
        B = k.B
        wo = sb("wo", [P, CB, C])
        rowb = {n: sb(f"rowb_{n}", [P, C]) for n in ("bo", "l1_ln1_g", "l1_ln1_b", "router_w")}
        before, ones = sb("before", [P, P]), sb("ones", [P, P])
        experts = sb("experts", [P, NE])
        ids = sb("ids", [P, B * J], I32)
        mrow = sb("mrow", [P, 3, C])
        shift = sb("shift", [P, C])
        att = sb("att", [P, J, C])
        aT = sb("aT", [P, CB, T])
        z, t = sb("z", [P, J, C]), sb("t", [P, J, C])
        rows = sb("rows_out", [P, J, ROW])
        junk = sb("junk", [P, C])
        key, key_f, above = sb("key", [P, J]), sb("key_f", [P, J]), sb("above", [P, J])
        key_i, expert_i, expert_f = sb("key_i", [P, J], I32), sb("expert_i", [P, J], I32), sb("expert_f", [P, J])
        member = sb("member", [P, J, NE])
        place = sb("place", [P, J, NE])
        slot = sb("slot", [P, J])
        slot_i = sb("slot_i", [P, J], I32)
        pool_pause = sb("pool_pause", [P, 1])
        nxt = k.next_row
        ln0, ln1 = Norm(nc, ctx, "rou_ln0"), Norm(nc, ctx, "rou_ln1")
        psA, psY = ps("psA", [P, CB, T]), ps("psY", [P, J, C])
        psR = ps("psR", [P, T])
        PREFIX, TOTAL = psR[:, 0:J * NE], psR[:, J * NE:(J + 1) * NE]
        weights, mrow_loaded, att_loaded, init = sem("weights"), sem("mrow_loaded"), sem("att_loaded"), sem("init")
        aT_ps, aT_done, y_done = sem("aT_ps"), sem("aT_done"), sem("y_done")
        z_done, shift_done, zs_done, src_done = sem("z_done"), sem("shift_done"), sem("zs_done"), sem("src_done")
        t_done, z1_done, z1g_done, x1_done = sem("t_done"), sem("z1_done"), sem("z1g_done"), sem("x1_done")
        copied, key_done, step, member_done = sem("copied"), sem("key_done"), sem("step"), sem("member_done")
        ranks_done, slot_done, scattered = sem("ranks_done"), sem("slot_done"), sem("scattered")
        block = ctx.enter_context(nc.Block())
        STEPS = 10

        @block.sync
        def _(sp):
            sp.dma_start(wo[:], d["Wo"].rearrange("(k p) n -> p k n", p=P)).then_inc(weights, 16)
            for n, ap in rowb.items():
                sp.dma_start(ap[:], d["rows"][ROWS.index(n)].partition_broadcast(P)).then_inc(weights, 16)
            for ap, n in ((before, "before"), (experts, "experts"), (ids, "ids")):
                sp.dma_start(ap[:], d[n]).then_inc(weights, 16)
            with sp.Fori(0, B) as b:
                sp.wait_ge(aT_ps, b)
                sp.dma_start(att[:], k.att_dram[b]).then_inc(att_loaded, 16)
                sp.wait_ge(shift_done, b)
                sp.wait_ge(zs_done, b)
                sp.wait_ge(copied, b)
                for n, row in enumerate((4, 5, 3)):
                    sp.dma_start(mrow[:, n, :], k.mrows_dram[row, b].partition_broadcast(P)).then_inc(mrow_loaded, 16)

        @block.tensor
        def _(pe):
            def project_out(b):
                pe.wait_ge(att_loaded, 16 * b + 16)
                pe.wait_ge(aT_done, b)
                to_channels(nc, k, psA, att).then_inc(aT_ps, 1)
                pe.wait_ge(aT_done, b + 1)
                pe.wait_ge(t_done, b)
                for j in range(J):
                    for cb in range(CB):
                        last = nc.tensor.matmul(psY[:, j, :], aT[:, cb, j * P:(j + 1) * P], wo[:, cb, :],
                                                start=(cb == 0), stop=(cb == CB - 1))
                last.then_inc(y_done, 1)

            def count(b):
                pe.wait_ge(member_done, b + 1)
                pe.wait_ge(slot_done, b)
                for j in range(J):
                    out = PREFIX[:, j * NE:(j + 1) * NE]
                    nc.tensor.matmul(out, before[:], member[:, j, :], start=True, stop=(j == 0))
                    for earlier in range(j):
                        nc.tensor.matmul(out, ones[:], member[:, earlier, :], start=False, stop=(earlier == j - 1))
                for j in range(J):
                    last = nc.tensor.matmul(TOTAL, ones[:], member[:, j, :], start=(j == 0), stop=(j == J - 1))
                last.then_inc(ranks_done, 1)

            pe.wait_ge(weights, 128)
            pe.wait_ge(init, 1)
            project_out(0)
            with pe.Fori(0, B - 1) as b:
                project_out(b + 1)
                count(b)
            count(B - 1)

        @block.scalar
        def _(act):
            def copy_attention(b):
                act.wait_ge(aT_ps, b + 1)
                act.wait_ge(y_done, b)
                nc.scalar.activation(aT[:], psA[:], ACT.Copy).then_inc(aT_done, 1)

            def fill_rows(b):
                act.wait_ge(mrow_loaded, 48 * b + 48)
                act.wait_ge(scattered, 64 * b)
                nc.scalar.activation(rows[:, :, ROW_X:ROW_X + C], k.x[:, bass.ds(b * J, J), :], ACT.Copy)
                nc.scalar.activation(rows[:, :, ROW_GATE:ROW_GATE + C], over_tiles(mrow[:, 2, :]), ACT.Copy
                                     ).then_inc(copied, 1)

            copy_attention(0)
            with act.Fori(0, B - 1) as b:
                fill_rows(b)
                copy_attention(b + 1)
            fill_rows(B - 1)

        @block.gpsimd
        def _(pool):
            def source(b):
                ln0.rsqrt(nc, k, pool, b)
                pool.wait_ge(mrow_loaded, 48 * b + 48)
                pool.wait_ge(z_done, b + 1)
                nc.gpsimd.tensor_tensor(z[:], z[:], over_tiles(mrow[:, 0, :]), ALU.mult).then_inc(zs_done, 1)
                pool.wait_ge(zs_done, b + 1)
                pool.wait_ge(shift_done, b + 1)
                nc.gpsimd.tensor_tensor(z[:], z[:], over_tiles(shift[:]), ALU.add).then_inc(src_done, 1)

            def scatter(b):
                pool.wait_ge(slot_done, b + 1)
                pool.wait_ge(copied, b + 1)
                nc.gpsimd.tensor_tensor(pool_pause[:], k.eps[:, 0:1], k.eps[:, 0:1], ALU.add)
                for j in range(J):
                    nc.gpsimd.indirect_dma_start(k.rows_dram, bass.IndirectOffsetOnAxis(ap=slot_i[:, j:j + 1], axis=0),
                                                 rows[:, j, :], None).then_inc(scattered, 16)

            nc.gpsimd.memset(ones[:], 1.0)
            nc.gpsimd.memset(rows[:, :, ROW_ID:ROW], 0.0).then_inc(init, 1)
            pool.wait_ge(init, 1)
            source(0)
            ln1.rsqrt(nc, k, pool, 0)
            with pool.Fori(0, B - 1) as b:
                source(b + 1)
                scatter(b)
                ln1.rsqrt(nc, k, pool, b + 1)
            scatter(B - 1)
            pool.wait_ge(scattered, 64 * B)

        @block.vector
        def _(dve):
            def norm_source(b):
                tile = lambda j: k.x[:, b * J + j, :]
                ln0.moments(nc, dve, tile, b)
                dve.wait_ge(t_done, b)
                ln0.apply(nc, dve, z, tile, b).then_inc(z_done, 1)
                dve.wait_ge(mrow_loaded, 48 * b + 48)
                dve.wait_ge(src_done, b)
                nc.vector.tensor_tensor(shift[:], mrow[:, 1, :], rowb["bo"][:], ALU.add).then_inc(shift_done, 1)

            def norm1(b):
                dve.wait_ge(y_done, b + 1)
                dve.wait_ge(src_done, b + 1)
                dve.wait_ge(x1_done, b)
                nc.vector.tensor_tensor(t[:], psY[:], z[:], ALU.add).then_inc(t_done, 1)
                dve.wait_ge(t_done, b + 1)
                nc.vector.memset(ln1.pause[:], 0.0)
                tile = lambda j: t[:, j, :]
                ln1.moments(nc, dve, tile, b)
                ln1.apply(nc, dve, t, tile, b).then_inc(z1_done, 1)
                dve.wait_ge(z1_done, b + 1)
                nc.vector.tensor_tensor(t[:], t[:], over_tiles(rowb["l1_ln1_g"][:]), ALU.mult).then_inc(z1g_done, 1)
                dve.wait_ge(z1g_done, b + 1)
                dve.wait_ge(scattered, 64 * b)
                nc.vector.tensor_copy(rows[:, :, ROW_ID:ROW_ID + 1].bitcast(I32), ids[:, bass.ds(b * J, J)].unsqueeze(2))
                nc.vector.tensor_tensor(rows[:, :, ROW_X1:ROW_X1 + C], t[:], over_tiles(rowb["l1_ln1_b"][:]), ALU.add
                                        ).then_inc(x1_done, 1)

            def route(b):
                taken = [0]

                def follow(instruction):
                    taken[0] += 1
                    instruction.then_inc(step, 1)
                    dve.wait_ge(step, STEPS * b + taken[0])

                dve.wait_ge(x1_done, b + 1)
                for j in range(J):
                    instruction = nc.vector.tensor_tensor_reduce(
                        out=junk[:], in0=rows[:, j, ROW_X1:ROW_X1 + C], in1=rowb["router_w"][:], scale=1.0,
                        scalar=k.cols[:, COLS["router_b"][0]:COLS["router_b"][0] + 1], op0=ALU.mult, op1=ALU.add,
                        accum_out=key[:, j:j + 1])
                    if j < J - 1:
                        instruction.then_inc(key_done, 1)
                        dve.wait_ge(key_done, (J - 1) * b + j + 1)
                follow(instruction)
                follow(nc.vector.tensor_copy(key_i[:], key[:]))
                follow(nc.vector.tensor_copy(key_f[:], key_i[:]))
                follow(nc.vector.tensor_tensor(above[:], key_f[:], key[:], ALU.is_gt))
                follow(nc.vector.tensor_tensor(key_i[:], key_f[:], above[:], ALU.subtract))
                follow(nc.vector.tensor_scalar(expert_i[:], key_i[:], NE - 1, None, ALU.bitwise_and))
                follow(nc.vector.tensor_copy(expert_f[:], expert_i[:]))
                nc.vector.tensor_tensor(member[:], expert_f[:].unsqueeze(2).to_broadcast([P, J, NE]),
                                        experts[:].unsqueeze(1).to_broadcast([P, J, NE]), ALU.is_equal
                                        ).then_inc(member_done, 1)
                dve.wait_ge(member_done, b + 1)
                dve.wait_ge(ranks_done, b + 1)
                follow(nc.vector.tensor_tensor(place[:], PREFIX.rearrange("p (j e) -> p j e", e=NE),
                                               nxt[:].unsqueeze(1).to_broadcast([P, J, NE]), ALU.add))
                follow(nc.vector.tensor_tensor(place[:], place[:], member[:], ALU.mult))
                nc.vector.tensor_tensor(nxt[:], nxt[:], TOTAL, ALU.add)
                follow(nc.vector.tensor_reduce(slot[:], place[:], op=ALU.add, axis=AX.X))
                dve.wait_ge(scattered, 64 * b)
                nc.vector.tensor_copy(slot_i[:], slot[:]).then_inc(slot_done, 1)
                dve.wait_ge(slot_done, b + 1)
                nc.vector.memset(ln1.pause[:], 0.0)
                assert taken[0] == STEPS

            dve.wait_ge(weights, 128)
            dve.wait_ge(init, 1)
            nc.vector.tensor_scalar(nxt[:], experts[:], float(k.CAP), None, ALU.mult)
            norm_source(0)
            norm1(0)
            with dve.Fori(0, B - 1) as b:
                route(b)
                norm_source(b + 1)
                norm1(b + 1)
            route(B - 1)


def expert_phase(nc, k, d, out):
    with ExitStack() as ctx:
        sb = lambda n, s, t=F32: ctx.enter_context(nc.sbuf_tensor("exp_" + n, s, t))
        sem = lambda n: nc.alloc_semaphore("exp_" + n)
        ps = lambda n, s: ctx.enter_context(nc.psum_tensor("exp_" + n, s, F32))
        N = k.B * T
        NT = k.NT
        assert NT % 2 == 0
        PADS = 2 * NE
        w1, w2 = k.moe_w1, k.moe_w2
        b1 = sb("b1", [P, NE, FF])
        b2 = sb("b2", [P, NE, C])
        rowb = {n: sb(f"rowb_{n}", [P, C]) for n in ("l1_ln2_g", "l1_ln2_b")}
        experts = sb("experts", [P, NE])
        lane = sb("lane", [P, 1])
        pad_ids = sb("pad_ids", [P, 1], I32)
        pad = sb("pad", [P, ROW])
        pad_row = sb("pad_row", [P, PADS])
        pad_slot = sb("pad_slot", [P, PADS], I32)
        number = sb("number", [1, NT])
        tiles_f, tiles_i = sb("tiles_f", [1, NE]), sb("tiles_i", [1, NE], I32)
        ends, jump = sb("ends", [1, NE]), sb("jump", [1, NE])
        reached = sb("reached", [1, NT])
        plan_e, plan_r = sb("plan_e", [1, NT]), sb("plan_r", [1, NT])
        expert_of, row_of = sb("expert_of", [1, NT], I32), sb("row_of", [1, NT], I32)
        rt = [sb(f"rt{i}", [P, ROW]) for i in range(2)]
        x1T = [sb(f"x1T{i}", [P, CB, P]) for i in range(2)]
        hid = sb("hid", [P, FF])
        hidT = sb("hidT", [P, FB, P])
        t = [sb(f"t{i}", [P, C]) for i in range(2)]
        stats, mv = sb("stats", [P, 6]), sb("mv", [P, 2])
        pool_pause = sb("pool_pause", [P, 1])
        ve, rstd, pause = sb("ve", [P, 1]), sb("rstd", [P, 1]), sb("pause", [P, 1])
        psX, psH, psT = ps("psX", [P, CB, P]), ps("psH", [P, 2, T]), ps("psT", [P, FB, P])
        psY = ps("psY", [P, C])
        loaded, init, step, plan_done, padded = sem("loaded"), sem("init"), sem("step"), sem("plan_done"), sem("padded")
        rt_loaded = [sem(f"rt_loaded{i}") for i in range(2)]
        scattered = [sem(f"scattered{i}") for i in range(2)]
        xT_ps, xT_done, hid_ps, hid_done = sem("xT_ps"), sem("xT_done"), sem("hid_ps"), sem("hid_done")
        hT_ps, hT_done, y_done, t_done = sem("hT_ps"), sem("hT_done"), sem("y_done"), sem("t_done")
        tb_done, stats_done, mv_done, ve_done = sem("tb_done"), sem("stats_done"), sem("mv_done"), sem("ve_done")
        rstd_done, z_done, u_done = sem("rstd_done"), sem("z_done"), sem("u_done")
        block = ctx.enter_context(nc.Block())
        half = NT // 2

        @block.sync
        def _(sp):
            for src, ap in (("moe_b1_rows", b1), ("moe_b2_rows", b2)):
                sp.dma_start(ap[:], d[src].partition_broadcast(P)).then_inc(loaded, 16)
            for n, ap in rowb.items():
                sp.dma_start(ap[:], d["rows"][ROWS.index(n)].partition_broadcast(P)).then_inc(loaded, 16)
            for n, ap in (("experts", experts), ("lane", lane), ("pad_ids", pad_ids), ("number", number)):
                sp.dma_start(ap[:], d[n]).then_inc(loaded, 16)

            def load(c, i, p):
                row = sp.value_load(row_of[0:1, bass.ds(c, 1)], min_val=0, max_val=k.ROWS_ALL - P)
                if i is not None:
                    sp.wait_ge(scattered[p], 16 * (i + 1))
                sp.dma_start(rt[p][:], k.rows_dram[bass.ds(row, P), :]).then_inc(rt_loaded[p], 16)

            sp.wait_ge(plan_done, 1)
            sp.wait_ge(padded, 16 * PADS)
            load(0, None, 0)
            load(1, None, 1)
            with sp.Fori(0, half - 1) as i:
                for p in range(2):
                    load(2 * i + 2 + p, i, p)

        @block.vector
        def _(dve):
            taken = [0]

            def follow(instruction):
                taken[0] += 1
                instruction.then_inc(step, 1)
                dve.wait_ge(step, taken[0])

            dve.wait_ge(loaded, 128)
            dve.wait_ge(init, 1)
            nc.vector.tensor_copy(pad[:, ROW_ID:ROW_ID + 1].bitcast(I32), pad_ids[:])
            for n in range(PADS):
                if n < NE:
                    last = nc.vector.tensor_tensor(pad_row[:, n:n + 1], lane[:], k.next_row[:, n:n + 1], ALU.add)
                else:
                    last = nc.vector.tensor_scalar(pad_row[:, n:n + 1], lane[:], float(NE * k.CAP + (n - NE) * P),
                                                   None, ALU.add)
            follow(last)
            follow(nc.vector.tensor_copy(pad_slot[:], pad_row[:]))
            follow(nc.vector.tensor_scalar(tiles_f[:], experts[0:1, :], -float(k.CAP), float(P - 1), ALU.mult, ALU.add))
            follow(nc.vector.tensor_tensor(tiles_i[:], tiles_f[:], k.next_row[0:1, :], ALU.add))
            follow(nc.vector.tensor_scalar(tiles_i[:], tiles_i[:], 7, None, ALU.arith_shift_right))
            follow(nc.vector.tensor_copy(tiles_f[:], tiles_i[:]))
            follow(nc.vector.tensor_scalar(jump[:], tiles_f[:], -float(P), float(k.CAP), ALU.mult, ALU.add))
            follow(nc.vector.tensor_copy(ends[:], tiles_f[:]))
            for e in range(1, NE):
                follow(nc.vector.tensor_tensor(ends[:, e:e + 1], ends[:, e:e + 1], ends[:, e - 1:e], ALU.add))
            follow(nc.vector.tensor_scalar(plan_r[:], number[:], float(P), None, ALU.mult))
            follow(nc.vector.memset(plan_e[:], 0.0))
            for e in range(NE):
                follow(nc.vector.tensor_scalar(reached[:], number[:], ends[:, e:e + 1], None, ALU.is_ge))
                follow(nc.vector.tensor_tensor(plan_e[:], plan_e[:], reached[:], ALU.add))
                follow(nc.vector.scalar_tensor_tensor(plan_r[:], reached[:], jump[:, e:e + 1], plan_r[:],
                                                      ALU.mult, ALU.add))
            nc.vector.tensor_scalar(expert_of[:], plan_e[:], float(NE - 1), None, ALU.min)
            nc.vector.tensor_copy(row_of[:], plan_r[:]).then_inc(plan_done, 1)
            dve.wait_ge(plan_done, 1)

            def hidden_bias(c):
                e = dve.value_load(expert_of[0:1, bass.ds(c, 1)], min_val=0, max_val=NE - 1)
                for n in range(2):
                    dve.wait_ge(hid_ps, 2 * c + n + 1)
                    if n == 0:
                        dve.wait_ge(hT_ps, c)
                    nc.vector.tensor_tensor(hid[:, n * T:(n + 1) * T], psH[:, n, :],
                                            b1[:, bass.ds(e, 1), n * T:(n + 1) * T].rearrange("p o f -> p (o f)"),
                                            ALU.add).then_inc(hid_done, 1)

            def norm(c, p):
                e = dve.value_load(expert_of[0:1, bass.ds(c, 1)], min_val=0, max_val=NE - 1)
                dve.wait_ge(y_done, c + 1)
                nc.vector.tensor_tensor(t[p][:], psY[:], rt[p][:, ROW_X1:ROW_X1 + C], ALU.add).then_inc(t_done, 1)
                dve.wait_ge(t_done, c + 1)
                nc.vector.tensor_tensor(t[p][:], t[p][:], b2[:, bass.ds(e, 1), :].rearrange("p o f -> p (o f)"),
                                        ALU.add).then_inc(tb_done, 1)
                dve.wait_ge(tb_done, c + 1)
                nc.vector.bn_stats(stats[:], t[p][:]).then_inc(stats_done, 1)
                dve.wait_ge(stats_done, c + 1)
                nc.vector.memset(pause[:], 0.0)
                nc.vector.bn_aggr(mv[:], stats[:]).then_inc(mv_done, 1)
                dve.wait_ge(rstd_done, c + 1)
                nc.vector.tensor_scalar(t[p][:], t[p][:], mv[:, 0:1], rstd[:], ALU.subtract, ALU.mult
                                        ).then_inc(z_done, 1)

            hidden_bias(0)
            with dve.Fori(0, half - 1) as i:
                for p in range(2):
                    hidden_bias(2 * i + p + 1)
                    norm(2 * i + p, p)
            hidden_bias(NT - 1)
            norm(NT - 2, 0)
            norm(NT - 1, 1)

        @block.tensor
        def _(pe):
            def expert(c):
                return pe.value_load(expert_of[0:1, bass.ds(c, 1)], min_val=0, max_val=NE - 1)

            def transpose_x(c, i, p):
                pe.wait_ge(rt_loaded[p], 16 * (i + 1))
                pe.wait_ge(xT_done, c)
                for cb in range(CB):
                    last = nc.tensor.transpose(psX[:, cb, :], rt[p][:, ROW_X1 + cb * P:ROW_X1 + (cb + 1) * P],
                                               k.ident[:])
                last.then_inc(xT_ps, 1)

            def hidden(c, p, e):
                pe.wait_ge(xT_done, c + 1)
                for n in range(2):
                    pe.wait_ge(hid_done, 2 * c)
                    for cb in range(CB):
                        last = nc.tensor.matmul(psH[:, n, :], x1T[p][:, cb, :],
                                                w1[:, bass.ds(e, 1), cb, n * T:(n + 1) * T].rearrange("p o f -> p (o f)"),
                                                start=(cb == 0), stop=(cb == CB - 1))
                    last.then_inc(hid_ps, 1)

            def transpose_hidden(c):
                pe.wait_ge(hid_done, 2 * c + 2)
                pe.wait_ge(hT_done, c)
                for f in range(FB):
                    last = nc.tensor.transpose(psT[:, f, :], hid[:, f * P:(f + 1) * P], k.ident[:])
                last.then_inc(hT_ps, 1)

            def output(c, e):
                pe.wait_ge(hT_done, c + 1)
                pe.wait_ge(t_done, c)
                for f in range(FB):
                    last = nc.tensor.matmul(psY[:], hidT[:, f, :],
                                            w2[:, bass.ds(e, 1), f, :].rearrange("p o f -> p (o f)"),
                                            start=(f == 0), stop=(f == FB - 1))
                last.then_inc(y_done, 1)

            pe.wait_ge(plan_done, 1)
            pe.wait_ge(k.moe_loaded, 32)
            transpose_x(0, 0, 0)
            hidden(0, 0, expert(0))
            transpose_hidden(0)
            transpose_x(1, 0, 1)
            with pe.Fori(0, half - 1) as i:
                for p in range(2):
                    c = 2 * i + p
                    hidden(c + 1, 1 - p, expert(c + 1))
                    output(c, expert(c))
                    transpose_hidden(c + 1)
                    transpose_x(c + 2, i + 1, p)
            hidden(NT - 1, 1, expert(NT - 1))
            output(NT - 2, expert(NT - 2))
            transpose_hidden(NT - 1)
            output(NT - 1, expert(NT - 1))

        @block.scalar
        def _(act):
            def copy_x(c, p):
                act.wait_ge(xT_ps, c + 1)
                act.wait_ge(hid_ps, 2 * c)
                nc.scalar.activation(x1T[p][:], psX[:], ACT.Copy).then_inc(xT_done, 1)

            def relu(c):
                act.wait_ge(hT_ps, c + 1)
                act.wait_ge(y_done, c)
                nc.scalar.activation(hidT[:], psT[:], ACT.Relu).then_inc(hT_done, 1)

            copy_x(0, 0)
            relu(0)
            copy_x(1, 1)
            with act.Fori(0, half - 1) as i:
                for p in range(2):
                    relu(2 * i + p + 1)
                    copy_x(2 * i + p + 2, p)
            relu(NT - 1)

        @block.gpsimd
        def _(pool):
            def finish(c, p):
                pool.wait_ge(mv_done, c + 1)
                nc.gpsimd.tensor_tensor(ve[:], mv[:, 1:2], k.eps[:, 0:1], ALU.add).then_inc(ve_done, 1)
                pool.wait_ge(ve_done, c + 1)
                nc.gpsimd.tensor_tensor(rstd[:], ve[:], k.minus_half[:, 0:1], ALU.pow).then_inc(rstd_done, 1)
                pool.wait_ge(z_done, c + 1)
                for n, (operand, op) in enumerate(((rowb["l1_ln2_g"][:], ALU.mult), (rowb["l1_ln2_b"][:], ALU.add),
                                                   (rt[p][:, ROW_GATE:ROW_GATE + C], ALU.mult),
                                                   (rt[p][:, ROW_X:ROW_X + C], ALU.add))):
                    nc.gpsimd.tensor_tensor(t[p][:], t[p][:], operand, op).then_inc(u_done, 1)
                    pool.wait_ge(u_done, 4 * c + n + 1)
                nc.gpsimd.tensor_tensor(pool_pause[:], k.eps[:, 0:1], k.eps[:, 0:1], ALU.add)
                nc.gpsimd.indirect_dma_start(out, bass.IndirectOffsetOnAxis(
                    ap=rt[p][:, ROW_ID:ROW_ID + 1].bitcast(mybir.dt.uint32), axis=0), t[p][:], None,
                    bounds_check=last_token, oob_is_err=False).then_inc(scattered[p], 16)

            last_token = nc.gpsimd.to_reg(N - 1)
            nc.gpsimd.memset(pad[:], 0.0).then_inc(init, 1)
            pool.wait_ge(plan_done, 1)
            for n in range(PADS):
                nc.gpsimd.indirect_dma_start(k.rows_dram, bass.IndirectOffsetOnAxis(ap=pad_slot[:, n:n + 1], axis=0),
                                             pad[:], None).then_inc(padded, 16)
            with pool.Fori(0, half) as i:
                for p in range(2):
                    finish(2 * i + p, p)
            for p in range(2):
                pool.wait_ge(scattered[p], 16 * half)


def cleared(nc):
    return nc.cleanup_on_exit()


def build(nc, d, out, B, upto="all"):
    k = Core()
    k.B = B
    with ExitStack() as ctx:
        sb = lambda n, s, t=F32: ctx.enter_context(nc.sbuf_tensor(n, s, t))
        k.x = sb("x_res", [P, B * J, C])
        k.mod = sb("mod", [P, 2, 12, B])
        k.cols = sb("cols_sb", [P, NCOLS])
        k.ident = sb("ident_sb", [P, P])
        k.ident_bf = sb("ident_bf", [P, P], BF16)
        k.mask_bf = sb("mask_bf", [P, P], BF16)
        k.half = sb("half", [P, T])
        k.eps = sb("eps", [P, J])
        k.minus_half = sb("minus_half", [P, J])
        k.mrows_dram = nc.dram_tensor("mrows", (len(MROWS), B, C), F32, kind="Internal").ap()
        init = ctx.enter_context(nc.semaphore("consts"))
        with nc.Block() as block:
            @block.gpsimd
            def _(pool):
                nc.gpsimd.memset(k.eps[:], EPS)
                nc.gpsimd.memset(k.minus_half[:], -0.5).then_inc(init, 1)
                pool.wait_ge(init, 1)
        with cleared(nc):
            setup_phase(nc, k, d)
        k.parts_dram = nc.dram_tensor("parts_dram", (B, 3, 2 * CB, P, T), BF16, kind="Internal").ap()
        k.att_dram = nc.dram_tensor("att_dram", (B, P, J, C), F32, kind="Internal").ap()
        k.v_dram = nc.dram_tensor("v_dram", (B, P, J, C), F32, kind="Internal").ap()
        with cleared(nc):
            retention_phase(nc, k, d)
        if upto != "A":
            with cleared(nc):
                channel_mix_phase(nc, k, d)
        if upto not in "AB":
            with cleared(nc):
                rotary_qkv_phase(nc, k, d)
            with cleared(nc):
                attention_phase(nc, k, "causal", True)
            with cleared(nc):
                output_and_qkv_phase(nc, k, d)
        if upto == "all":
            with cleared(nc):
                attention_phase(nc, k, "full", False)
            k.CAP = B * T + P
            k.ROWS_ALL = NE * k.CAP + NE * P
            k.NT = B * J + NE
            k.rows_dram = nc.dram_tensor("rows_dram", (k.ROWS_ALL, ROW), F32, kind="Internal").ap()
            k.next_row = sb("next_row", [P, NE])
            k.moe_w1 = sb("moe_w1", [P, NE, CB, FF])
            k.moe_w2 = sb("moe_w2", [P, NE, FB, C])
            k.moe_loaded = ctx.enter_context(nc.semaphore("moe_loaded"))
            with nc.Block() as block:
                @block.sync
                def _(sp):
                    sp.dma_start(k.moe_w1[:], d["moe_W1"].rearrange("e (k p) f -> p (e k) f", p=P)
                                 ).then_inc(k.moe_loaded, 16)
                    sp.dma_start(k.moe_w2[:], d["moe_W2"].rearrange("e (k p) f -> p (e k) f", p=P)
                                 ).then_inc(k.moe_loaded, 16)
            with cleared(nc):
                route_phase(nc, k, d)
            with cleared(nc):
                expert_phase(nc, k, d, out.rearrange("n p c -> (n p) c"))
            return
        stored = ctx.enter_context(nc.semaphore("x_stored"))
        with nc.Block() as block:
            @block.sync
            def _(sp):
                sp.dma_start(out.rearrange("n p c -> p n c"), k.x[:]).then_inc(stored, 16)
                sp.wait_ge(stored, 16)


def lay_out(inp):
    import numpy as np
    f = lambda n: np.asarray(inp[n])
    B = f("L0_c").shape[0]
    columns = lambda v: np.asarray(v).reshape(-1, P).T
    A, R, E = "L0_attn_", "L0_ffn_", "L1_ffn_"
    cols = {"b_ret": f(A + "b_ret"), "ln1_scale": f(A + "ln1_scale"), "ln1_bias": f(A + "ln1_bias"), "b1": f(A + "b1"),
            "mu_r": f(R + "mu_r"), "mu_k": f(R + "mu_k"), "bq": f(E + "bq"), "bk": f(E + "bk"),
            "l1_ln1_g": f(E + "ln1_g"), "l1_ln1_b": f(E + "ln1_b"),
            "router_b": np.broadcast_to(f(E + "router_b"), (P,))}
    rows = {"ln1_scale": f(A + "ln1_scale"), "ln1_bias": f(A + "ln1_bias"), "b2": f(A + "b2"),
            "ln2_scale": f(A + "ln2_scale"), "ln2_bias": f(A + "ln2_bias"), "bv": f(E + "bv"), "bo": f(E + "bo"),
            "l1_ln1_g": f(E + "ln1_g"), "l1_ln1_b": f(E + "ln1_b"), "router_w": f(E + "router_w")[:, 0],
            "l1_ln2_g": f(E + "ln2_g"), "l1_ln2_b": f(E + "ln2_b")}
    angle = np.arange(T, dtype=np.float32)[:, None] / np.power(
        np.float32(10000.0), np.arange(0, HD, 2, dtype=np.float32)[None, :] / np.float32(HD))
    angle = angle.astype(np.float32).reshape(J, P, HD // 2).transpose(1, 0, 2)
    cos = np.concatenate([np.cos(angle), np.cos(angle)], axis=2)
    sin = np.concatenate([-np.sin(angle), np.sin(angle)], axis=2)
    arrays = {
        "x": f("L0_attn_x").reshape(B * J, P, C),
        "cT0": f("L0_c").T, "cT1": f("L1_c").T, "wmod0": f("L0_wmod"), "wmod1": f("L1_wmod"),
        "cols": np.concatenate([columns(cols[n]) for n in COLS], axis=1),
        "rows": np.stack([rows[n] for n in ROWS]),
        "mask": np.triu(np.full((P, P), -1e9, np.float32), 1),
        "w_out": f("L1_attn_w_out"), "Wq": f(E + "Wq"), "Wk": f(E + "Wk"), "Wv": f(E + "Wv"), "Wo": f(E + "Wo"),
        "moe_W1": f(E + "W1"), "moe_W2": f(E + "W2"), "moe_b1_rows": f(E + "b1"), "moe_b2_rows": f(E + "b2"),
        "before": np.triu(np.ones((P, P), np.float32), 1),
        "experts": np.broadcast_to(np.arange(NE, dtype=np.float32), (P, NE)),
        "ids": np.arange(B * T, dtype=np.int32).reshape(B * J, P).T,
        "lane": np.arange(P, dtype=np.float32)[:, None],
        "pad_ids": (B * T + np.arange(P, dtype=np.int32))[:, None],
        "number": np.arange(B * J + NE, dtype=np.float32)[None, :],
        "ident": np.eye(P, dtype=np.float32),
        "W_rT": f(R + "W_r").T, "W_kT": f(R + "W_k").T, "W_vT": f(R + "W_v").T,
        "w_qkv": f("L1_attn_w_qkv"), "cos": cos, "sin": sin,
        "W_ret": f(A + "W_ret"), "W1": f(A + "W1"), "W2": f(A + "W2"),
    }
    return {n: np.ascontiguousarray(a) for n, a in arrays.items()}


def kernel(**inputs):
    import numpy as np
    import concourse.bacc as bacc
    from concourse.bass_utils import run_bass_kernel_spmd

    arrays = lay_out(inputs)
    B = arrays["cT0"].shape[1]
    nc = bacc.Bacc("TRN2", target_bir_lowering=False, num_devices=1)
    d = {n: nc.dram_tensor(f"in_{n}", a.shape, mybir.dt.from_np(a.dtype), kind="ExternalInput").ap()
         for n, a in arrays.items()}
    out = nc.dram_tensor("out", (B * J, P, C), F32, kind="ExternalOutput").ap()
    build(nc, d, out, B)
    result = run_bass_kernel_spmd(nc, [{f"in_{n}": a for n, a in arrays.items()}], core_ids=[0])
    return result.results[0]["out"].reshape(B, T, C)
```

```python
import concourse.bass as bass
from concourse import mybir
from concourse.alu_op_type import AluOpType as ALU
from contextlib import ExitStack

F32 = mybir.dt.float32
BF16 = mybir.dt.bfloat16
ACT = mybir.ActivationFunctionType
AX = mybir.AxisListType

P = 128
C = 256
CB = C // P
T = 512
J = T // P
FF = 1024
FB = FF // P
NE = 4
NH = 16
HD = C // NH
EPS = 1e-5
KS = 3 * 2 * HD
RING = 4
G4 = 4

COLS = {}
for _name, _n in (("b_ret", 2), ("ln1_scale", 2), ("ln1_bias", 2), ("b1", 8), ("mu_r", 2), ("mu_k", 2),
                  ("bq", 2), ("bk", 2), ("l1_ln1_g", 2), ("l1_ln1_b", 2), ("router_b", 1)):
    COLS[_name] = sum(n for _, n in COLS.values()) if COLS else 0
    COLS[_name] = (COLS[_name], _n)
NCOLS = sum(n for _, n in COLS.values())
ROWS = ("ln1_scale", "ln1_bias", "b2", "ln2_scale", "ln2_bias",
        "bv", "bo", "l1_ln1_g", "l1_ln1_b", "router_w", "l1_ln2_g", "l1_ln2_b")
SA, CA, GA, SB, CBM, GB = range(6)
MROWS = ((0, GA), (0, GB), (1, GA), (1, GB), (1, CBM), (1, SB))


class Core:
    pass


def col(k, name, i=0):
    first, _ = COLS[name]
    return k.cols[:, first + i:first + i + 1]


def over_tiles(ap):
    return ap.unsqueeze(1).to_broadcast([P, J, C])


def setup_phase(nc, k, d):
    with ExitStack() as ctx:
        sb = lambda n, s, t=F32: ctx.enter_context(nc.sbuf_tensor("set_" + n, s, t))
        sem = lambda n: nc.alloc_semaphore("set_" + n)
        B = k.B
        wmod = [sb(f"wmod{l}", [P, CB, 6 * C]) for l in range(2)]
        cT = sb("cT", [P, 2, CB, B])
        sg = sb("sg", [P, 2, CB, B])
        rowmod = sb("rowmod", [B, len(MROWS), C])
        mask = sb("mask", [P, P])
        t_sign = sb("t_sign", [B, C])
        t_abs = sb("t_abs", [B, C])
        colps = [ctx.enter_context(nc.psum_tensor(f"colps{l}", [P, 12, B], F32)) for l in range(2)]
        rowps = [ctx.enter_context(nc.psum_tensor(f"rowps{i}", [B, C], F32)) for i in range(len(MROWS))]
        loaded, c_loaded, sig_done, silu_done = sem("loaded"), sem("c_loaded"), sem("sig_done"), sem("silu_done")
        colmod_ready, rowmod_ready = sem("colmod_ready"), sem("rowmod_ready")
        cols_done, step, rows_done, stored = sem("cols_done"), sem("step"), sem("rows_done"), sem("stored")
        block = ctx.enter_context(nc.Block())

        @block.sync
        def _(sp):
            for l in range(2):
                sp.dma_start(cT[:, l], d[f"cT{l}"].rearrange("(k p) b -> p k b", p=P)).then_inc(c_loaded, 16)
            for l in range(2):
                sp.dma_start(wmod[l][:], d[f"wmod{l}"].rearrange("(k p) n -> p k n", p=P)).then_inc(loaded, 16)
            sp.dma_start(k.cols[:], d["cols"]).then_inc(loaded, 16)
            sp.dma_start(k.ident[:], d["ident"]).then_inc(loaded, 16)
            sp.dma_start(mask[:], d["mask"]).then_inc(loaded, 16)
            sp.wait_ge(rows_done, 1)
            sp.dma_start(k.mrows_dram.rearrange("r b c -> b r c"), rowmod[:]).then_inc(stored, 16)
            sp.wait_ge(stored, 16)
            sp.wait_ge(loaded, 80)

        @block.scalar
        def _(act):
            act.wait_ge(c_loaded, 32)
            nc.scalar.activation(sg[:], cT[:], ACT.Sigmoid).then_inc(sig_done, 1)

        @block.tensor
        def _(pe):
            pe.wait_ge(loaded, 80)
            pe.wait_ge(silu_done, 1)
            for l in range(2):
                for m in range(12):
                    for kb in range(CB):
                        last = nc.tensor.matmul(colps[l][:, m, :], wmod[l][:, kb, m * P:(m + 1) * P], sg[:, l, kb, :],
                                                start=(kb == 0), stop=(kb == CB - 1))
            last.then_inc(colmod_ready, 1)
            for i, (l, part) in enumerate(MROWS):
                for kb in range(CB):
                    last = nc.tensor.matmul(rowps[i][:], sg[:, l, kb, :], wmod[l][:, kb, part * C:(part + 1) * C],
                                            start=(kb == 0), stop=(kb == CB - 1))
            last.then_inc(rowmod_ready, 1)

        @block.vector
        def _(dve):
            dve.wait_ge(loaded, 80)
            dve.wait_ge(sig_done, 1)
            nc.vector.tensor_tensor(sg[:], sg[:], cT[:], ALU.mult).then_inc(silu_done, 1)
            dve.wait_ge(colmod_ready, 1)
            for l in range(2):
                for m in range(12):
                    plus = 1.0 if m // 2 in (CA, CBM) else 0.0
                    nc.vector.tensor_scalar(k.mod[:, l, m, :], colps[l][:, m, :], plus, None, ALU.add)
            nc.vector.tensor_copy(k.ident_bf[:], k.ident[:])
            nc.vector.tensor_copy(k.mask_bf[:], mask[:])
            nc.vector.memset(k.half[:], 0.5).then_inc(cols_done, 1)
            dve.wait_ge(rowmod_ready, 1)
            steps = [0]

            def follow(instruction):
                steps[0] += 1
                instruction.then_inc(step, 1)
                dve.wait_ge(step, steps[0])

            for i, (l, part) in enumerate(MROWS):
                if part in (GA, GB):
                    follow(nc.vector.tensor_scalar(t_sign[:], rowps[i][:], 0.0, 2.0, ALU.is_ge, ALU.mult))
                    follow(nc.vector.tensor_scalar(t_sign[:], t_sign[:], -1.0, None, ALU.add))
                    follow(nc.vector.tensor_tensor(t_abs[:], t_sign[:], rowps[i][:], ALU.mult))
                    follow(nc.vector.scalar_tensor_tensor(rowmod[:, i, :], t_abs[:], 0.25, t_sign[:],
                                                          ALU.max, ALU.mult))
                else:
                    nc.vector.tensor_scalar(rowmod[:, i, :], rowps[i][:], 1.0 if part == CBM else 0.0, None, ALU.add)
            nc.vector.tensor_copy(t_sign[:], t_abs[:]).then_inc(rows_done, 1)


class Norm:

    def __init__(self, nc, ctx, name):
        self.stats = ctx.enter_context(nc.sbuf_tensor(f"{name}_stats", [P, J, 6], F32))
        self.mv = ctx.enter_context(nc.sbuf_tensor(f"{name}_mv", [P, J, 2], F32))
        self.pause = ctx.enter_context(nc.sbuf_tensor(f"{name}_pause", [P, 1], F32))
        self.ve = ctx.enter_context(nc.sbuf_tensor(f"{name}_ve", [P, J], F32))
        self.rstd = ctx.enter_context(nc.sbuf_tensor(f"{name}_rstd", [P, J], F32))
        self.stats_ready = nc.alloc_semaphore(f"{name}_stats_ready")
        self.mv_ready = nc.alloc_semaphore(f"{name}_mv_ready")
        self.ve_ready = nc.alloc_semaphore(f"{name}_ve_ready")
        self.rstd_ready = nc.alloc_semaphore(f"{name}_rstd_ready")

    def moments(self, nc, dve, tile, b):
        for j in range(J):
            last = nc.vector.bn_stats(self.stats[:, j, :], tile(j))
        last.then_inc(self.stats_ready, 1)
        dve.wait_ge(self.stats_ready, b + 1)
        nc.vector.memset(self.pause[:], 0.0)
        for j in range(J):
            last = nc.vector.bn_aggr(self.mv[:, j, :], self.stats[:, j, :])
        last.then_inc(self.mv_ready, 1)

    def rsqrt(self, nc, k, pool, b):
        pool.wait_ge(self.mv_ready, b + 1)
        nc.gpsimd.tensor_tensor(self.ve[:], self.mv[:, :, 1], k.eps[:], ALU.add).then_inc(self.ve_ready, 1)
        pool.wait_ge(self.ve_ready, b + 1)
        nc.gpsimd.tensor_tensor(self.rstd[:], self.ve[:], k.minus_half[:], ALU.pow).then_inc(self.rstd_ready, 1)

    def apply(self, nc, dve, out, tile, b):
        dve.wait_ge(self.rstd_ready, b + 1)
        for j in range(J):
            last = nc.vector.tensor_scalar(out[:, j, :], tile(j), self.mv[:, j, 0:1], self.rstd[:, j:j + 1],
                                           ALU.subtract, ALU.mult)
        return last


def to_channels(nc, k, out, z):
    for cb in range(CB):
        for j in range(J):
            last = nc.tensor.transpose(out[:, cb, j * P:(j + 1) * P], z[:, j, cb * P:(cb + 1) * P], k.ident[:])
    return last


def retention_phase(nc, k, d):
    with ExitStack() as ctx:
        sb = lambda n, s, t=F32: ctx.enter_context(nc.sbuf_tensor("ret_" + n, s, t))
        sem = lambda n: nc.alloc_semaphore("ret_" + n)
        B = k.B
        w_ret = sb("w_ret", [P, CB, C])
        w1 = sb("w1", [P, CB, FF])
        w2 = sb("w2", [P, FB, C])
        rowb = {n: sb(f"rowb_{n}", [P, C]) for n in ("ln1_scale", "ln1_bias", "b2", "ln2_scale", "ln2_bias")}
        hbias = sb("hbias", [P, C])
        gate = sb("gate", [P, C])
        gate_scale = sb("gate_scale", [P, C])
        gate_bias = sb("gate_bias", [P, C])
        half_b_ret = sb("half_b_ret", [P, CB])
        z0 = sb("z0", [P, J, C])
        hT = sb("hT", [P, CB, T])
        sT = sb("sT", [P, CB, T])
        tT = sb("tT", [P, CB, T])
        z1 = sb("z1", [P, J, C])
        h1T = sb("h1T", [P, CB, T])
        h1b = sb("h1b", [P, J, C])
        gT = sb("gT", [P, FB, T])
        t2 = sb("t2", [P, J, C])
        ln0, ln1, ln2 = (Norm(nc, ctx, "ret_" + n) for n in ("ln0", "ln1", "ln2"))
        ps = lambda n, s: ctx.enter_context(nc.psum_tensor("ret_" + n, s, F32))
        psA = ps("psA", [P, 2, T])
        psB = ps("psB", [P, 2, T])
        psF = ps("psF", [P, 2, T])
        psY = ps("psY", [P, J, C])
        weights, rows, x_loaded, gate_loaded = sem("weights"), sem("rows"), sem("x_loaded"), sem("gate_loaded")
        init, hbias_done = sem("init"), sem("hbias_done")
        z0_done, zT_done, hT_done, pre_done = sem("z0_done"), sem("zT_done"), sem("hT_done"), sem("pre_done")
        tanh_done, s_done, scan_done, tT_done = sem("tanh_done"), sem("s_done"), sem("scan_done"), sem("tT_done")
        tok_done, z1_done, z1T_done, h1T_done = sem("tok_done"), sem("z1_done"), sem("z1T_done"), sem("h1T_done")
        h1g_done, h1b_done, ffn1_done, gelu_done = sem("h1g_done"), sem("h1b_done"), sem("ffn1_done"), sem("gelu_done")
        y_done, t2_done, z2_done, gate_done = sem("y_done"), sem("t2_done"), sem("z2_done"), sem("gate_done")
        zg_done, out_done, x_done = sem("zg_done"), sem("out_done"), sem("x_done")
        block = ctx.enter_context(nc.Block())

        @block.sync
        def _(sp):
            for ap, src in ((w_ret, "W_ret"), (w1, "W1"), (w2, "W2")):
                sp.dma_start(ap[:], d[src].rearrange("(k p) n -> p k n", p=P)).then_inc(weights, 16)
            for n, ap in rowb.items():
                sp.dma_start(ap[:], d["rows"][ROWS.index(n)].partition_broadcast(P)).then_inc(rows, 16)
            with sp.Fori(0, B) as b:
                sp.wait_ge(x_loaded, 16 * b)
                sp.dma_start(k.x[:, bass.ds(b * J, J), :],
                             d["x"][bass.ds(b * J, J)].rearrange("j p c -> p j c")).then_inc(x_loaded, 16)
                sp.wait_ge(gate_done, b)
                sp.dma_start(gate[:], k.mrows_dram[0, b].partition_broadcast(P)).then_inc(gate_loaded, 16)

        @block.vector
        def _(dve):
            def norm0(b):
                dve.wait_ge(x_loaded, 16 * b + 16)
                tile = lambda j: k.x[:, b * J + j, :]
                ln0.moments(nc, dve, tile, b)
                dve.wait_ge(zT_done, b)
                ln0.apply(nc, dve, z0, tile, b).then_inc(z0_done, 1)

            def retention(b):
                dve.wait_ge(s_done, b + 1)
                dve.wait_ge(tok_done, b)
                for cb in range(CB):
                    last = nc.vector.tensor_tensor_scan(tT[:, cb, :], k.half[:], sT[:, cb, :], 0.0, ALU.mult, ALU.add)
                last.then_inc(scan_done, 1)
                dve.wait_ge(scan_done, b + 1)
                nc.vector.scalar_tensor_tensor(tT[:], tT[:], 0.5, hT[:], ALU.mult, ALU.add).then_inc(tT_done, 1)

            def norm1(b):
                dve.wait_ge(tok_done, b + 1)
                tile = lambda j: psA[:, j // 2, (j % 2) * C:(j % 2 + 1) * C]
                ln1.moments(nc, dve, tile, b)
                dve.wait_ge(z1T_done, b)
                dve.wait_ge(h1b_done, b)
                ln1.apply(nc, dve, z1, tile, b).then_inc(z1_done, 1)

            def norm2(b):
                dve.wait_ge(y_done, J * b + J)
                dve.wait_ge(h1b_done, b + 1)
                dve.wait_ge(x_done, b)
                nc.vector.tensor_tensor(t2[:], psY[:], h1b[:], ALU.add).then_inc(t2_done, 1)
                dve.wait_ge(t2_done, b + 1)
                tile = lambda j: t2[:, j, :]
                ln2.moments(nc, dve, tile, b)
                ln2.apply(nc, dve, t2, tile, b).then_inc(z2_done, 1)

            def residual(b):
                dve.wait_ge(out_done, b + 1)
                xb = k.x[:, bass.ds(b * J, J), :]
                nc.vector.tensor_tensor(xb, xb, t2[:], ALU.add).then_inc(x_done, 1)

            dve.wait_ge(rows, 16 * len(rowb))
            nc.vector.tensor_scalar(half_b_ret[:], k.cols[:, COLS["b_ret"][0]:COLS["b_ret"][0] + CB], 0.5, None,
                                    ALU.mult)
            nc.vector.tensor_tensor(hbias[:], rowb["ln1_bias"][:], rowb["b2"][:], ALU.add).then_inc(init, 1)
            norm0(0)
            retention(0)
            norm1(0)
            if True:
                with dve.Fori(0, B - 1) as b:
                    norm0(b + 1)
                    retention(b + 1)
                    norm1(b + 1)
                    norm2(b)
                    residual(b)
            norm2(B - 1)
            residual(B - 1)

        @block.gpsimd
        def _(pool):
            def add_bias(b):
                pool.wait_ge(z1_done, b + 1)
                pool.wait_ge(t2_done, b)
                nc.gpsimd.tensor_tensor(h1b[:], z1[:], over_tiles(rowb["ln1_scale"][:]), ALU.mult).then_inc(h1g_done, 1)
                pool.wait_ge(h1g_done, b + 1)
                nc.gpsimd.tensor_tensor(h1b[:], h1b[:], over_tiles(hbias[:]), ALU.add).then_inc(h1b_done, 1)

            def gates(b):
                pool.wait_ge(gate_loaded, 16 * b + 16)
                pool.wait_ge(out_done, b)
                nc.gpsimd.tensor_tensor(gate_scale[:], gate[:], rowb["ln2_scale"][:], ALU.mult)
                nc.gpsimd.tensor_tensor(gate_bias[:], gate[:], rowb["ln2_bias"][:], ALU.mult).then_inc(gate_done, 1)

            def scale_out(b):
                pool.wait_ge(z2_done, b + 1)
                pool.wait_ge(gate_done, b + 1)
                nc.gpsimd.tensor_tensor(t2[:], t2[:], over_tiles(gate_scale[:]), ALU.mult).then_inc(zg_done, 1)
                pool.wait_ge(zg_done, b + 1)
                nc.gpsimd.tensor_tensor(t2[:], t2[:], over_tiles(gate_bias[:]), ALU.add).then_inc(out_done, 1)

            pool.wait_ge(init, 1)
            ln0.rsqrt(nc, k, pool, 0)
            ln1.rsqrt(nc, k, pool, 0)
            add_bias(0)
            if True:
                with pool.Fori(0, B - 1) as b:
                    gates(b)
                    ln0.rsqrt(nc, k, pool, b + 1)
                    ln1.rsqrt(nc, k, pool, b + 1)
                    ln2.rsqrt(nc, k, pool, b)
                    scale_out(b)
                    add_bias(b + 1)
            gates(B - 1)
            ln2.rsqrt(nc, k, pool, B - 1)
            scale_out(B - 1)

        @block.tensor
        def _(pe):
            def transpose_h(b):
                pe.wait_ge(z0_done, b + 1)
                pe.wait_ge(z1_done, b)
                to_channels(nc, k, psA, z0).then_inc(zT_done, 1)

            def retention_product(b):
                pe.wait_ge(hT_done, b + 1)
                pe.wait_ge(h1T_done, b)
                for db in range(CB):
                    for cb in range(CB):
                        last = nc.tensor.matmul(psB[:, db, :], w_ret[:, cb, db * P:(db + 1) * P], hT[:, cb, :],
                                                start=(cb == 0), stop=(cb == CB - 1))
                last.then_inc(pre_done, 1)

            def transpose_back(b):
                pe.wait_ge(tT_done, b + 1)
                for j in range(J):
                    for cb in range(CB):
                        last = nc.tensor.transpose(psA[:, j // 2, (j % 2) * C + cb * P:(j % 2) * C + (cb + 1) * P],
                                                   tT[:, cb, j * P:(j + 1) * P], k.ident[:])
                last.then_inc(tok_done, 1)

            def transpose_h1(b):
                pe.wait_ge(z1_done, b + 1)
                pe.wait_ge(tanh_done, b + 1)
                to_channels(nc, k, psB, z1).then_inc(z1T_done, 1)

            def hidden(b, blocks):
                for f in blocks:
                    if f == 0:
                        pe.wait_ge(h1T_done, b + 1)
                    pe.wait_ge(gelu_done, FB * b + max(f - 1, 0))
                    for cb in range(CB):
                        last = nc.tensor.matmul(psF[:, f % 2, :], w1[:, cb, f * P:(f + 1) * P], h1T[:, cb, :],
                                                start=(cb == 0), stop=(cb == CB - 1))
                    last.then_inc(ffn1_done, 1)

            def output(b, tiles):
                for j in tiles:
                    if j == 0:
                        pe.wait_ge(gelu_done, FB * b + FB)
                        pe.wait_ge(t2_done, b)
                    for f in range(FB):
                        last = nc.tensor.matmul(psY[:, j, :], gT[:, f, j * P:(j + 1) * P], w2[:, f, :],
                                                start=(f == 0), stop=(f == FB - 1))
                    last.then_inc(y_done, 1)

            pe.wait_ge(weights, 48)
            transpose_h(0)
            retention_product(0)
            transpose_back(0)
            transpose_h1(0)
            if True:
                with pe.Fori(0, B - 1) as b:
                    hidden(b, range(0, 5))
                    transpose_h(b + 1)
                    hidden(b, range(5, 6))
                    retention_product(b + 1)
                    hidden(b, range(6, 8))
                    output(b, range(0, 1))
                    transpose_back(b + 1)
                    output(b, range(1, 3))
                    transpose_h1(b + 1)
                    output(b, range(3, 4))
            hidden(B - 1, range(FB))
            output(B - 1, range(J))

        @block.scalar
        def _(act):
            def modulate(b):
                act.wait_ge(zT_done, b + 1)
                act.wait_ge(tT_done, b)
                for cb in range(CB):
                    last = nc.scalar.activation(hT[:, cb, :], psA[:, cb, :], ACT.Identity,
                                                scale=k.mod[:, 0, CA * CB + cb, bass.ds(b, 1)],
                                                bias=k.mod[:, 0, SA * CB + cb, bass.ds(b, 1)])
                last.then_inc(hT_done, 1)

            def sigmoid(b):
                act.wait_ge(pre_done, b + 1)
                for cb in range(CB):
                    last = nc.scalar.activation(sT[:, cb, :], psB[:, cb, :], ACT.Tanh, scale=0.5,
                                                bias=half_b_ret[:, cb:cb + 1])
                last.then_inc(tanh_done, 1)
                act.wait_ge(tanh_done, b + 1)
                nc.scalar.activation(sT[:], sT[:], ACT.Copy, scale=0.5, bias=0.5).then_inc(s_done, 1)

            def scale_h1(b):
                act.wait_ge(z1T_done, b + 1)
                act.wait_ge(ffn1_done, FB * b)
                for cb in range(CB):
                    last = nc.scalar.activation(h1T[:, cb, :], psB[:, cb, :], ACT.Identity,
                                                scale=col(k, "ln1_scale", cb), bias=col(k, "ln1_bias", cb))
                last.then_inc(h1T_done, 1)

            def gelu(b, blocks):
                for f in blocks:
                    if f == 0:
                        act.wait_ge(y_done, J * b)
                    act.wait_ge(ffn1_done, FB * b + f + 1)
                    nc.scalar.activation(gT[:, f, :], psF[:, f % 2, :], ACT.Gelu_apprx_tanh,
                                         bias=col(k, "b1", f)).then_inc(gelu_done, 1)

            act.wait_ge(init, 1)
            modulate(0)
            sigmoid(0)
            scale_h1(0)
            if True:
                with act.Fori(0, B - 1) as b:
                    gelu(b, range(0, 5))
                    modulate(b + 1)
                    gelu(b, range(5, 6))
                    sigmoid(b + 1)
                    gelu(b, range(6, 8))
                    scale_h1(b + 1)
            gelu(B - 1, range(FB))


def channel_mix_phase(nc, k, d):
    with ExitStack() as ctx:
        sb = lambda n, s, t=F32: ctx.enter_context(nc.sbuf_tensor("mix_" + n, s, t))
        sem = lambda n: nc.alloc_semaphore("mix_" + n)
        ps = lambda n, s: ctx.enter_context(nc.psum_tensor("mix_" + n, s, F32))
        B = k.B
        wr, wk, wv = sb("wr", [P, CB, C]), sb("wk", [P, CB, C]), sb("wv", [P, CB, C])
        gate = sb("gate", [P, C])
        z = sb("z", [P, J, C])
        hT = sb("hT", [P, CB, 1 + T])
        dT = sb("dT", [P, CB, T])
        xkT, xrT = sb("xkT", [P, CB, T]), sb("xrT", [P, CB, T])
        kT = sb("kT", [P, CB, T])
        r = sb("r", [P, J, C])
        o = sb("o", [P, J, C])
        ln = Norm(nc, ctx, "mix_ln")
        psA, psK = ps("psA", [P, CB, T]), ps("psK", [P, CB, T])
        psR, psV = ps("psR", [P, J, C]), ps("psV", [P, J, C])
        weights, gate_loaded, zero_done = sem("weights"), sem("gate_loaded"), sem("zero_done")
        z_done, zT_done, hT_done, d_done = sem("z_done"), sem("zT_done"), sem("hT_done"), sem("d_done")
        xk_done, xr_done, k_done, relu_done = sem("xk_done"), sem("xr_done"), sem("k_done"), sem("relu_done")
        sq_done, r_done, sig_done, rg_done = sem("sq_done"), sem("r_done"), sem("sig_done"), sem("rg_done")
        v_done, o_done, x_done = sem("v_done"), sem("o_done"), sem("x_done")
        block = ctx.enter_context(nc.Block())

        @block.sync
        def _(sp):
            for ap, src in ((wr, "W_rT"), (wk, "W_kT"), (wv, "W_vT")):
                sp.dma_start(ap[:], d[src].rearrange("(k p) n -> p k n", p=P)).then_inc(weights, 16)
            with sp.Fori(0, B) as b:
                sp.wait_ge(rg_done, b)
                sp.dma_start(gate[:], k.mrows_dram[1, b].partition_broadcast(P)).then_inc(gate_loaded, 16)

        @block.vector
        def _(dve):
            def norm(b):
                tile = lambda j: k.x[:, b * J + j, :]
                ln.moments(nc, dve, tile, b)
                dve.wait_ge(zT_done, b)
                ln.apply(nc, dve, z, tile, b).then_inc(z_done, 1)

            def mix(b):
                dve.wait_ge(hT_done, b + 1)
                now, before = hT[:, :, 1:1 + T], hT[:, :, 0:T]
                nc.vector.tensor_tensor(dT[:], now, before, ALU.subtract).then_inc(d_done, 1)
                dve.wait_ge(d_done, b + 1)
                dve.wait_ge(k_done, b)
                for cb in range(CB):
                    last = nc.vector.scalar_tensor_tensor(xkT[:, cb, :], dT[:, cb, :], col(k, "mu_k", cb),
                                                          hT[:, cb, 0:T], ALU.mult, ALU.add)
                last.then_inc(xk_done, 1)
                dve.wait_ge(r_done, b)
                for cb in range(CB):
                    last = nc.vector.scalar_tensor_tensor(xrT[:, cb, :], dT[:, cb, :], col(k, "mu_r", cb),
                                                          hT[:, cb, 0:T], ALU.mult, ALU.add)
                last.then_inc(xr_done, 1)

            def output(b):
                dve.wait_ge(v_done, b + 1)
                dve.wait_ge(rg_done, b + 1)
                dve.wait_ge(x_done, b)
                nc.vector.tensor_tensor(o[:], psV[:], r[:], ALU.mult).then_inc(o_done, 1)
                dve.wait_ge(o_done, b + 1)
                xb = k.x[:, bass.ds(b * J, J), :]
                nc.vector.tensor_tensor(xb, xb, o[:], ALU.add).then_inc(x_done, 1)

            nc.vector.memset(hT[:, :, 0:1], 0.0).then_inc(zero_done, 1)
            dve.wait_ge(zero_done, 1)
            norm(0)
            mix(0)
            if True:
                with dve.Fori(0, B - 1) as b:
                    norm(b + 1)
                    mix(b + 1)
                    output(b)
            output(B - 1)

        @block.gpsimd
        def _(pool):
            def gate_r(b):
                pool.wait_ge(sig_done, b + 1)
                pool.wait_ge(gate_loaded, 16 * b + 16)
                nc.gpsimd.tensor_tensor(r[:], r[:], over_tiles(gate[:]), ALU.mult).then_inc(rg_done, 1)

            ln.rsqrt(nc, k, pool, 0)
            if True:
                with pool.Fori(0, B - 1) as b:
                    ln.rsqrt(nc, k, pool, b + 1)
                    gate_r(b)
            gate_r(B - 1)

        @block.tensor
        def _(pe):
            def transpose_h(b):
                pe.wait_ge(z_done, b + 1)
                pe.wait_ge(hT_done, b)
                to_channels(nc, k, psA, z).then_inc(zT_done, 1)

            def key(b):
                pe.wait_ge(xk_done, b + 1)
                pe.wait_ge(relu_done, b)
                for db in range(CB):
                    for cb in range(CB):
                        last = nc.tensor.matmul(psK[:, db, :], wk[:, cb, db * P:(db + 1) * P], xkT[:, cb, :],
                                                start=(cb == 0), stop=(cb == CB - 1))
                last.then_inc(k_done, 1)

            def by_tokens(out, xT, w):
                for j in range(J):
                    for cb in range(CB):
                        last = nc.tensor.matmul(out[:, j, :], xT[:, cb, j * P:(j + 1) * P], w[:, cb, :],
                                                start=(cb == 0), stop=(cb == CB - 1))
                return last

            def receptance(b):
                pe.wait_ge(xr_done, b + 1)
                pe.wait_ge(sig_done, b)
                by_tokens(psR, xrT, wr).then_inc(r_done, 1)

            def value(b):
                pe.wait_ge(sq_done, b + 1)
                pe.wait_ge(o_done, b)
                by_tokens(psV, kT, wv).then_inc(v_done, 1)

            pe.wait_ge(weights, 48)
            transpose_h(0)
            if True:
                with pe.Fori(0, B - 1) as b:
                    key(b)
                    transpose_h(b + 1)
                    receptance(b)
                    value(b)
            key(B - 1)
            receptance(B - 1)
            value(B - 1)

        @block.scalar
        def _(act):
            def modulate(b):
                act.wait_ge(zT_done, b + 1)
                act.wait_ge(xr_done, b)
                for cb in range(CB):
                    last = nc.scalar.activation(hT[:, cb, 1:1 + T], psA[:, cb, :], ACT.Identity,
                                                scale=k.mod[:, 0, CBM * CB + cb, bass.ds(b, 1)],
                                                bias=k.mod[:, 0, SB * CB + cb, bass.ds(b, 1)])
                last.then_inc(hT_done, 1)

            def activate(b):
                act.wait_ge(k_done, b + 1)
                act.wait_ge(v_done, b)
                nc.scalar.activation(kT[:], psK[:], ACT.Relu).then_inc(relu_done, 1)
                act.wait_ge(relu_done, b + 1)
                nc.scalar.activation(kT[:], kT[:], ACT.Square).then_inc(sq_done, 1)
                act.wait_ge(r_done, b + 1)
                act.wait_ge(o_done, b)
                nc.scalar.activation(r[:], psR[:], ACT.Sigmoid).then_inc(sig_done, 1)

            act.wait_ge(zero_done, 1)
            modulate(0)
            if True:
                with act.Fori(0, B - 1) as b:
                    modulate(b + 1)
                    activate(b)
            activate(B - 1)


def rotary_qkv_phase(nc, k, d):
    with ExitStack() as ctx:
        sb = lambda n, s, t=F32: ctx.enter_context(nc.sbuf_tensor("rot_" + n, s, t))
        sem = lambda n: nc.alloc_semaphore("rot_" + n)
        ps = lambda n, s: ctx.enter_context(nc.psum_tensor("rot_" + n, s, F32))
        B = k.B
        w = sb("w_qkv", [P, CB, 3 * C])
        cos, sin = sb("cos", [P, J, HD]), sb("sin", [P, J, HD])
        z = sb("z", [P, J, C])
        hT = sb("hT", [P, CB, T])
        by_cos, by_sin = sb("by_cos", [P, 2, 2 * C]), sb("by_sin", [P, 2, 2 * C])
        rot = sb("rot", [P, J, 2 * C])
        rest = sb("rest", [P, 2, T])
        parts = sb("parts", [P, 3, 2 * CB, T], BF16)
        v = sb("v", [P, J, C])
        ln = Norm(nc, ctx, "rot_ln")
        psA = ps("psA", [P, CB, T])
        psQK = ps("psQK", [P, 2, 2 * C])
        psV = ps("psV", [P, 2, T])[:, :, 0:C]
        psT = ps("psT", [P, 2, T])
        weights, z_done, zT_done, hT_done = sem("weights"), sem("z_done"), sem("zT_done"), sem("hT_done")
        qk_done, v_done, prod_done, rot_done = sem("qk_done"), sem("v_done"), sem("prod_done"), sem("rot_done")
        vcopy_done, rT_done, hi_done = sem("vcopy_done"), sem("rT_done"), sem("hi_done")
        rest_done, mid_done, lo_done = sem("rest_done"), sem("mid_done"), sem("lo_done")
        parts_stored, v_stored = sem("parts_stored"), sem("v_stored")
        block = ctx.enter_context(nc.Block())
        NB = 2 * CB

        @block.sync
        def _(sp):
            sp.dma_start(w[:], d["w_qkv"].rearrange("(k p) n -> p k n", p=P)).then_inc(weights, 16)
            sp.dma_start(cos[:], d["cos"]).then_inc(weights, 16)
            sp.dma_start(sin[:], d["sin"]).then_inc(weights, 16)
            with sp.Fori(0, B) as b:
                sp.wait_ge(v_stored, 16 * b)
                sp.wait_ge(vcopy_done, J * b + J)
                sp.dma_start(k.v_dram[b], v[:]).then_inc(v_stored, 16)
                sp.wait_ge(parts_stored, 16 * b)
                sp.wait_ge(hi_done, NB * b + NB)
                sp.wait_ge(mid_done, NB * b + NB)
                sp.wait_ge(lo_done, NB * b + NB)
                sp.dma_start(k.parts_dram[b].rearrange("s n p t -> p s n t"), parts[:]).then_inc(parts_stored, 16)
            sp.wait_ge(v_stored, 16 * B)
            sp.wait_ge(parts_stored, 16 * B)

        @block.vector
        def _(dve):
            def norm(b):
                tile = lambda j: k.x[:, b * J + j, :]
                ln.moments(nc, dve, tile, b)
                dve.wait_ge(zT_done, b)
                ln.apply(nc, dve, z, tile, b).then_inc(z_done, 1)

            def rotate(b):
                for j in range(J):
                    i = j % 2
                    dve.wait_ge(qk_done, J * b + j + 1)
                    dve.wait_ge(rot_done, J * b + max(j - 1, 0))
                    heads = psQK[:, i, :].rearrange("p (h e) -> p h e", e=HD)
                    nc.vector.tensor_tensor(by_cos[:, i, :].rearrange("p (h e) -> p h e", e=HD), heads,
                                            cos[:, j, :].unsqueeze(1).to_broadcast([P, 2 * NH, HD]), ALU.mult)
                    out = by_sin[:, i, :].rearrange("p (h e) -> p h e", e=HD)
                    H2 = HD // 2
                    for half in range(2):
                        own, other = slice(half * H2, half * H2 + H2), slice(H2 - half * H2, HD - half * H2)
                        last = nc.vector.tensor_tensor(out[:, :, own], heads[:, :, other],
                                                       sin[:, j, own].unsqueeze(1).to_broadcast([P, 2 * NH, H2]),
                                                       ALU.mult)
                    last.then_inc(prod_done, 1)

            def split(b):
                for n in range(NB):
                    dve.wait_ge(hi_done, NB * b + n + 1)
                    dve.wait_ge(lo_done, NB * b + max(n - 1, 0))
                    nc.vector.tensor_tensor(rest[:, n % 2, :], psT[:, n % 2, :], parts[:, 0, n, :],
                                            ALU.subtract).then_inc(rest_done, 1)

            norm(0)
            with dve.Fori(0, B - 1) as b:
                rotate(b)
                norm(b + 1)
                split(b)
            rotate(B - 1)
            split(B - 1)

        @block.gpsimd
        def _(pool):
            def add_rotated(b):
                for j in range(J):
                    pool.wait_ge(prod_done, J * b + j + 1)
                    if j == 0:
                        pool.wait_ge(rT_done, NB * b)
                    nc.gpsimd.tensor_tensor(rot[:, j, :], by_cos[:, j % 2, :], by_sin[:, j % 2, :],
                                            ALU.add).then_inc(rot_done, 1)

            def low_parts(b):
                for n in range(NB):
                    pool.wait_ge(mid_done, NB * b + n + 1)
                    nc.gpsimd.tensor_tensor(parts[:, 2, n, :], rest[:, n % 2, :], parts[:, 1, n, :],
                                            ALU.subtract).then_inc(lo_done, 1)

            ln.rsqrt(nc, k, pool, 0)
            with pool.Fori(0, B - 1) as b:
                add_rotated(b)
                ln.rsqrt(nc, k, pool, b + 1)
                low_parts(b)
            add_rotated(B - 1)
            low_parts(B - 1)

        @block.tensor
        def _(pe):
            def transpose_h(b):
                pe.wait_ge(z_done, b + 1)
                pe.wait_ge(hT_done, b)
                to_channels(nc, k, psA, z).then_inc(zT_done, 1)

            def project(b):
                pe.wait_ge(hT_done, b + 1)
                for j in range(J):
                    tok = slice(j * P, (j + 1) * P)
                    pe.wait_ge(prod_done, J * b + max(j - 1, 0))
                    for cb in range(CB):
                        last = nc.tensor.matmul(psQK[:, j % 2, :], hT[:, cb, tok], w[:, cb, 0:2 * C],
                                                start=(cb == 0), stop=(cb == CB - 1))
                    last.then_inc(qk_done, 1)
                    pe.wait_ge(vcopy_done, J * b + max(j - 1, 0))
                    for cb in range(CB):
                        last = nc.tensor.matmul(psV[:, j % 2, :], hT[:, cb, tok], w[:, cb, 2 * C:3 * C],
                                                start=(cb == 0), stop=(cb == CB - 1))
                    last.then_inc(v_done, 1)

            def transpose_rotated(b):
                pe.wait_ge(rot_done, J * b + J)
                for n in range(NB):
                    pe.wait_ge(rest_done, NB * b + max(n - 1, 0))
                    for j in range(J):
                        last = nc.tensor.transpose(psT[:, n % 2, j * P:(j + 1) * P], rot[:, j, n * P:(n + 1) * P],
                                                   k.ident[:])
                    last.then_inc(rT_done, 1)

            pe.wait_ge(weights, 48)
            transpose_h(0)
            project(0)
            with pe.Fori(0, B - 1) as b:
                transpose_h(b + 1)
                transpose_rotated(b)
                project(b + 1)
            transpose_rotated(B - 1)

        @block.scalar
        def _(act):
            def modulate(b):
                act.wait_ge(zT_done, b + 1)
                act.wait_ge(v_done, J * b)
                for cb in range(CB):
                    last = nc.scalar.activation(hT[:, cb, :], psA[:, cb, :], ACT.Identity,
                                                scale=k.mod[:, 1, CA * CB + cb, bass.ds(b, 1)],
                                                bias=k.mod[:, 1, SA * CB + cb, bass.ds(b, 1)])
                last.then_inc(hT_done, 1)

            def copy_v(b):
                act.wait_ge(v_stored, 16 * b)
                for j in range(J):
                    act.wait_ge(v_done, J * b + j + 1)
                    nc.scalar.activation(v[:, j, :], psV[:, j % 2, :], ACT.Copy).then_inc(vcopy_done, 1)

            def split(b):
                act.wait_ge(parts_stored, 16 * b)
                for n in range(NB):
                    act.wait_ge(rT_done, NB * b + n + 1)
                    nc.scalar.activation(parts[:, 0, n, :], psT[:, n % 2, :], ACT.Copy).then_inc(hi_done, 1)
                    act.wait_ge(rest_done, NB * b + n + 1)
                    nc.scalar.activation(parts[:, 1, n, :], rest[:, n % 2, :], ACT.Copy).then_inc(mid_done, 1)

            modulate(0)
            copy_v(0)
            with act.Fori(0, B - 1) as b:
                modulate(b + 1)
                split(b)
                copy_v(b + 1)
            split(B - 1)


def attention_phase(nc, k, tag, causal):
    with ExitStack() as ctx:
        sb = lambda n, s, t=F32: ctx.enter_context(nc.sbuf_tensor(f"{tag}_{n}", s, t))
        sem = lambda n: nc.alloc_semaphore(f"{tag}_{n}")
        ps = lambda n, s: ctx.enter_context(nc.psum_tensor(f"{tag}_{n}", s, F32))
        B = k.B
        half_B = B // 2
        U = NH // G4 * J
        GR = NH // G4
        Q_PARTS, K_PARTS = (0, 0, 1, 0, 2, 1), (0, 1, 0, 2, 0, 1)
        LOADS = len(Q_PARTS) + len(K_PARTS)
        KX = KS + 2
        VW = 2 * HD
        qs = [sb(f"qs{i}", [P, NH, T], BF16) for i in range(2)]
        ks = [sb(f"ks{i}", [P, NH, T], BF16) for i in range(2)]
        vd = [sb(f"vd{i}", [P, J, C]) for i in range(2)]
        vp = [sb(f"vp{i}", [P, J, NH, VW]) for i in range(2)]
        pT = sb("pT", [P, 2, G4, T])
        mx = sb("mx", [P, J, NH])
        mrow = sb("mrow", [NH, 2, T], BF16)
        o_sb = sb("o_sb", [P, T])
        rec = sb("rec", [P, J, G4])
        att = sb("att", [P, J, C])
        one, pause = sb("one", [P, 1]), sb("pause", [P, 1])
        psS = ps("psS", [P, 2, T])
        psT = ps("psT", [P, 2, 2, T])
        psO = ps("psO", [P, T])
        psM = ps("psM", [P, T])
        stack_loaded = [[sem(f"stack_loaded{i}_{g}") for g in range(GR)] for i in range(2)]
        v_loaded = [sem(f"v_loaded{i}") for i in range(2)]
        m_loaded = [sem(f"m_loaded{i}") for i in range(2)]
        ones_done, k_ones, v_exp = sem("ones_done"), sem("k_ones"), sem("v_exp")
        s_done, max_done, mT_done, mhi_done, mrow_done = (sem("s_done"), sem("max_done"), sem("mT_done"),
                                                          sem("mhi_done"), sem("mrow_done"))
        st_done, exp_done, sel_done, pv_done = sem("st_done"), sem("exp_done"), sem("sel_done"), sem("pv_done")
        evac_done, oT_done, rec_done, att_done = sem("evac_done"), sem("oT_done"), sem("rec_done"), sem("att_done")
        att_stored = sem("att_stored")
        block = ctx.enter_context(nc.Block())

        heads_of = lambda u: [u] if u < U - 2 else ([u, u + 1] if u == U - 2 else [])
        first_q = lambda kt: kt * P if causal else 0
        seen = lambda qt: (qt + 1) * P if causal else T

        @block.sync
        def _(sp):
            def load_group(b, p, g):
                for dst, qk, which in ((qs[p], 0, Q_PARTS), (ks[p], 1, K_PARTS)):
                    for n, part in enumerate(which):
                        src = k.parts_dram[b, part, qk * CB:(qk + 1) * CB].rearrange("n p t -> (n p) t")
                        src = src[g * G4 * HD:(g + 1) * G4 * HD].rearrange("(h e) t -> e h t", e=HD)
                        sp.dma_start(dst[n * HD:(n + 1) * HD, g * G4:(g + 1) * G4, :], src
                                     ).then_inc(stack_loaded[p][g], 16)

            def load_v(b, p):
                sp.dma_start(vd[p][:], k.v_dram[b]).then_inc(v_loaded[p], 16)

            def load_maxima(b, p):
                sp.wait_ge(mrow_done, b + 1)
                for n in range(2):
                    sp.dma_start(qs[p][KS + n:KS + n + 1, :, :].rearrange("o h t -> o (h t)"), mrow[:, n, :]
                                 ).then_inc(m_loaded[p], 16)

            def store(b):
                sp.wait_ge(att_done, GR * b + GR)
                sp.dma_start(k.att_dram[b], att[:]).then_inc(att_stored, 16)

            def step(b, p, last_two=False, last=False):
                for g in range(GR):
                    if g == GR - 1 and not last:
                        load_maxima(b + 1, 1 - p)
                    if not last_two:
                        sp.wait_ge(pv_done, U * b + J * (g + 1))
                        load_group(b + 2, p, g)
                if not last_two:
                    sp.wait_ge(v_exp, b + 1)
                    load_v(b + 2, p)
                store(b)

            for p in range(2):
                for g in range(GR):
                    load_group(p, p, g)
                load_v(p, p)
            load_maxima(0, 0)
            if half_B > 1:
                with sp.Fori(0, half_B - 1) as i:
                    for p in range(2):
                        step(2 * i + p, p)
            step(B - 2, 0, last_two=True)
            step(B - 1, 1, last_two=True, last=True)
            sp.wait_ge(att_stored, 16 * B)

        @block.tensor
        def _(pe):
            def scores_by_queries(b, i, p, heads):
                for h in heads:
                    if h % G4 == 0:
                        pe.wait_ge(stack_loaded[p][h // G4], 16 * LOADS * (i + 1))
                    for qt in range(J):
                        n = J * h + qt
                        pe.wait_ge(max_done, J * NH * b + max(n - 1, 0))
                        out = psS[:, qt % 2, 0:seen(qt)]
                        last = nc.tensor.matmul(out, qs[p][0:KS, h, qt * P:(qt + 1) * P], ks[p][0:KS, h, 0:seen(qt)],
                                                start=True, stop=not causal)
                        if causal:
                            last = nc.tensor.matmul(psS[:, qt % 2, qt * P:(qt + 1) * P], k.ident_bf[:], k.mask_bf[:],
                                                    start=False, stop=True)
                        last.then_inc(s_done, 1)

            def transpose_maxima(b):
                pe.wait_ge(max_done, J * NH * (b + 1))
                for j in range(J):
                    last = nc.tensor.transpose(psM[0:NH, j * P:(j + 1) * P], mx[:, j, :], k.ident[:])
                last.then_inc(mT_done, 1)

            def scores_by_keys(b, p, u):
                g, kt = divmod(u, J)
                for pr in range(2):
                    pe.wait_ge(exp_done, 2 * U * b + max(2 * u + pr - 1, 0))
                    for n in range(2):
                        h = G4 * g + 2 * pr + n
                        last = nc.tensor.matmul(psT[:, pr, n, first_q(kt):T], ks[p][0:KX, h, kt * P:(kt + 1) * P],
                                                qs[p][0:KX, h, first_q(kt):T], start=True, stop=True)
                    last.then_inc(st_done, 1)

            def values(b, p, u):
                g, kt = divmod(u, J)
                if causal:
                    pe.wait_ge(sel_done, U * b + u + 1)
                else:
                    pe.wait_ge(exp_done, 2 * U * b + 2 * u + 2)
                if u == 0:
                    pe.wait_ge(v_exp, b + 1)
                if kt == 0:
                    pe.wait_ge(evac_done, GR * b + g)
                for n in range(G4):
                    last = nc.tensor.matmul(psO[VW * n:VW * (n + 1), first_q(kt):T], vp[p][:, kt, G4 * g + n, :],
                                            pT[:, u % 2, n, first_q(kt):T], start=(kt == 0), stop=(kt == J - 1))
                last.then_inc(pv_done, 1)

            def transpose_outputs(b, g):
                pe.wait_ge(evac_done, GR * b + g + 1)
                for j in range(J):
                    last = nc.tensor.transpose(psM[:, j * P:(j + 1) * P], o_sb[:, j * P:(j + 1) * P], k.ident[:])
                last.then_inc(oT_done, 1)

            def step(b, i, p, last=False):
                for u in range(U):
                    if u == 0:
                        pe.wait_ge(m_loaded[p], 32 * (i + 1))
                    scores_by_keys(b, p, u)
                    if not last:
                        scores_by_queries(b + 1, i + p, 1 - p, heads_of(u))
                    if u > 0:
                        values(b, p, u - 1)
                    if u % J == 2 and u > J:
                        if u == J + 2:
                            pe.wait_ge(mrow_done, b + 1)
                        pe.wait_ge(att_done, GR * b + u // J - 1)
                        transpose_outputs(b, u // J - 1)
                    if u == U - 1 and not last:
                        pe.wait_ge(att_done, GR * b + GR - 1)
                        transpose_maxima(b + 1)
                values(b, p, U - 1)
                if not last:
                    pe.wait_ge(mrow_done, b + 2)
                else:
                    pe.wait_ge(att_done, GR * b + GR - 1)
                transpose_outputs(b, GR - 1)

            pe.wait_ge(k_ones, 1)
            scores_by_queries(0, 0, 0, range(NH))
            transpose_maxima(0)
            if half_B > 1:
                with pe.Fori(0, half_B - 1) as i:
                    for p in range(2):
                        step(2 * i + p, i, p)
            step(B - 2, half_B - 1, 0)
            step(B - 1, half_B - 1, 1, last=True)

        @block.scalar
        def _(act):
            def exponentials(b, u):
                kt = u % J
                for pr in range(2):
                    act.wait_ge(st_done, 2 * U * b + 2 * u + pr + 1)
                    if pr == 0:
                        act.wait_ge(pv_done, U * b + max(u - 1, 0))
                    nc.scalar.activation(pT[:, u % 2, 2 * pr:2 * pr + 2, first_q(kt):T], psT[:, pr, :, first_q(kt):T],
                                         ACT.Exp, scale=HD ** -0.5).then_inc(exp_done, 1)

            def read_outputs(b, g):
                act.wait_ge(pv_done, U * b + J * (g + 1))
                act.wait_ge(oT_done, GR * b + g)
                nc.scalar.activation(o_sb[:], psO[:], ACT.Copy).then_inc(evac_done, 1)

            def negate_maxima(b, i, p):
                if i is not None:
                    act.wait_ge(m_loaded[p], 32 * (i + 1))
                act.wait_ge(mT_done, b + 1)
                nc.scalar.activation(mrow[:, 0, :], psM[0:NH, :], ACT.Copy, scale=-1.0).then_inc(mhi_done, 1)

            def step(b, i, p, last=False):
                for u in range(U):
                    exponentials(b, u)
                    if u % J == 0 and u > 0:
                        read_outputs(b, u // J - 1)
                if not last:
                    negate_maxima(b + 1, i, p)
                read_outputs(b, GR - 1)

            negate_maxima(0, None, None)
            if half_B > 1:
                with act.Fori(0, half_B - 1) as i:
                    for p in range(2):
                        step(2 * i + p, i, p)
            step(B - 2, half_B - 1, 0)
            step(B - 1, half_B - 1, 1, last=True)

        @block.vector
        def _(dve):
            def maxima(b, heads):
                for h in heads:
                    if h == 0:
                        dve.wait_ge(mT_done, b)
                    for qt in range(J):
                        dve.wait_ge(s_done, J * NH * b + J * h + qt + 1)
                        nc.vector.reduce_max(mx[:, qt, h:h + 1], psS[:, qt % 2, 0:seen(qt)], axis=AX.X
                                             ).then_inc(max_done, 1)

            def second_part(b):
                dve.wait_ge(mhi_done, b + 1)
                nc.vector.scalar_tensor_tensor(mrow[:, 1, :], psM[0:NH, :], -1.0, mrow[:, 0, :],
                                               ALU.mult, ALU.subtract).then_inc(mrow_done, 1)

            def normalize(b, g):
                heads = psM[:].rearrange("p (j h e) -> p j h e", j=J, e=VW)
                dve.wait_ge(oT_done, GR * b + g + 1)
                nc.vector.reciprocal(rec[:], heads[:, :, :, HD]).then_inc(rec_done, 1)
                dve.wait_ge(rec_done, GR * b + g + 1)
                if g == 0:
                    dve.wait_ge(att_stored, 16 * b)
                out = att[:].rearrange("p j (h e) -> p j h e", e=HD)[:, :, G4 * g:G4 * (g + 1), :]
                nc.vector.tensor_tensor(out, heads[:, :, :, 0:HD], rec[:].unsqueeze(3).to_broadcast([P, J, G4, HD]),
                                        ALU.mult).then_inc(att_done, 1)

            def step(b, last=False):
                for u in range(U):
                    if not last:
                        maxima(b + 1, heads_of(u))
                    if u % J == 2 and u > J:
                        normalize(b, u // J - 1)
                if not last:
                    second_part(b + 1)
                normalize(b, GR - 1)

            for p in range(2):
                last = nc.vector.memset(ks[p][KS:KX, :, :], 1.0)
            last.then_inc(k_ones, 1)
            maxima(0, range(NH))
            second_part(0)
            if half_B > 1:
                with dve.Fori(0, half_B - 1) as i:
                    for p in range(2):
                        step(2 * i + p)
            step(B - 2)
            step(B - 1, last=True)

        @block.gpsimd
        def _(pool):
            def expand_v(b, i, p):
                pool.wait_ge(v_loaded[p], 16 * (i + 1))
                heads = vd[p][:].rearrange("p j (h e) -> p j h e", e=HD)
                nc.gpsimd.tensor_tensor(vp[p][:, :, :, 0:HD], heads, one[:].unsqueeze(2).unsqueeze(3).to_broadcast(
                    [P, J, NH, HD]), ALU.mult).then_inc(v_exp, 1)

            def mask(b, u):
                kt = u % J
                pool.wait_ge(exp_done, 2 * U * b + 2 * u + 2)
                diagonal = pT[:, u % 2, :, kt * P:(kt + 1) * P]
                pool.wait_ge(sel_done, U * b + u)
                nc.gpsimd.tensor_tensor(pause[:], one[:], one[:], ALU.add)
                nc.gpsimd.affine_select(diagonal, diagonal, pattern=[[0, G4], [1, P]], compare_op=ALU.is_ge, fill=0.0,
                                        base=0, channel_multiplier=-1).then_inc(sel_done, 1)

            def step(b, i, p, last=False):
                if not last:
                    pool.wait_ge(pv_done, U * b)
                    expand_v(b + 1, i + p, 1 - p)
                if causal:
                    for u in range(U):
                        mask(b, u)

            for p in range(2):
                nc.gpsimd.memset(vp[p][:, :, :, HD:VW], 1.0)
            nc.gpsimd.memset(one[:], 1.0).then_inc(ones_done, 1)
            pool.wait_ge(ones_done, 1)
            expand_v(0, 0, 0)
            if half_B > 1:
                with pool.Fori(0, half_B - 1) as i:
                    for p in range(2):
                        step(2 * i + p, i, p)
            step(B - 2, half_B - 1, 0)
            step(B - 1, half_B - 1, 1, last=True)


def output_and_qkv_phase(nc, k, d):
    with ExitStack() as ctx:
        sb = lambda n, s, t=F32: ctx.enter_context(nc.sbuf_tensor("mid_" + n, s, t))
        sem = lambda n: nc.alloc_semaphore("mid_" + n)
        ps = lambda n, s: ctx.enter_context(nc.psum_tensor("mid_" + n, s, F32))
        B = k.B
        NB = 2 * CB
        wo, wq, wk, wv = sb("wo", [P, CB, C]), sb("wq", [P, CB, C]), sb("wk", [P, CB, C]), sb("wv", [P, CB, C])
        bv = sb("bv", [P, C])
        gate = sb("gate", [P, C])
        att = sb("att", [P, J, C])
        aT = sb("aT", [P, CB, T])
        y = sb("y", [P, J, C])
        z = sb("z", [P, J, C])
        hT = sb("hT", [P, CB, T])
        rest = sb("rest", [P, 2, T])
        parts = sb("parts", [P, 3, NB, T], BF16)
        v = sb("v", [P, J, C])
        ln = Norm(nc, ctx, "mid_ln")
        psA, psY, psV = ps("psA", [P, CB, T]), ps("psY", [P, J, C]), ps("psV", [P, J, C])
        psQ = ps("psQ", [P, 2, T])
        weights, gate_loaded, att_loaded = sem("weights"), sem("gate_loaded"), sem("att_loaded")
        aT_ps, aT_done, y_done, yg_done, x_done = sem("aT_ps"), sem("aT_done"), sem("y_done"), sem("yg_done"), sem("x_done")
        z_done, zT_done, hT_done, q_done = sem("z_done"), sem("zT_done"), sem("hT_done"), sem("q_done")
        hi_done, rest_done, mid_done, lo_done = sem("hi_done"), sem("rest_done"), sem("mid_done"), sem("lo_done")
        v_done, vb_done, v_stored, parts_stored = sem("v_done"), sem("vb_done"), sem("v_stored"), sem("parts_stored")
        block = ctx.enter_context(nc.Block())
        bias = lambda n: col(k, "bq" if n < CB else "bk", n % CB)

        @block.sync
        def _(sp):
            for ap, src in ((wo, "w_out"), (wq, "Wq"), (wk, "Wk"), (wv, "Wv")):
                sp.dma_start(ap[:], d[src].rearrange("(k p) n -> p k n", p=P)).then_inc(weights, 16)
            sp.dma_start(bv[:], d["rows"][ROWS.index("bv")].partition_broadcast(P)).then_inc(weights, 16)

            def load(b):
                sp.wait_ge(yg_done, b)
                sp.dma_start(gate[:], k.mrows_dram[2, b].partition_broadcast(P)).then_inc(gate_loaded, 16)
                sp.dma_start(att[:], k.att_dram[b]).then_inc(att_loaded, 16)

            def store(b):
                sp.wait_ge(v_stored, 16 * b)
                sp.wait_ge(vb_done, b + 1)
                sp.dma_start(k.v_dram[b], v[:]).then_inc(v_stored, 16)
                sp.wait_ge(parts_stored, 16 * b)
                sp.wait_ge(mid_done, NB * b + NB)
                sp.wait_ge(lo_done, NB * b + NB)
                sp.dma_start(k.parts_dram[b].rearrange("s n p t -> p s n t"), parts[:]).then_inc(parts_stored, 16)

            load(0)
            with sp.Fori(0, B - 1) as b:
                load(b + 1)
                store(b)
            store(B - 1)
            sp.wait_ge(v_stored, 16 * B)
            sp.wait_ge(parts_stored, 16 * B)

        @block.tensor
        def _(pe):
            def project_out(b):
                pe.wait_ge(att_loaded, 16 * b + 16)
                pe.wait_ge(hT_done, b)
                to_channels(nc, k, psA, att).then_inc(aT_ps, 1)
                pe.wait_ge(aT_done, b + 1)
                pe.wait_ge(yg_done, b)
                for j in range(J):
                    for cb in range(CB):
                        last = nc.tensor.matmul(psY[:, j, :], aT[:, cb, j * P:(j + 1) * P], wo[:, cb, :],
                                                start=(cb == 0), stop=(cb == CB - 1))
                last.then_inc(y_done, 1)

            def transpose_h(b):
                pe.wait_ge(z_done, b + 1)
                to_channels(nc, k, psA, z).then_inc(zT_done, 1)

            def project_v(b):
                pe.wait_ge(hT_done, b + 1)
                pe.wait_ge(vb_done, b)
                for j in range(J):
                    for cb in range(CB):
                        last = nc.tensor.matmul(psV[:, j, :], hT[:, cb, j * P:(j + 1) * P], wv[:, cb, :],
                                                start=(cb == 0), stop=(cb == CB - 1))
                last.then_inc(v_done, 1)

            def project_qk(b):
                for n in range(NB):
                    w = wq if n < CB else wk
                    pe.wait_ge(rest_done, NB * b + max(n - 1, 0))
                    for cb in range(CB):
                        last = nc.tensor.matmul(psQ[:, n % 2, :], w[:, cb, (n % CB) * P:(n % CB + 1) * P],
                                                hT[:, cb, :], start=(cb == 0), stop=(cb == CB - 1))
                    last.then_inc(q_done, 1)

            pe.wait_ge(weights, 80)
            project_out(0)
            transpose_h(0)
            with pe.Fori(0, B - 1) as b:
                project_v(b)
                project_out(b + 1)
                project_qk(b)
                transpose_h(b + 1)
            project_v(B - 1)
            project_qk(B - 1)

        @block.scalar
        def _(act):
            def copy_attention(b):
                act.wait_ge(aT_ps, b + 1)
                act.wait_ge(y_done, b)
                nc.scalar.activation(aT[:], psA[:], ACT.Copy).then_inc(aT_done, 1)

            def modulate(b):
                act.wait_ge(zT_done, b + 1)
                act.wait_ge(v_done, b)
                act.wait_ge(q_done, NB * b)
                for cb in range(CB):
                    last = nc.scalar.activation(hT[:, cb, :], psA[:, cb, :], ACT.Identity,
                                                scale=k.mod[:, 1, CBM * CB + cb, bass.ds(b, 1)],
                                                bias=k.mod[:, 1, SB * CB + cb, bass.ds(b, 1)])
                last.then_inc(hT_done, 1)

            def split(b):
                act.wait_ge(parts_stored, 16 * b)
                for n in range(NB):
                    act.wait_ge(q_done, NB * b + n + 1)
                    nc.scalar.activation(parts[:, 0, n, :], psQ[:, n % 2, :], ACT.Identity, bias=bias(n)
                                         ).then_inc(hi_done, 1)
                    act.wait_ge(rest_done, NB * b + n + 1)
                    nc.scalar.activation(parts[:, 1, n, :], rest[:, n % 2, :], ACT.Copy).then_inc(mid_done, 1)

            copy_attention(0)
            modulate(0)
            with act.Fori(0, B - 1) as b:
                copy_attention(b + 1)
                split(b)
                modulate(b + 1)
            split(B - 1)

        @block.vector
        def _(dve):
            def residual(b):
                dve.wait_ge(y_done, b + 1)
                dve.wait_ge(gate_loaded, 16 * b + 16)
                dve.wait_ge(x_done, b)
                nc.vector.tensor_tensor(y[:], psY[:], over_tiles(gate[:]), ALU.mult).then_inc(yg_done, 1)
                dve.wait_ge(yg_done, b + 1)
                xb = k.x[:, bass.ds(b * J, J), :]
                nc.vector.tensor_tensor(xb, xb, y[:], ALU.add).then_inc(x_done, 1)
                dve.wait_ge(x_done, b + 1)
                nc.vector.memset(ln.pause[:], 0.0)
                tile = lambda j: k.x[:, b * J + j, :]
                ln.moments(nc, dve, tile, b)
                dve.wait_ge(zT_done, b)
                ln.apply(nc, dve, z, tile, b).then_inc(z_done, 1)

            def add_bias(b):
                dve.wait_ge(v_done, b + 1)
                dve.wait_ge(v_stored, 16 * b)
                nc.vector.tensor_tensor(v[:], psV[:], over_tiles(bv[:]), ALU.add).then_inc(vb_done, 1)

            def split(b, blocks):
                for n in blocks:
                    dve.wait_ge(hi_done, NB * b + n + 1)
                    dve.wait_ge(lo_done, NB * b + max(n - 1, 0))
                    nc.vector.scalar_tensor_tensor(rest[:, n % 2, :], psQ[:, n % 2, :], bias(n), parts[:, 0, n, :],
                                                   ALU.add, ALU.subtract).then_inc(rest_done, 1)

            dve.wait_ge(weights, 80)
            residual(0)
            with dve.Fori(0, B - 1) as b:
                add_bias(b)
                split(b, range(0, 2))
                residual(b + 1)
                split(b, range(2, NB))
            add_bias(B - 1)
            split(B - 1, range(NB))

        @block.gpsimd
        def _(pool):
            def low_parts(b, blocks):
                for n in blocks:
                    pool.wait_ge(mid_done, NB * b + n + 1)
                    if n == 0:
                        pool.wait_ge(parts_stored, 16 * b)
                    nc.gpsimd.tensor_tensor(parts[:, 2, n, :], rest[:, n % 2, :], parts[:, 1, n, :],
                                            ALU.subtract).then_inc(lo_done, 1)

            ln.rsqrt(nc, k, pool, 0)
            with pool.Fori(0, B - 1) as b:
                low_parts(b, range(0, 2))
                ln.rsqrt(nc, k, pool, b + 1)
                low_parts(b, range(2, NB))
            low_parts(B - 1, range(NB))


ROW_X1, ROW_X, ROW_GATE, ROW_ID, ROW = 0, C, 2 * C, 3 * C, 3 * C + 4
I32 = mybir.dt.int32


def route_phase(nc, k, d):
    with ExitStack() as ctx:
        sb = lambda n, s, t=F32: ctx.enter_context(nc.sbuf_tensor("rou_" + n, s, t))
        sem = lambda n: nc.alloc_semaphore("rou_" + n)
        ps = lambda n, s: ctx.enter_context(nc.psum_tensor("rou_" + n, s, F32))
        B = k.B
        wo = sb("wo", [P, CB, C])
        rowb = {n: sb(f"rowb_{n}", [P, C]) for n in ("bo", "l1_ln1_g", "l1_ln1_b", "router_w")}
        before, ones = sb("before", [P, P]), sb("ones", [P, P])
        experts = sb("experts", [P, NE])
        ids = sb("ids", [P, B * J], I32)
        mrow = [sb(f"mrow{i}", [P, 3, C]) for i in range(2)]
        att = sb("att", [P, J, C])
        aT = sb("aT", [P, CB, T])
        z = [sb(f"z{i}", [P, J, C]) for i in range(2)]
        rows = [sb(f"rows_out{i}", [P, J, ROW]) for i in range(2)]
        junk = sb("junk", [P, J, C])
        key, key_f, above = sb("key", [P, J]), sb("key_f", [P, J]), sb("above", [P, J])
        key_i, expert_i, expert_f = sb("key_i", [P, J], I32), sb("expert_i", [P, J], I32), sb("expert_f", [P, J])
        member = sb("member", [P, J, NE])
        place = sb("place", [P, J, NE])
        slot = sb("slot", [P, J])
        slot_i = [sb(f"slot_i{i}", [P, J], I32) for i in range(2)]
        pool_pause = sb("pool_pause", [P, 2])
        nxt = k.next_row
        ln0, ln1 = Norm(nc, ctx, "rou_ln0"), Norm(nc, ctx, "rou_ln1")
        psA, psY = ps("psA", [P, CB, T]), ps("psY", [P, J, C])
        psR = ps("psR", [P, T])
        PREFIX, TOTAL = psR[:, 0:J * NE], psR[:, J * NE:(J + 1) * NE]
        weights, att_loaded, init = sem("weights"), sem("att_loaded"), sem("init")
        mrow_loaded = [sem(f"mrow_loaded{i}") for i in range(2)]
        scattered = [sem(f"scattered{i}") for i in range(2)]
        aT_ps, aT_done, y_done = sem("aT_ps"), sem("aT_done"), sem("y_done")
        z_done, shift_done, zs_done, src_done = sem("z_done"), sem("shift_done"), sem("zs_done"), sem("src_done")
        t_done, z1g_done, x1_done = sem("t_done"), sem("z1g_done"), sem("x1_done")
        copied, member_done = sem("copied"), sem("member_done")
        key_step, slot_step = sem("key_step"), sem("slot_step")
        ranks_done, slot_done = sem("ranks_done"), sem("slot_done")
        block = ctx.enter_context(nc.Block())
        KEY_STEPS, SLOT_STEPS = 7, 3
        rounds = B // 2

        @block.sync
        def _(sp):
            sp.dma_start(wo[:], d["Wo"].rearrange("(k p) n -> p k n", p=P)).then_inc(weights, 16)
            for n, ap in rowb.items():
                sp.dma_start(ap[:], d["rows"][ROWS.index(n)].partition_broadcast(P)).then_inc(weights, 16)
            for ap, n in ((before, "before"), (experts, "experts"), (ids, "ids")):
                sp.dma_start(ap[:], d[n]).then_inc(weights, 16)

            def load_attention(b):
                sp.dma_start(att[:], k.att_dram[b]).then_inc(att_loaded, 16)

            def load_rows(b, p):
                for n, row in enumerate((4, 5, 3)):
                    sp.dma_start(mrow[p][:, n, :], k.mrows_dram[row, b].partition_broadcast(P)
                                 ).then_inc(mrow_loaded[p], 16)

            def step(b, p):
                sp.wait_ge(aT_ps, b + 2)
                load_attention(b + 2)
                sp.wait_ge(copied, b + 1)
                sp.wait_ge(src_done, b + 1)
                load_rows(b + 2, p)

            load_attention(0)
            for p in range(2):
                load_rows(p, p)
            sp.wait_ge(aT_ps, 1)
            load_attention(1)
            with sp.Fori(0, rounds - 1) as i:
                for p in range(2):
                    step(2 * i + p, p)

        @block.tensor
        def _(pe):
            def project_out(b):
                pe.wait_ge(att_loaded, 16 * b + 16)
                pe.wait_ge(aT_done, b)
                to_channels(nc, k, psA, att).then_inc(aT_ps, 1)
                pe.wait_ge(aT_done, b + 1)
                pe.wait_ge(t_done, b)
                for j in range(J):
                    for cb in range(CB):
                        last = nc.tensor.matmul(psY[:, j, :], aT[:, cb, j * P:(j + 1) * P], wo[:, cb, :],
                                                start=(cb == 0), stop=(cb == CB - 1))
                last.then_inc(y_done, 1)

            def count(b):
                pe.wait_ge(member_done, b + 1)
                pe.wait_ge(slot_done, b)
                for j in range(J):
                    out = PREFIX[:, j * NE:(j + 1) * NE]
                    nc.tensor.matmul(out, before[:], member[:, j, :], start=True, stop=(j == 0))
                    for earlier in range(j):
                        nc.tensor.matmul(out, ones[:], member[:, earlier, :], start=False, stop=(earlier == j - 1))
                for j in range(J):
                    last = nc.tensor.matmul(TOTAL, ones[:], member[:, j, :], start=(j == 0), stop=(j == J - 1))
                last.then_inc(ranks_done, 1)

            pe.wait_ge(weights, 128)
            pe.wait_ge(init, 1)
            def round_(i, last=False):
                for p in range(2):
                    count(2 * i + p)
                    if not last:
                        project_out(2 * i + p + 2)

            project_out(0)
            project_out(1)
            round_(0)
            with pe.Fori(1, rounds - 1) as i:
                round_(i)
            round_(rounds - 1, last=True)

        @block.scalar
        def _(act):
            def copy_attention(b):
                act.wait_ge(aT_ps, b + 1)
                act.wait_ge(y_done, b)
                nc.scalar.activation(aT[:], psA[:], ACT.Copy).then_inc(aT_done, 1)

            def fill_rows(b, i, p):
                act.wait_ge(mrow_loaded[p], 48 * (i + 1))
                if not (isinstance(i, int) and i == 0):
                    act.wait_ge(scattered[p], 64 * i)
                nc.scalar.activation(rows[p][:, :, ROW_X:ROW_X + C], k.x[:, bass.ds(b * J, J), :], ACT.Copy)
                nc.scalar.activation(rows[p][:, :, ROW_GATE:ROW_GATE + C], over_tiles(mrow[p][:, 2, :]), ACT.Copy
                                     ).then_inc(copied, 1)

            def round_(i, last=False):
                for p in range(2):
                    if not (last and p == 1):
                        fill_rows(2 * i + p + 1, i + p, 1 - p)
                    if not last:
                        copy_attention(2 * i + p + 2)

            copy_attention(0)
            fill_rows(0, 0, 0)
            copy_attention(1)
            round_(0)
            with act.Fori(1, rounds - 1) as i:
                round_(i)
            round_(rounds - 1, last=True)

        @block.gpsimd
        def _(pool):
            def source(b, i, p):
                pool.wait_ge(mrow_loaded[p], 48 * (i + 1))
                pool.wait_ge(z_done, b + 1)
                nc.gpsimd.tensor_tensor(z[p][:], z[p][:], over_tiles(mrow[p][:, 0, :]), ALU.mult).then_inc(zs_done, 1)
                pool.wait_ge(zs_done, b + 1)
                pool.wait_ge(shift_done, b + 1)
                nc.gpsimd.tensor_tensor(z[p][:], z[p][:], over_tiles(mrow[p][:, 1, :]), ALU.add).then_inc(src_done, 1)

            def scatter(b, p):
                pool.wait_ge(slot_done, b + 1)
                pool.wait_ge(copied, b + 1)
                nc.gpsimd.tensor_tensor(pool_pause[:, p:p + 1], k.eps[:, 0:1], k.eps[:, 0:1], ALU.add)
                for j in range(J):
                    nc.gpsimd.indirect_dma_start(k.rows_dram, bass.IndirectOffsetOnAxis(ap=slot_i[p][:, j:j + 1], axis=0),
                                                 rows[p][:, j, :], None).then_inc(scattered[p], 16)

            def round_(i, last=False):
                for p in range(2):
                    b = 2 * i + p
                    if not last:
                        ln0.rsqrt(nc, k, pool, b + 2)
                    if not (last and p == 1):
                        ln1.rsqrt(nc, k, pool, b + 1)
                    scatter(b, p)
                    if not last:
                        source(b + 2, i + 1, p)

            nc.gpsimd.memset(ones[:], 1.0)
            for p in range(2):
                last = nc.gpsimd.memset(rows[p][:, :, ROW_ID:ROW], 0.0)
            last.then_inc(init, 1)
            pool.wait_ge(init, 1)
            ln0.rsqrt(nc, k, pool, 0)
            source(0, 0, 0)
            ln0.rsqrt(nc, k, pool, 1)
            ln1.rsqrt(nc, k, pool, 0)
            source(1, 0, 1)
            round_(0)
            with pool.Fori(1, rounds - 1) as i:
                round_(i)
            round_(rounds - 1, last=True)
            for p in range(2):
                pool.wait_ge(scattered[p], 64 * rounds)

        @block.vector
        def _(dve):
            def source_moments(b):
                ln0.moments(nc, dve, lambda j: k.x[:, b * J + j, :], b)

            def source_normalize(b, i, p):
                if not (isinstance(b, int) and b < 2):
                    dve.wait_ge(x1_done, b - 1)
                ln0.apply(nc, dve, z[p], lambda j: k.x[:, b * J + j, :], b).then_inc(z_done, 1)
                dve.wait_ge(mrow_loaded[p], 48 * (i + 1))
                nc.vector.tensor_tensor(mrow[p][:, 1, :], mrow[p][:, 1, :], rowb["bo"][:], ALU.add).then_inc(shift_done, 1)

            def add_source(b, p):
                dve.wait_ge(y_done, b + 1)
                dve.wait_ge(src_done, b + 1)
                nc.vector.tensor_tensor(z[p][:], psY[:], z[p][:], ALU.add).then_inc(t_done, 1)
                dve.wait_ge(t_done, b + 1)
                nc.vector.memset(ln1.pause[:], 0.0)
                ln1.moments(nc, dve, lambda j: z[p][:, j, :], b)

            def normalize(b, i, p):
                dve.wait_ge(ln1.rstd_ready, b + 1)
                for j in range(J):
                    last = nc.vector.scalar_tensor_tensor(z[p][:, j, :], z[p][:, j, :], ln1.mv[:, j, 0:1],
                                                          rowb["l1_ln1_g"][:], ALU.subtract, ALU.mult)
                last.then_inc(z1g_done, 1)
                dve.wait_ge(z1g_done, b + 1)
                if not (isinstance(i, int) and i == 0):
                    dve.wait_ge(scattered[p], 64 * i)
                nc.vector.tensor_copy(rows[p][:, :, ROW_ID:ROW_ID + 1].bitcast(I32),
                                      ids[:, bass.ds(b * J, J)].unsqueeze(2))
                for j in range(J):
                    last = nc.vector.scalar_tensor_tensor(rows[p][:, j, ROW_X1:ROW_X1 + C], z[p][:, j, :],
                                                          ln1.rstd[:, j:j + 1], rowb["l1_ln1_b"][:], ALU.mult, ALU.add)
                last.then_inc(x1_done, 1)

            def choose(b, p):
                taken = [0]

                def follow(instruction):
                    taken[0] += 1
                    instruction.then_inc(key_step, 1)
                    dve.wait_ge(key_step, KEY_STEPS * b + taken[0])

                dve.wait_ge(x1_done, b + 1)
                for j in range(J):
                    instruction = nc.vector.tensor_tensor_reduce(
                        out=junk[:, j, :], in0=rows[p][:, j, ROW_X1:ROW_X1 + C], in1=rowb["router_w"][:], scale=1.0,
                        scalar=k.cols[:, COLS["router_b"][0]:COLS["router_b"][0] + 1], op0=ALU.mult, op1=ALU.add,
                        accum_out=key[:, j:j + 1])
                follow(instruction)
                follow(nc.vector.tensor_copy(key_i[:], key[:]))
                follow(nc.vector.tensor_copy(key_f[:], key_i[:]))
                follow(nc.vector.tensor_tensor(above[:], key_f[:], key[:], ALU.is_gt))
                follow(nc.vector.tensor_tensor(key_i[:], key_f[:], above[:], ALU.subtract))
                follow(nc.vector.tensor_scalar(expert_i[:], key_i[:], NE - 1, None, ALU.bitwise_and))
                follow(nc.vector.tensor_copy(expert_f[:], expert_i[:]))
                nc.vector.tensor_tensor(member[:], expert_f[:].unsqueeze(2).to_broadcast([P, J, NE]),
                                        experts[:].unsqueeze(1).to_broadcast([P, J, NE]), ALU.is_equal
                                        ).then_inc(member_done, 1)
                assert taken[0] == KEY_STEPS

            def place_rows(b, i, p):
                taken = [0]

                def follow(instruction):
                    taken[0] += 1
                    instruction.then_inc(slot_step, 1)
                    dve.wait_ge(slot_step, SLOT_STEPS * b + taken[0])

                dve.wait_ge(member_done, b + 1)
                dve.wait_ge(ranks_done, b + 1)
                follow(nc.vector.tensor_tensor(place[:], PREFIX.rearrange("p (j e) -> p j e", e=NE),
                                               nxt[:].unsqueeze(1).to_broadcast([P, J, NE]), ALU.add))
                follow(nc.vector.tensor_tensor(place[:], place[:], member[:], ALU.mult))
                nc.vector.tensor_tensor(nxt[:], nxt[:], TOTAL, ALU.add)
                follow(nc.vector.tensor_reduce(slot[:], place[:], op=ALU.add, axis=AX.X))
                if not (isinstance(i, int) and i == 0):
                    dve.wait_ge(scattered[p], 64 * i)
                nc.vector.tensor_copy(slot_i[p][:], slot[:]).then_inc(slot_done, 1)
                dve.wait_ge(slot_done, b + 1)
                nc.vector.memset(ln1.pause[:], 0.0)
                assert taken[0] == SLOT_STEPS

            def round_(i, last=False):
                for p in range(2):
                    b = 2 * i + p
                    if not last:
                        source_moments(b + 2)
                    if not (last and p == 1):
                        add_source(b + 1, 1 - p)
                    place_rows(b, i, p)
                    if not last:
                        source_normalize(b + 2, i + 1, p)
                    if not (last and p == 1):
                        normalize(b + 1, i + p, 1 - p)
                        choose(b + 1, 1 - p)

            dve.wait_ge(weights, 128)
            dve.wait_ge(init, 1)
            nc.vector.tensor_scalar(nxt[:], experts[:], float(k.CAP), None, ALU.mult)
            source_moments(0)
            source_normalize(0, 0, 0)
            source_moments(1)
            add_source(0, 0)
            source_normalize(1, 0, 1)
            normalize(0, 0, 0)
            choose(0, 0)
            round_(0)
            with dve.Fori(1, rounds - 1) as i:
                round_(i)
            round_(rounds - 1, last=True)


def expert_phase(nc, k, d, out):
    with ExitStack() as ctx:
        sb = lambda n, s, t=F32: ctx.enter_context(nc.sbuf_tensor("exp_" + n, s, t))
        sem = lambda n: nc.alloc_semaphore("exp_" + n)
        ps = lambda n, s: ctx.enter_context(nc.psum_tensor("exp_" + n, s, F32))
        N = k.B * T
        NT = k.NT
        assert NT % RING == 0
        PADS = 2 * NE
        w1, w2 = k.moe_w1, k.moe_w2
        b1 = sb("b1", [P, NE, FF])
        b2 = sb("b2", [P, NE, C])
        rowb = {n: sb(f"rowb_{n}", [P, C]) for n in ("l1_ln2_g", "l1_ln2_b")}
        experts = sb("experts", [P, NE])
        lane = sb("lane", [P, 1])
        pad_ids = sb("pad_ids", [P, 1], I32)
        pad = sb("pad", [P, ROW])
        pad_row = sb("pad_row", [P, PADS])
        pad_slot = sb("pad_slot", [P, PADS], I32)
        number = sb("number", [1, NT])
        tiles_f, tiles_i = sb("tiles_f", [1, NE]), sb("tiles_i", [1, NE], I32)
        ends, jump = sb("ends", [1, NE]), sb("jump", [1, NE])
        reached = sb("reached", [1, NT])
        plan_e, plan_r = sb("plan_e", [1, NT]), sb("plan_r", [1, NT])
        expert_of, row_of = sb("expert_of", [1, NT], I32), sb("row_of", [1, NT], I32)
        rt = [sb(f"rt{i}", [P, ROW]) for i in range(RING)]
        x1T = [sb(f"x1T{i}", [P, CB, P]) for i in range(2)]
        hid = sb("hid", [P, FF])
        hidT = sb("hidT", [P, FB, P])
        t = [sb(f"t{i}", [P, C]) for i in range(RING)]
        stats, mv = sb("stats", [P, 6]), sb("mv", [P, 2, 2])
        pool_pause = sb("pool_pause", [P, 1])
        ve, rstd, pause = sb("ve", [P, 1]), sb("rstd", [P, 2]), sb("pause", [P, 1])
        psX, psH, psT = ps("psX", [P, CB, P]), ps("psH", [P, 2, T]), ps("psT", [P, FB, P])
        psY = ps("psY", [P, C])
        loaded, init, step, plan_done, padded = sem("loaded"), sem("init"), sem("step"), sem("plan_done"), sem("padded")
        rt_loaded = [sem(f"rt_loaded{i}") for i in range(RING)]
        scattered = [sem(f"scattered{i}") for i in range(RING)]
        xT_ps, xT_done, hid_ps, hid_done = sem("xT_ps"), sem("xT_done"), sem("hid_ps"), sem("hid_done")
        hT_ps, hT_done, y_done, t_done = sem("hT_ps"), sem("hT_done"), sem("y_done"), sem("t_done")
        tb_done, stats_done, mv_done, ve_done = sem("tb_done"), sem("stats_done"), sem("mv_done"), sem("ve_done")
        rstd_done, zg_done, z_done, u_done = sem("rstd_done"), sem("zg_done"), sem("z_done"), sem("u_done")
        block = ctx.enter_context(nc.Block())
        rounds = NT // RING

        @block.sync
        def _(sp):
            for src, ap in (("moe_b1_rows", b1), ("moe_b2_rows", b2)):
                sp.dma_start(ap[:], d[src].partition_broadcast(P)).then_inc(loaded, 16)
            for n, ap in rowb.items():
                sp.dma_start(ap[:], d["rows"][ROWS.index(n)].partition_broadcast(P)).then_inc(loaded, 16)
            for n, ap in (("experts", experts), ("lane", lane), ("pad_ids", pad_ids), ("number", number)):
                sp.dma_start(ap[:], d[n]).then_inc(loaded, 16)

            def load(c, i, p):
                row = sp.value_load(row_of[0:1, bass.ds(c, 1)], min_val=0, max_val=k.ROWS_ALL - P)
                if i is not None:
                    sp.wait_ge(scattered[p], 16 * i)
                sp.dma_start(rt[p][:], k.rows_dram[bass.ds(row, P), :]).then_inc(rt_loaded[p], 16)

            sp.wait_ge(plan_done, 1)
            sp.wait_ge(padded, 16 * PADS)
            for p in range(RING):
                load(p, None, p)
            with sp.Fori(1, rounds) as i:
                for p in range(RING):
                    load(RING * i + p, i, p)

        @block.vector
        def _(dve):
            taken = [0]

            def follow(instruction):
                taken[0] += 1
                instruction.then_inc(step, 1)
                dve.wait_ge(step, taken[0])

            dve.wait_ge(loaded, 128)
            dve.wait_ge(init, 1)
            nc.vector.tensor_copy(pad[:, ROW_ID:ROW_ID + 1].bitcast(I32), pad_ids[:])
            for n in range(PADS):
                if n < NE:
                    last = nc.vector.tensor_tensor(pad_row[:, n:n + 1], lane[:], k.next_row[:, n:n + 1], ALU.add)
                else:
                    last = nc.vector.tensor_scalar(pad_row[:, n:n + 1], lane[:], float(NE * k.CAP + (n - NE) * P),
                                                   None, ALU.add)
            follow(last)
            follow(nc.vector.tensor_copy(pad_slot[:], pad_row[:]))
            follow(nc.vector.tensor_scalar(tiles_f[:], experts[0:1, :], -float(k.CAP), float(P - 1), ALU.mult, ALU.add))
            follow(nc.vector.tensor_tensor(tiles_i[:], tiles_f[:], k.next_row[0:1, :], ALU.add))
            follow(nc.vector.tensor_scalar(tiles_i[:], tiles_i[:], 7, None, ALU.arith_shift_right))
            follow(nc.vector.tensor_copy(tiles_f[:], tiles_i[:]))
            follow(nc.vector.tensor_scalar(jump[:], tiles_f[:], -float(P), float(k.CAP), ALU.mult, ALU.add))
            follow(nc.vector.tensor_copy(ends[:], tiles_f[:]))
            for e in range(1, NE):
                follow(nc.vector.tensor_tensor(ends[:, e:e + 1], ends[:, e:e + 1], ends[:, e - 1:e], ALU.add))
            follow(nc.vector.tensor_scalar(plan_r[:], number[:], float(P), None, ALU.mult))
            follow(nc.vector.memset(plan_e[:], 0.0))
            for e in range(NE):
                follow(nc.vector.tensor_scalar(reached[:], number[:], ends[:, e:e + 1], None, ALU.is_ge))
                follow(nc.vector.tensor_tensor(plan_e[:], plan_e[:], reached[:], ALU.add))
                follow(nc.vector.scalar_tensor_tensor(plan_r[:], reached[:], jump[:, e:e + 1], plan_r[:],
                                                      ALU.mult, ALU.add))
            nc.vector.tensor_scalar(expert_of[:], plan_e[:], float(NE - 1), None, ALU.min)
            nc.vector.tensor_copy(row_of[:], plan_r[:]).then_inc(plan_done, 1)
            dve.wait_ge(plan_done, 1)

            def hidden_bias(c):
                e = dve.value_load(expert_of[0:1, bass.ds(c, 1)], min_val=0, max_val=NE - 1)
                for n in range(2):
                    dve.wait_ge(hid_ps, 2 * c + n + 1)
                    if n == 0:
                        dve.wait_ge(hT_ps, c)
                    nc.vector.tensor_tensor(hid[:, n * T:(n + 1) * T], psH[:, n, :],
                                            b1[:, bass.ds(e, 1), n * T:(n + 1) * T].rearrange("p o f -> p (o f)"),
                                            ALU.add).then_inc(hid_done, 1)

            def moments(c, p):
                e = dve.value_load(expert_of[0:1, bass.ds(c, 1)], min_val=0, max_val=NE - 1)
                dve.wait_ge(y_done, c + 1)
                nc.vector.tensor_tensor(t[p][:], psY[:], rt[p][:, ROW_X1:ROW_X1 + C], ALU.add).then_inc(t_done, 1)
                dve.wait_ge(t_done, c + 1)
                nc.vector.tensor_tensor(t[p][:], t[p][:], b2[:, bass.ds(e, 1), :].rearrange("p o f -> p (o f)"),
                                        ALU.add).then_inc(tb_done, 1)
                dve.wait_ge(tb_done, c + 1)
                nc.vector.bn_stats(stats[:], t[p][:]).then_inc(stats_done, 1)
                dve.wait_ge(stats_done, c + 1)
                nc.vector.memset(pause[:], 0.0)
                nc.vector.bn_aggr(mv[:, p % 2, :], stats[:]).then_inc(mv_done, 1)

            def normalize(c, p):
                dve.wait_ge(rstd_done, c + 1)
                nc.vector.scalar_tensor_tensor(t[p][:], t[p][:], mv[:, p % 2, 0:1], rowb["l1_ln2_g"][:],
                                               ALU.subtract, ALU.mult).then_inc(zg_done, 1)
                dve.wait_ge(zg_done, c + 1)
                nc.vector.scalar_tensor_tensor(t[p][:], t[p][:], rstd[:, p % 2:p % 2 + 1], rowb["l1_ln2_b"][:],
                                               ALU.mult, ALU.add).then_inc(z_done, 1)

            def round_(i, first=False, last=False):
                for p in range(RING):
                    c = RING * i + p
                    if not (first and p == 0):
                        normalize(c - 1, (p - 1) % RING)
                    if not (last and p == RING - 1):
                        hidden_bias(c + 1)
                    moments(c, p)

            hidden_bias(0)
            round_(0, first=True)
            with dve.Fori(1, rounds - 1) as i:
                round_(i)
            round_(rounds - 1, last=True)
            normalize(NT - 1, RING - 1)

        @block.tensor
        def _(pe):
            def expert(c):
                return pe.value_load(expert_of[0:1, bass.ds(c, 1)], min_val=0, max_val=NE - 1)

            def transpose_x(c, i, p):
                pe.wait_ge(rt_loaded[p], 16 * (i + 1))
                pe.wait_ge(xT_done, c)
                for cb in range(CB):
                    last = nc.tensor.transpose(psX[:, cb, :], rt[p][:, ROW_X1 + cb * P:ROW_X1 + (cb + 1) * P],
                                               k.ident[:])
                last.then_inc(xT_ps, 1)

            def hidden(c, p, e):
                pe.wait_ge(xT_done, c + 1)
                for n in range(2):
                    pe.wait_ge(hid_done, 2 * c)
                    for cb in range(CB):
                        last = nc.tensor.matmul(psH[:, n, :], x1T[p][:, cb, :],
                                                w1[:, bass.ds(e, 1), cb, n * T:(n + 1) * T].rearrange("p o f -> p (o f)"),
                                                start=(cb == 0), stop=(cb == CB - 1))
                    last.then_inc(hid_ps, 1)

            def transpose_hidden(c):
                pe.wait_ge(hid_done, 2 * c + 2)
                pe.wait_ge(hT_done, c)
                for f in range(FB):
                    last = nc.tensor.transpose(psT[:, f, :], hid[:, f * P:(f + 1) * P], k.ident[:])
                last.then_inc(hT_ps, 1)

            def output(c, e):
                pe.wait_ge(hT_done, c + 1)
                pe.wait_ge(t_done, c)
                for f in range(FB):
                    last = nc.tensor.matmul(psY[:], hidT[:, f, :],
                                            w2[:, bass.ds(e, 1), f, :].rearrange("p o f -> p (o f)"),
                                            start=(f == 0), stop=(f == FB - 1))
                last.then_inc(y_done, 1)

            def round_(i, last=False):
                for p in range(RING):
                    c = RING * i + p
                    if not (last and p == RING - 1):
                        hidden(c + 1, (p + 1) % 2, expert(c + 1))
                    if not (last and p >= RING - 2):
                        transpose_x(c + 2, i + (p + 2) // RING, (p + 2) % RING)
                    output(c, expert(c))
                    if not (last and p == RING - 1):
                        transpose_hidden(c + 1)

            pe.wait_ge(plan_done, 1)
            pe.wait_ge(k.moe_loaded, 32)
            transpose_x(0, 0, 0)
            hidden(0, 0, expert(0))
            transpose_hidden(0)
            transpose_x(1, 0, 1)
            round_(0)
            with pe.Fori(1, rounds - 1) as i:
                round_(i)
            round_(rounds - 1, last=True)

        @block.scalar
        def _(act):
            def copy_x(c, p):
                act.wait_ge(xT_ps, c + 1)
                act.wait_ge(hid_ps, 2 * c)
                nc.scalar.activation(x1T[p][:], psX[:], ACT.Copy).then_inc(xT_done, 1)

            def relu(c):
                act.wait_ge(hT_ps, c + 1)
                act.wait_ge(y_done, c)
                nc.scalar.activation(hidT[:], psT[:], ACT.Relu).then_inc(hT_done, 1)

            def round_(i, last=False):
                for p in range(RING):
                    c = RING * i + p
                    if not (last and p >= RING - 2):
                        copy_x(c + 2, p % 2)
                    if not (last and p == RING - 1):
                        relu(c + 1)

            copy_x(0, 0)
            relu(0)
            copy_x(1, 1)
            round_(0)
            with act.Fori(1, rounds - 1) as i:
                round_(i)
            round_(rounds - 1, last=True)

        @block.gpsimd
        def _(pool):
            def rsqrt(c, p):
                pool.wait_ge(mv_done, c + 1)
                nc.gpsimd.tensor_tensor(ve[:], mv[:, p % 2, 1:2], k.eps[:, 0:1], ALU.add).then_inc(ve_done, 1)
                pool.wait_ge(ve_done, c + 1)
                nc.gpsimd.tensor_tensor(rstd[:, p % 2:p % 2 + 1], ve[:], k.minus_half[:, 0:1], ALU.pow
                                        ).then_inc(rstd_done, 1)

            def finish(c, p):
                pool.wait_ge(z_done, c + 1)
                nc.gpsimd.tensor_tensor(t[p][:], t[p][:], rt[p][:, ROW_GATE:ROW_GATE + C], ALU.mult).then_inc(u_done, 1)
                pool.wait_ge(u_done, 2 * c + 1)
                nc.gpsimd.tensor_tensor(t[p][:], t[p][:], rt[p][:, ROW_X:ROW_X + C], ALU.add).then_inc(u_done, 1)
                pool.wait_ge(u_done, 2 * c + 2)
                nc.gpsimd.tensor_tensor(pool_pause[:], k.eps[:, 0:1], k.eps[:, 0:1], ALU.add)
                nc.gpsimd.indirect_dma_start(out, bass.IndirectOffsetOnAxis(
                    ap=rt[p][:, ROW_ID:ROW_ID + 1].bitcast(mybir.dt.uint32), axis=0), t[p][:], None,
                    bounds_check=last_token, oob_is_err=False).then_inc(scattered[p], 16)

            def round_(i, last=False):
                for p in range(RING):
                    finish(RING * i + p, p)
                    if not (last and p == RING - 1):
                        rsqrt(RING * i + p + 1, p + 1)

            last_token = nc.gpsimd.to_reg(N - 1)
            nc.gpsimd.memset(pad[:], 0.0).then_inc(init, 1)
            pool.wait_ge(plan_done, 1)
            for n in range(PADS):
                nc.gpsimd.indirect_dma_start(k.rows_dram, bass.IndirectOffsetOnAxis(ap=pad_slot[:, n:n + 1], axis=0),
                                             pad[:], None).then_inc(padded, 16)
            rsqrt(0, 0)
            round_(0)
            with pool.Fori(1, rounds - 1) as i:
                round_(i)
            round_(rounds - 1, last=True)
            for p in range(RING):
                pool.wait_ge(scattered[p], 16 * rounds)


def cleared(nc):
    return nc.cleanup_on_exit()


def build(nc, d, out, B, upto="all"):
    k = Core()
    k.B = B
    with ExitStack() as ctx:
        sb = lambda n, s, t=F32: ctx.enter_context(nc.sbuf_tensor(n, s, t))
        k.x = sb("x_res", [P, B * J, C])
        k.mod = sb("mod", [P, 2, 12, B])
        k.cols = sb("cols_sb", [P, NCOLS])
        k.ident = sb("ident_sb", [P, P])
        k.ident_bf = sb("ident_bf", [P, P], BF16)
        k.mask_bf = sb("mask_bf", [P, P], BF16)
        k.half = sb("half", [P, T])
        k.eps = sb("eps", [P, J])
        k.minus_half = sb("minus_half", [P, J])
        k.mrows_dram = nc.dram_tensor("mrows", (len(MROWS), B, C), F32, kind="Internal").ap()
        init = ctx.enter_context(nc.semaphore("consts"))
        with nc.Block() as block:
            @block.gpsimd
            def _(pool):
                nc.gpsimd.memset(k.eps[:], EPS)
                nc.gpsimd.memset(k.minus_half[:], -0.5).then_inc(init, 1)
                pool.wait_ge(init, 1)
        with cleared(nc):
            setup_phase(nc, k, d)
        k.parts_dram = nc.dram_tensor("parts_dram", (B, 3, 2 * CB, P, T), BF16, kind="Internal").ap()
        k.att_dram = nc.dram_tensor("att_dram", (B, P, J, C), F32, kind="Internal").ap()
        k.v_dram = nc.dram_tensor("v_dram", (B, P, J, C), F32, kind="Internal").ap()
        with cleared(nc):
            retention_phase(nc, k, d)
        if upto != "A":
            with cleared(nc):
                channel_mix_phase(nc, k, d)
        if upto not in "AB":
            with cleared(nc):
                rotary_qkv_phase(nc, k, d)
            with cleared(nc):
                attention_phase(nc, k, "causal", True)
            with cleared(nc):
                output_and_qkv_phase(nc, k, d)
        if upto == "all":
            with cleared(nc):
                attention_phase(nc, k, "full", False)
            k.CAP = B * T + P
            k.ROWS_ALL = NE * k.CAP + NE * P
            k.NT = B * J + NE
            k.rows_dram = nc.dram_tensor("rows_dram", (k.ROWS_ALL, ROW), F32, kind="Internal").ap()
            k.next_row = sb("next_row", [P, NE])
            k.moe_w1 = sb("moe_w1", [P, NE, CB, FF])
            k.moe_w2 = sb("moe_w2", [P, NE, FB, C])
            k.moe_loaded = ctx.enter_context(nc.semaphore("moe_loaded"))
            with nc.Block() as block:
                @block.sync
                def _(sp):
                    sp.dma_start(k.moe_w1[:], d["moe_W1"].rearrange("e (k p) f -> p (e k) f", p=P)
                                 ).then_inc(k.moe_loaded, 16)
                    sp.dma_start(k.moe_w2[:], d["moe_W2"].rearrange("e (k p) f -> p (e k) f", p=P)
                                 ).then_inc(k.moe_loaded, 16)
            with cleared(nc):
                route_phase(nc, k, d)
            with cleared(nc):
                expert_phase(nc, k, d, out.rearrange("n p c -> (n p) c"))
            return
        stored = ctx.enter_context(nc.semaphore("x_stored"))
        with nc.Block() as block:
            @block.sync
            def _(sp):
                sp.dma_start(out.rearrange("n p c -> p n c"), k.x[:]).then_inc(stored, 16)
                sp.wait_ge(stored, 16)


def lay_out(inp):
    import numpy as np
    f = lambda n: np.asarray(inp[n])
    B = f("L0_c").shape[0]
    columns = lambda v: np.asarray(v).reshape(-1, P).T
    A, R, E = "L0_attn_", "L0_ffn_", "L1_ffn_"
    cols = {"b_ret": f(A + "b_ret"), "ln1_scale": f(A + "ln1_scale"), "ln1_bias": f(A + "ln1_bias"), "b1": f(A + "b1"),
            "mu_r": f(R + "mu_r"), "mu_k": f(R + "mu_k"), "bq": f(E + "bq"), "bk": f(E + "bk"),
            "l1_ln1_g": f(E + "ln1_g"), "l1_ln1_b": f(E + "ln1_b"),
            "router_b": np.broadcast_to(f(E + "router_b"), (P,))}
    rows = {"ln1_scale": f(A + "ln1_scale"), "ln1_bias": f(A + "ln1_bias"), "b2": f(A + "b2"),
            "ln2_scale": f(A + "ln2_scale"), "ln2_bias": f(A + "ln2_bias"), "bv": f(E + "bv"), "bo": f(E + "bo"),
            "l1_ln1_g": f(E + "ln1_g"), "l1_ln1_b": f(E + "ln1_b"), "router_w": f(E + "router_w")[:, 0],
            "l1_ln2_g": f(E + "ln2_g"), "l1_ln2_b": f(E + "ln2_b")}
    angle = np.arange(T, dtype=np.float32)[:, None] / np.power(
        np.float32(10000.0), np.arange(0, HD, 2, dtype=np.float32)[None, :] / np.float32(HD))
    angle = angle.astype(np.float32).reshape(J, P, HD // 2).transpose(1, 0, 2)
    cos = np.concatenate([np.cos(angle), np.cos(angle)], axis=2)
    sin = np.concatenate([-np.sin(angle), np.sin(angle)], axis=2)
    arrays = {
        "x": f("L0_attn_x").reshape(B * J, P, C),
        "cT0": f("L0_c").T, "cT1": f("L1_c").T, "wmod0": f("L0_wmod"), "wmod1": f("L1_wmod"),
        "cols": np.concatenate([columns(cols[n]) for n in COLS], axis=1),
        "rows": np.stack([rows[n] for n in ROWS]),
        "mask": np.triu(np.full((P, P), -1e9, np.float32), 1),
        "w_out": f("L1_attn_w_out"), "Wq": f(E + "Wq"), "Wk": f(E + "Wk"), "Wv": f(E + "Wv"), "Wo": f(E + "Wo"),
        "moe_W1": f(E + "W1"), "moe_W2": f(E + "W2"), "moe_b1_rows": f(E + "b1"), "moe_b2_rows": f(E + "b2"),
        "before": np.triu(np.ones((P, P), np.float32), 1),
        "experts": np.broadcast_to(np.arange(NE, dtype=np.float32), (P, NE)),
        "ids": np.arange(B * T, dtype=np.int32).reshape(B * J, P).T,
        "lane": np.arange(P, dtype=np.float32)[:, None],
        "pad_ids": (B * T + np.arange(P, dtype=np.int32))[:, None],
        "number": np.arange(B * J + NE, dtype=np.float32)[None, :],
        "ident": np.eye(P, dtype=np.float32),
        "W_rT": f(R + "W_r").T, "W_kT": f(R + "W_k").T, "W_vT": f(R + "W_v").T,
        "w_qkv": f("L1_attn_w_qkv"), "cos": cos, "sin": sin,
        "W_ret": f(A + "W_ret"), "W1": f(A + "W1"), "W2": f(A + "W2"),
    }
    return {n: np.ascontiguousarray(a) for n, a in arrays.items()}


def kernel(**inputs):
    import numpy as np
    import concourse.bacc as bacc
    from concourse.bass_utils import run_bass_kernel_spmd

    arrays = lay_out(inputs)
    B = arrays["cT0"].shape[1]
    nc = bacc.Bacc("TRN2", target_bir_lowering=False, num_devices=1)
    d = {n: nc.dram_tensor(f"in_{n}", a.shape, mybir.dt.from_np(a.dtype), kind="ExternalInput").ap()
         for n, a in arrays.items()}
    out = nc.dram_tensor("out", (B * J, P, C), F32, kind="ExternalOutput").ap()
    build(nc, d, out, B)
    result = run_bass_kernel_spmd(nc, [{f"in_{n}": a for n, a in arrays.items()}], core_ids=[0])
    return result.results[0]["out"].reshape(B, T, C)
```

```python
import concourse.bass as bass
from concourse import mybir
from concourse.alu_op_type import AluOpType as ALU
from contextlib import ExitStack

F32 = mybir.dt.float32
BF16 = mybir.dt.bfloat16
ACT = mybir.ActivationFunctionType
AX = mybir.AxisListType

P = 128
C = 256
CB = C // P
T = 512
J = T // P
FF = 1024
FB = FF // P
NE = 4
NH = 16
HD = C // NH
EPS = 1e-5
KS = 3 * 2 * HD
RING = 4
G4 = 4

COLS = {}
for _name, _n in (("b_ret", 2), ("ln1_scale", 2), ("ln1_bias", 2), ("b1", 8), ("mu_r", 2), ("mu_k", 2),
                  ("bq", 2), ("bk", 2), ("l1_ln1_g", 2), ("l1_ln1_b", 2), ("router_b", 1)):
    COLS[_name] = sum(n for _, n in COLS.values()) if COLS else 0
    COLS[_name] = (COLS[_name], _n)
NCOLS = sum(n for _, n in COLS.values())
ROWS = ("ln1_scale", "ln1_bias", "b2", "ln2_scale", "ln2_bias",
        "bv", "bo", "l1_ln1_g", "l1_ln1_b", "router_w", "l1_ln2_g", "l1_ln2_b")
SA, CA, GA, SB, CBM, GB = range(6)
MROWS = ((0, GA), (0, GB), (1, GA), (1, GB), (1, CBM), (1, SB))


class Core:
    pass


def col(k, name, i=0):
    first, _ = COLS[name]
    return k.cols[:, first + i:first + i + 1]


def over_tiles(ap):
    return ap.unsqueeze(1).to_broadcast([P, J, C])


def setup_phase(nc, k, d):
    with ExitStack() as ctx:
        sb = lambda n, s, t=F32: ctx.enter_context(nc.sbuf_tensor("set_" + n, s, t))
        sem = lambda n: nc.alloc_semaphore("set_" + n)
        B = k.B
        wmod = [sb(f"wmod{l}", [P, CB, 6 * C]) for l in range(2)]
        cT = sb("cT", [P, 2, CB, B])
        sg = sb("sg", [P, 2, CB, B])
        rowmod = sb("rowmod", [B, len(MROWS), C])
        mask = sb("mask", [P, P])
        t_sign = sb("t_sign", [B, C])
        t_abs = sb("t_abs", [B, C])
        colps = [ctx.enter_context(nc.psum_tensor(f"colps{l}", [P, 12, B], F32)) for l in range(2)]
        rowps = [ctx.enter_context(nc.psum_tensor(f"rowps{i}", [B, C], F32)) for i in range(len(MROWS))]
        loaded, c_loaded, sig_done, silu_done = sem("loaded"), sem("c_loaded"), sem("sig_done"), sem("silu_done")
        colmod_ready, rowmod_ready = sem("colmod_ready"), sem("rowmod_ready")
        cols_done, step, rows_done, stored = sem("cols_done"), sem("step"), sem("rows_done"), sem("stored")
        block = ctx.enter_context(nc.Block())

        @block.sync
        def _(sp):
            for l in range(2):
                sp.dma_start(cT[:, l], d[f"cT{l}"].rearrange("(k p) b -> p k b", p=P)).then_inc(c_loaded, 16)
            for l in range(2):
                sp.dma_start(wmod[l][:], d[f"wmod{l}"].rearrange("(k p) n -> p k n", p=P)).then_inc(loaded, 16)
            sp.dma_start(k.cols[:], d["cols"]).then_inc(loaded, 16)
            sp.dma_start(k.ident[:], d["ident"]).then_inc(loaded, 16)
            sp.dma_start(mask[:], d["mask"]).then_inc(loaded, 16)
            sp.wait_ge(rows_done, 1)
            sp.dma_start(k.mrows_dram.rearrange("r b c -> b r c"), rowmod[:]).then_inc(stored, 16)
            sp.wait_ge(stored, 16)
            sp.wait_ge(loaded, 80)

        @block.scalar
        def _(act):
            act.wait_ge(c_loaded, 32)
            nc.scalar.activation(sg[:], cT[:], ACT.Sigmoid).then_inc(sig_done, 1)

        @block.tensor
        def _(pe):
            pe.wait_ge(loaded, 80)
            pe.wait_ge(silu_done, 1)
            for l in range(2):
                for m in range(12):
                    for kb in range(CB):
                        last = nc.tensor.matmul(colps[l][:, m, :], wmod[l][:, kb, m * P:(m + 1) * P], sg[:, l, kb, :],
                                                start=(kb == 0), stop=(kb == CB - 1))
            last.then_inc(colmod_ready, 1)
            for i, (l, part) in enumerate(MROWS):
                for kb in range(CB):
                    last = nc.tensor.matmul(rowps[i][:], sg[:, l, kb, :], wmod[l][:, kb, part * C:(part + 1) * C],
                                            start=(kb == 0), stop=(kb == CB - 1))
            last.then_inc(rowmod_ready, 1)

        @block.vector
        def _(dve):
            dve.wait_ge(loaded, 80)
            dve.wait_ge(sig_done, 1)
            nc.vector.tensor_tensor(sg[:], sg[:], cT[:], ALU.mult).then_inc(silu_done, 1)
            dve.wait_ge(colmod_ready, 1)
            for l in range(2):
                for m in range(12):
                    plus = 1.0 if m // 2 in (CA, CBM) else 0.0
                    nc.vector.tensor_scalar(k.mod[:, l, m, :], colps[l][:, m, :], plus, None, ALU.add)
            nc.vector.tensor_copy(k.ident_bf[:], k.ident[:])
            nc.vector.tensor_copy(k.mask_bf[:], mask[:])
            nc.vector.memset(k.half[:], 0.5).then_inc(cols_done, 1)
            dve.wait_ge(rowmod_ready, 1)
            steps = [0]

            def follow(instruction):
                steps[0] += 1
                instruction.then_inc(step, 1)
                dve.wait_ge(step, steps[0])

            for i, (l, part) in enumerate(MROWS):
                if part in (GA, GB):
                    follow(nc.vector.tensor_scalar(t_sign[:], rowps[i][:], 0.0, 2.0, ALU.is_ge, ALU.mult))
                    follow(nc.vector.tensor_scalar(t_sign[:], t_sign[:], -1.0, None, ALU.add))
                    follow(nc.vector.tensor_tensor(t_abs[:], t_sign[:], rowps[i][:], ALU.mult))
                    follow(nc.vector.scalar_tensor_tensor(rowmod[:, i, :], t_abs[:], 0.25, t_sign[:],
                                                          ALU.max, ALU.mult))
                else:
                    nc.vector.tensor_scalar(rowmod[:, i, :], rowps[i][:], 1.0 if part == CBM else 0.0, None, ALU.add)
            nc.vector.tensor_copy(t_sign[:], t_abs[:]).then_inc(rows_done, 1)


class Norm:

    def __init__(self, nc, ctx, name):
        self.stats = ctx.enter_context(nc.sbuf_tensor(f"{name}_stats", [P, J, 6], F32))
        self.mv = ctx.enter_context(nc.sbuf_tensor(f"{name}_mv", [P, J, 2], F32))
        self.pause = ctx.enter_context(nc.sbuf_tensor(f"{name}_pause", [P, 1], F32))
        self.ve = ctx.enter_context(nc.sbuf_tensor(f"{name}_ve", [P, J], F32))
        self.rstd = ctx.enter_context(nc.sbuf_tensor(f"{name}_rstd", [P, J], F32))
        self.stats_ready = nc.alloc_semaphore(f"{name}_stats_ready")
        self.mv_ready = nc.alloc_semaphore(f"{name}_mv_ready")
        self.ve_ready = nc.alloc_semaphore(f"{name}_ve_ready")
        self.rstd_ready = nc.alloc_semaphore(f"{name}_rstd_ready")

    def moments(self, nc, dve, tile, b):
        for j in range(J):
            last = nc.vector.bn_stats(self.stats[:, j, :], tile(j))
        last.then_inc(self.stats_ready, 1)
        dve.wait_ge(self.stats_ready, b + 1)
        nc.vector.memset(self.pause[:], 0.0)
        for j in range(J):
            last = nc.vector.bn_aggr(self.mv[:, j, :], self.stats[:, j, :])
        last.then_inc(self.mv_ready, 1)

    def rsqrt(self, nc, k, pool, b):
        pool.wait_ge(self.mv_ready, b + 1)
        nc.gpsimd.tensor_tensor(self.ve[:], self.mv[:, :, 1], k.eps[:], ALU.add).then_inc(self.ve_ready, 1)
        pool.wait_ge(self.ve_ready, b + 1)
        nc.gpsimd.tensor_tensor(self.rstd[:], self.ve[:], k.minus_half[:], ALU.pow).then_inc(self.rstd_ready, 1)

    def apply(self, nc, dve, out, tile, b):
        dve.wait_ge(self.rstd_ready, b + 1)
        for j in range(J):
            last = nc.vector.tensor_scalar(out[:, j, :], tile(j), self.mv[:, j, 0:1], self.rstd[:, j:j + 1],
                                           ALU.subtract, ALU.mult)
        return last


def to_channels(nc, k, out, z):
    for cb in range(CB):
        for j in range(J):
            last = nc.tensor.transpose(out[:, cb, j * P:(j + 1) * P], z[:, j, cb * P:(cb + 1) * P], k.ident[:])
    return last


def retention_phase(nc, k, d):
    with ExitStack() as ctx:
        sb = lambda n, s, t=F32: ctx.enter_context(nc.sbuf_tensor("ret_" + n, s, t))
        sem = lambda n: nc.alloc_semaphore("ret_" + n)
        B = k.B
        w_ret = sb("w_ret", [P, CB, C])
        w1 = sb("w1", [P, CB, FF])
        w2 = sb("w2", [P, FB, C])
        rowb = {n: sb(f"rowb_{n}", [P, C]) for n in ("ln1_scale", "ln1_bias", "b2", "ln2_scale", "ln2_bias")}
        hbias = sb("hbias", [P, C])
        gate = sb("gate", [P, C])
        gate_scale = sb("gate_scale", [P, C])
        gate_bias = sb("gate_bias", [P, C])
        half_b_ret = sb("half_b_ret", [P, CB])
        z0 = sb("z0", [P, J, C])
        hT = sb("hT", [P, CB, T])
        sT = sb("sT", [P, CB, T])
        tT = sb("tT", [P, CB, T])
        z1 = sb("z1", [P, J, C])
        h1T = sb("h1T", [P, CB, T])
        h1b = sb("h1b", [P, J, C])
        gT = sb("gT", [P, FB, T])
        t2 = sb("t2", [P, J, C])
        ln0, ln1, ln2 = (Norm(nc, ctx, "ret_" + n) for n in ("ln0", "ln1", "ln2"))
        ps = lambda n, s: ctx.enter_context(nc.psum_tensor("ret_" + n, s, F32))
        psA = ps("psA", [P, 2, T])
        psB = ps("psB", [P, 2, T])
        psF = ps("psF", [P, 2, T])
        psY = ps("psY", [P, J, C])
        w_ret_loaded = sem("w_ret_loaded")
        weights, rows, x_loaded, gate_loaded = sem("weights"), sem("rows"), sem("x_loaded"), sem("gate_loaded")
        init, hbias_done = sem("init"), sem("hbias_done")
        z0_done, zT_done, hT_done, pre_done = sem("z0_done"), sem("zT_done"), sem("hT_done"), sem("pre_done")
        tanh_done, s_done, scan_done, tT_done = sem("tanh_done"), sem("s_done"), sem("scan_done"), sem("tT_done")
        tok_done, z1_done, z1T_done, h1T_done = sem("tok_done"), sem("z1_done"), sem("z1T_done"), sem("h1T_done")
        h1g_done, h1b_done, ffn1_done, gelu_done = sem("h1g_done"), sem("h1b_done"), sem("ffn1_done"), sem("gelu_done")
        y_done, t2_done, z2_done, gate_done = sem("y_done"), sem("t2_done"), sem("z2_done"), sem("gate_done")
        zg_done, out_done, x_done = sem("zg_done"), sem("out_done"), sem("x_done")
        block = ctx.enter_context(nc.Block())

        @block.sync
        def _(sp):
            def load_x(b):
                sp.dma_start(k.x[:, bass.ds(b * J, J), :],
                             d["x"][bass.ds(b * J, J)].rearrange("j p c -> p j c")).then_inc(x_loaded, 16)

            def load_gate(b):
                sp.dma_start(gate[:], k.mrows_dram[0, b].partition_broadcast(P)).then_inc(gate_loaded, 16)

            load_x(0)
            sp.dma_start(w_ret[:], d["W_ret"].rearrange("(k p) n -> p k n", p=P)).then_inc(w_ret_loaded, 16)
            for n, ap in rowb.items():
                sp.dma_start(ap[:], d["rows"][ROWS.index(n)].partition_broadcast(P)).then_inc(rows, 16)
            for ap, src in ((w1, "W1"), (w2, "W2")):
                sp.dma_start(ap[:], d[src].rearrange("(k p) n -> p k n", p=P)).then_inc(weights, 16)
            sp.wait_ge(x_loaded, 16)
            load_x(1)
            load_gate(0)
            with sp.Fori(1, B - 1) as b:
                sp.wait_ge(x_loaded, 16 * b + 16)
                load_x(b + 1)
                sp.wait_ge(gate_done, b)
                load_gate(b)
            sp.wait_ge(gate_done, B - 1)
            load_gate(B - 1)

        @block.vector
        def _(dve):
            def norm0(b):
                dve.wait_ge(x_loaded, 16 * b + 16)
                tile = lambda j: k.x[:, b * J + j, :]
                ln0.moments(nc, dve, tile, b)
                dve.wait_ge(zT_done, b)
                ln0.apply(nc, dve, z0, tile, b).then_inc(z0_done, 1)

            def retention(b):
                dve.wait_ge(s_done, b + 1)
                dve.wait_ge(tok_done, b)
                for cb in range(CB):
                    last = nc.vector.tensor_tensor_scan(tT[:, cb, :], k.half[:], sT[:, cb, :], 0.0, ALU.mult, ALU.add)
                last.then_inc(scan_done, 1)
                dve.wait_ge(scan_done, b + 1)
                nc.vector.scalar_tensor_tensor(tT[:], tT[:], 0.5, hT[:], ALU.mult, ALU.add).then_inc(tT_done, 1)

            def norm1(b):
                dve.wait_ge(tok_done, b + 1)
                tile = lambda j: psA[:, j // 2, (j % 2) * C:(j % 2 + 1) * C]
                ln1.moments(nc, dve, tile, b)
                dve.wait_ge(z1T_done, b)
                dve.wait_ge(h1b_done, b)
                ln1.apply(nc, dve, z1, tile, b).then_inc(z1_done, 1)

            def norm2(b):
                dve.wait_ge(y_done, J * b + J)
                dve.wait_ge(h1b_done, b + 1)
                dve.wait_ge(x_done, b)
                nc.vector.tensor_tensor(t2[:], psY[:], h1b[:], ALU.add).then_inc(t2_done, 1)
                dve.wait_ge(t2_done, b + 1)
                tile = lambda j: t2[:, j, :]
                ln2.moments(nc, dve, tile, b)
                ln2.apply(nc, dve, t2, tile, b).then_inc(z2_done, 1)

            def residual(b):
                dve.wait_ge(out_done, b + 1)
                xb = k.x[:, bass.ds(b * J, J), :]
                nc.vector.tensor_tensor(xb, xb, t2[:], ALU.add).then_inc(x_done, 1)

            def step(b, last=False):
                retention(b + 1)
                norm1(b + 1)
                if not last:
                    norm0(b + 2)
                norm2(b)
                residual(b)

            norm0(0)
            dve.wait_ge(rows, 16 * len(rowb))
            nc.vector.tensor_scalar(half_b_ret[:], k.cols[:, COLS["b_ret"][0]:COLS["b_ret"][0] + CB], 0.5, None,
                                    ALU.mult)
            nc.vector.tensor_tensor(hbias[:], rowb["ln1_bias"][:], rowb["b2"][:], ALU.add).then_inc(init, 1)
            retention(0)
            norm1(0)
            norm0(1)
            step(0)
            with dve.Fori(1, B - 2) as b:
                step(b)
            step(B - 2, last=True)
            norm2(B - 1)
            residual(B - 1)

        @block.gpsimd
        def _(pool):
            def add_bias(b):
                pool.wait_ge(z1_done, b + 1)
                pool.wait_ge(t2_done, b)
                nc.gpsimd.tensor_tensor(h1b[:], z1[:], over_tiles(rowb["ln1_scale"][:]), ALU.mult).then_inc(h1g_done, 1)
                pool.wait_ge(h1g_done, b + 1)
                nc.gpsimd.tensor_tensor(h1b[:], h1b[:], over_tiles(hbias[:]), ALU.add).then_inc(h1b_done, 1)

            def gates(b):
                pool.wait_ge(gate_loaded, 16 * b + 16)
                pool.wait_ge(out_done, b)
                nc.gpsimd.tensor_tensor(gate_scale[:], gate[:], rowb["ln2_scale"][:], ALU.mult)
                nc.gpsimd.tensor_tensor(gate_bias[:], gate[:], rowb["ln2_bias"][:], ALU.mult).then_inc(gate_done, 1)

            def scale_out(b):
                pool.wait_ge(z2_done, b + 1)
                pool.wait_ge(gate_done, b + 1)
                nc.gpsimd.tensor_tensor(t2[:], t2[:], over_tiles(gate_scale[:]), ALU.mult).then_inc(zg_done, 1)
                pool.wait_ge(zg_done, b + 1)
                nc.gpsimd.tensor_tensor(t2[:], t2[:], over_tiles(gate_bias[:]), ALU.add).then_inc(out_done, 1)


            def step(b, last=False):
                gates(b)
                ln1.rsqrt(nc, k, pool, b + 1)
                if not last:
                    ln0.rsqrt(nc, k, pool, b + 2)
                ln2.rsqrt(nc, k, pool, b)
                scale_out(b)
                add_bias(b + 1)

            ln0.rsqrt(nc, k, pool, 0)
            pool.wait_ge(init, 1)
            ln1.rsqrt(nc, k, pool, 0)
            ln0.rsqrt(nc, k, pool, 1)
            add_bias(0)
            step(0)
            with pool.Fori(1, B - 2) as b:
                step(b)
            step(B - 2, last=True)
            gates(B - 1)
            ln2.rsqrt(nc, k, pool, B - 1)
            scale_out(B - 1)

        @block.tensor
        def _(pe):
            def transpose_h(b):
                pe.wait_ge(z0_done, b + 1)
                pe.wait_ge(z1_done, b)
                to_channels(nc, k, psA, z0).then_inc(zT_done, 1)

            def retention_product(b):
                pe.wait_ge(hT_done, b + 1)
                pe.wait_ge(h1T_done, b)
                for db in range(CB):
                    for cb in range(CB):
                        last = nc.tensor.matmul(psB[:, db, :], w_ret[:, cb, db * P:(db + 1) * P], hT[:, cb, :],
                                                start=(cb == 0), stop=(cb == CB - 1))
                last.then_inc(pre_done, 1)

            def transpose_back(b):
                pe.wait_ge(tT_done, b + 1)
                for j in range(J):
                    for cb in range(CB):
                        last = nc.tensor.transpose(psA[:, j // 2, (j % 2) * C + cb * P:(j % 2) * C + (cb + 1) * P],
                                                   tT[:, cb, j * P:(j + 1) * P], k.ident[:])
                last.then_inc(tok_done, 1)

            def transpose_h1(b):
                pe.wait_ge(z1_done, b + 1)
                pe.wait_ge(tanh_done, b + 1)
                to_channels(nc, k, psB, z1).then_inc(z1T_done, 1)

            def hidden(b, blocks):
                for f in blocks:
                    if f == 0:
                        pe.wait_ge(h1T_done, b + 1)
                    pe.wait_ge(gelu_done, FB * b + max(f - 1, 0))
                    for cb in range(CB):
                        last = nc.tensor.matmul(psF[:, f % 2, :], w1[:, cb, f * P:(f + 1) * P], h1T[:, cb, :],
                                                start=(cb == 0), stop=(cb == CB - 1))
                    last.then_inc(ffn1_done, 1)

            def output(b, tiles):
                for j in tiles:
                    if j == 0:
                        pe.wait_ge(gelu_done, FB * b + FB)
                        pe.wait_ge(t2_done, b)
                    for f in range(FB):
                        last = nc.tensor.matmul(psY[:, j, :], gT[:, f, j * P:(j + 1) * P], w2[:, f, :],
                                                start=(f == 0), stop=(f == FB - 1))
                    last.then_inc(y_done, 1)

            transpose_h(0)
            pe.wait_ge(w_ret_loaded, 16)
            retention_product(0)
            transpose_back(0)
            transpose_h1(0)
            pe.wait_ge(weights, 32)

            def step(b):
                hidden(b, range(0, 2))
                transpose_h(b + 1)
                hidden(b, range(2, 4))
                retention_product(b + 1)
                hidden(b, range(4, 8))
                transpose_back(b + 1)
                output(b, range(0, 2))
                transpose_h1(b + 1)
                output(b, range(2, 4))

            step(0)
            with pe.Fori(1, B - 1) as b:
                step(b)
            hidden(B - 1, range(FB))
            output(B - 1, range(J))

        @block.scalar
        def _(act):
            def modulate(b):
                act.wait_ge(zT_done, b + 1)
                act.wait_ge(tT_done, b)
                for cb in range(CB):
                    last = nc.scalar.activation(hT[:, cb, :], psA[:, cb, :], ACT.Identity,
                                                scale=k.mod[:, 0, CA * CB + cb, bass.ds(b, 1)],
                                                bias=k.mod[:, 0, SA * CB + cb, bass.ds(b, 1)])
                last.then_inc(hT_done, 1)

            def sigmoid(b):
                act.wait_ge(pre_done, b + 1)
                for cb in range(CB):
                    last = nc.scalar.activation(sT[:, cb, :], psB[:, cb, :], ACT.Tanh, scale=0.5,
                                                bias=half_b_ret[:, cb:cb + 1])
                last.then_inc(tanh_done, 1)
                act.wait_ge(tanh_done, b + 1)
                nc.scalar.activation(sT[:], sT[:], ACT.Copy, scale=0.5, bias=0.5).then_inc(s_done, 1)

            def scale_h1(b):
                act.wait_ge(z1T_done, b + 1)
                act.wait_ge(ffn1_done, FB * b)
                for cb in range(CB):
                    last = nc.scalar.activation(h1T[:, cb, :], psB[:, cb, :], ACT.Identity,
                                                scale=col(k, "ln1_scale", cb), bias=col(k, "ln1_bias", cb))
                last.then_inc(h1T_done, 1)

            def gelu(b, blocks):
                for f in blocks:
                    if f == 0:
                        act.wait_ge(y_done, J * b)
                    act.wait_ge(ffn1_done, FB * b + f + 1)
                    nc.scalar.activation(gT[:, f, :], psF[:, f % 2, :], ACT.Gelu_apprx_tanh,
                                         bias=col(k, "b1", f)).then_inc(gelu_done, 1)

            modulate(0)
            act.wait_ge(init, 1)
            sigmoid(0)
            scale_h1(0)

            def step(b):
                gelu(b, range(0, 2))
                modulate(b + 1)
                gelu(b, range(2, 4))
                sigmoid(b + 1)
                gelu(b, range(4, 8))
                scale_h1(b + 1)

            step(0)
            with act.Fori(1, B - 1) as b:
                step(b)
            gelu(B - 1, range(FB))


def channel_mix_phase(nc, k, d):
    with ExitStack() as ctx:
        sb = lambda n, s, t=F32: ctx.enter_context(nc.sbuf_tensor("mix_" + n, s, t))
        sem = lambda n: nc.alloc_semaphore("mix_" + n)
        ps = lambda n, s: ctx.enter_context(nc.psum_tensor("mix_" + n, s, F32))
        B = k.B
        wr, wk, wv = sb("wr", [P, CB, C]), sb("wk", [P, CB, C]), sb("wv", [P, CB, C])
        gate = sb("gate", [P, C])
        z = sb("z", [P, J, C])
        hT = sb("hT", [P, CB, 1 + T])
        dT = sb("dT", [P, CB, T])
        xkT, xrT = sb("xkT", [P, CB, T]), sb("xrT", [P, CB, T])
        kT = sb("kT", [P, CB, T])
        r = sb("r", [P, J, C])
        o = sb("o", [P, J, C])
        ln = Norm(nc, ctx, "mix_ln")
        psA, psK = ps("psA", [P, CB, T]), ps("psK", [P, CB, T])
        psR, psV = ps("psR", [P, J, C]), ps("psV", [P, J, C])
        weights, gate_loaded, zero_done = sem("weights"), sem("gate_loaded"), sem("zero_done")
        z_done, zT_done, hT_done, d_done = sem("z_done"), sem("zT_done"), sem("hT_done"), sem("d_done")
        xk_done, xr_done, k_done, relu_done = sem("xk_done"), sem("xr_done"), sem("k_done"), sem("relu_done")
        sq_done, r_done, sig_done, rg_done = sem("sq_done"), sem("r_done"), sem("sig_done"), sem("rg_done")
        v_done, o_done, x_done = sem("v_done"), sem("o_done"), sem("x_done")
        block = ctx.enter_context(nc.Block())

        @block.sync
        def _(sp):
            for ap, src in ((wr, "W_rT"), (wk, "W_kT"), (wv, "W_vT")):
                sp.dma_start(ap[:], d[src].rearrange("(k p) n -> p k n", p=P)).then_inc(weights, 16)
            sp.dma_start(gate[:], k.mrows_dram[1, 0].partition_broadcast(P)).then_inc(gate_loaded, 16)
            with sp.Fori(1, B) as b:
                sp.wait_ge(rg_done, b)
                sp.dma_start(gate[:], k.mrows_dram[1, b].partition_broadcast(P)).then_inc(gate_loaded, 16)

        @block.vector
        def _(dve):
            def norm(b):
                tile = lambda j: k.x[:, b * J + j, :]
                ln.moments(nc, dve, tile, b)
                dve.wait_ge(zT_done, b)
                ln.apply(nc, dve, z, tile, b).then_inc(z_done, 1)

            def mix(b):
                dve.wait_ge(hT_done, b + 1)
                now, before = hT[:, :, 1:1 + T], hT[:, :, 0:T]
                nc.vector.tensor_tensor(dT[:], now, before, ALU.subtract).then_inc(d_done, 1)
                dve.wait_ge(d_done, b + 1)
                dve.wait_ge(k_done, b)
                for cb in range(CB):
                    last = nc.vector.scalar_tensor_tensor(xkT[:, cb, :], dT[:, cb, :], col(k, "mu_k", cb),
                                                          hT[:, cb, 0:T], ALU.mult, ALU.add)
                last.then_inc(xk_done, 1)
                dve.wait_ge(r_done, b)
                for cb in range(CB):
                    last = nc.vector.scalar_tensor_tensor(xrT[:, cb, :], dT[:, cb, :], col(k, "mu_r", cb),
                                                          hT[:, cb, 0:T], ALU.mult, ALU.add)
                last.then_inc(xr_done, 1)

            def output(b):
                dve.wait_ge(v_done, b + 1)
                dve.wait_ge(rg_done, b + 1)
                dve.wait_ge(x_done, b)
                nc.vector.tensor_tensor(o[:], psV[:], r[:], ALU.mult).then_inc(o_done, 1)
                dve.wait_ge(o_done, b + 1)
                xb = k.x[:, bass.ds(b * J, J), :]
                nc.vector.tensor_tensor(xb, xb, o[:], ALU.add).then_inc(x_done, 1)

            nc.vector.memset(hT[:, :, 0:1], 0.0).then_inc(zero_done, 1)
            dve.wait_ge(zero_done, 1)
            norm(0)
            mix(0)
            norm(1)
            mix(1)
            norm(2)
            output(0)
            with dve.Fori(1, B - 2) as b:
                mix(b + 1)
                norm(b + 2)
                output(b)
            mix(B - 1)
            output(B - 2)
            output(B - 1)

        @block.gpsimd
        def _(pool):
            def gate_r(b):
                pool.wait_ge(sig_done, b + 1)
                pool.wait_ge(gate_loaded, 16 * b + 16)
                nc.gpsimd.tensor_tensor(r[:], r[:], over_tiles(gate[:]), ALU.mult).then_inc(rg_done, 1)

            for b in range(3):
                ln.rsqrt(nc, k, pool, b)
            gate_r(0)
            with pool.Fori(1, B - 2) as b:
                ln.rsqrt(nc, k, pool, b + 2)
                gate_r(b)
            gate_r(B - 2)
            gate_r(B - 1)

        @block.tensor
        def _(pe):
            def transpose_h(b):
                pe.wait_ge(z_done, b + 1)
                pe.wait_ge(hT_done, b)
                to_channels(nc, k, psA, z).then_inc(zT_done, 1)

            def key(b):
                pe.wait_ge(xk_done, b + 1)
                pe.wait_ge(relu_done, b)
                for db in range(CB):
                    for cb in range(CB):
                        last = nc.tensor.matmul(psK[:, db, :], wk[:, cb, db * P:(db + 1) * P], xkT[:, cb, :],
                                                start=(cb == 0), stop=(cb == CB - 1))
                last.then_inc(k_done, 1)

            def by_tokens(out, xT, w):
                for j in range(J):
                    for cb in range(CB):
                        last = nc.tensor.matmul(out[:, j, :], xT[:, cb, j * P:(j + 1) * P], w[:, cb, :],
                                                start=(cb == 0), stop=(cb == CB - 1))
                return last

            def receptance(b):
                pe.wait_ge(xr_done, b + 1)
                pe.wait_ge(sig_done, b)
                by_tokens(psR, xrT, wr).then_inc(r_done, 1)

            def value(b):
                pe.wait_ge(sq_done, b + 1)
                pe.wait_ge(o_done, b)
                by_tokens(psV, kT, wv).then_inc(v_done, 1)

            pe.wait_ge(weights, 48)
            transpose_h(0)

            def step(b):
                key(b)
                transpose_h(b + 1)
                receptance(b)
                value(b)

            step(0)
            with pe.Fori(1, B - 1) as b:
                step(b)
            key(B - 1)
            receptance(B - 1)
            value(B - 1)

        @block.scalar
        def _(act):
            def modulate(b):
                act.wait_ge(zT_done, b + 1)
                act.wait_ge(xr_done, b)
                for cb in range(CB):
                    last = nc.scalar.activation(hT[:, cb, 1:1 + T], psA[:, cb, :], ACT.Identity,
                                                scale=k.mod[:, 0, CBM * CB + cb, bass.ds(b, 1)],
                                                bias=k.mod[:, 0, SB * CB + cb, bass.ds(b, 1)])
                last.then_inc(hT_done, 1)

            def activate(b):
                act.wait_ge(k_done, b + 1)
                act.wait_ge(v_done, b)
                nc.scalar.activation(kT[:], psK[:], ACT.Relu).then_inc(relu_done, 1)
                act.wait_ge(relu_done, b + 1)
                nc.scalar.activation(kT[:], kT[:], ACT.Square).then_inc(sq_done, 1)
                act.wait_ge(r_done, b + 1)
                act.wait_ge(o_done, b)
                nc.scalar.activation(r[:], psR[:], ACT.Sigmoid).then_inc(sig_done, 1)

            act.wait_ge(zero_done, 1)
            modulate(0)
            modulate(1)
            activate(0)
            with act.Fori(1, B - 1) as b:
                modulate(b + 1)
                activate(b)
            activate(B - 1)


def rotary_qkv_phase(nc, k, d):
    with ExitStack() as ctx:
        sb = lambda n, s, t=F32: ctx.enter_context(nc.sbuf_tensor("rot_" + n, s, t))
        sem = lambda n: nc.alloc_semaphore("rot_" + n)
        ps = lambda n, s: ctx.enter_context(nc.psum_tensor("rot_" + n, s, F32))
        B = k.B
        w = sb("w_qkv", [P, CB, 3 * C])
        cos, sin = sb("cos", [P, J, HD]), sb("sin", [P, J, HD])
        z = sb("z", [P, J, C])
        hT = [sb(f"hT{i}", [P, CB, T]) for i in range(2)]
        by_cos, by_sin = sb("by_cos", [P, 2, 2 * C]), sb("by_sin", [P, 2, 2 * C])
        rot = [sb(f"rot{i}", [P, J, 2 * C]) for i in range(2)]
        rest = sb("rest", [P, 2, T])
        parts = [sb(f"parts{i}", [P, 3, 2 * CB, T], BF16) for i in range(2)]
        v = [sb(f"v{i}", [P, J, C]) for i in range(2)]
        ln = Norm(nc, ctx, "rot_ln")
        psA = ps("psA", [P, CB, T])
        psQK = ps("psQK", [P, 2, 2 * C])
        psV = ps("psV", [P, 2, T])[:, :, 0:C]
        psT = ps("psT", [P, 2, T])
        weights, z_done, zT_done, hT_done = sem("weights"), sem("z_done"), sem("zT_done"), sem("hT_done")
        qk_done, v_done, prod_done, rot_done = sem("qk_done"), sem("v_done"), sem("prod_done"), sem("rot_done")
        vcopy_done, rT_done, hi_done = sem("vcopy_done"), sem("rT_done"), sem("hi_done")
        rest_done, mid_done, lo_done = sem("rest_done"), sem("mid_done"), sem("lo_done")
        parts_stored = [sem(f"parts_stored{i}") for i in range(2)]
        v_stored = [sem(f"v_stored{i}") for i in range(2)]
        block = ctx.enter_context(nc.Block())
        NB = 2 * CB
        assert NB == J
        rounds = B // 2

        @block.sync
        def _(sp):
            sp.dma_start(w[:], d["w_qkv"].rearrange("(k p) n -> p k n", p=P)).then_inc(weights, 16)
            sp.dma_start(cos[:], d["cos"]).then_inc(weights, 16)
            sp.dma_start(sin[:], d["sin"]).then_inc(weights, 16)
            with sp.Fori(0, rounds) as i:
                for p in range(2):
                    b = 2 * i + p
                    sp.wait_ge(vcopy_done, J * b + J)
                    sp.dma_start(k.v_dram[b], v[p][:]).then_inc(v_stored[p], 16)
                    sp.wait_ge(hi_done, NB * b + NB)
                    sp.wait_ge(mid_done, NB * b + NB)
                    sp.wait_ge(lo_done, NB * b + NB)
                    sp.dma_start(k.parts_dram[b].rearrange("s n p t -> p s n t"), parts[p][:]
                                 ).then_inc(parts_stored[p], 16)
            for p in range(2):
                sp.wait_ge(v_stored[p], 16 * rounds)
                sp.wait_ge(parts_stored[p], 16 * rounds)

        @block.vector
        def _(dve):
            def moments(b):
                ln.moments(nc, dve, lambda j: k.x[:, b * J + j, :], b)

            def normalize(b):
                if not (isinstance(b, int) and b == 0):
                    dve.wait_ge(zT_done, b)
                ln.apply(nc, dve, z, lambda j: k.x[:, b * J + j, :], b).then_inc(z_done, 1)

            def rotate(b, tiles):
                for j in tiles:
                    i = j % 2
                    dve.wait_ge(qk_done, J * b + j + 1)
                    dve.wait_ge(rot_done, J * b + max(j - 1, 0))
                    heads = psQK[:, i, :].rearrange("p (h e) -> p h e", e=HD)
                    nc.vector.tensor_tensor(by_cos[:, i, :].rearrange("p (h e) -> p h e", e=HD), heads,
                                            cos[:, j, :].unsqueeze(1).to_broadcast([P, 2 * NH, HD]), ALU.mult)
                    out = by_sin[:, i, :].rearrange("p (h e) -> p h e", e=HD)
                    H2 = HD // 2
                    for half in range(2):
                        own, other = slice(half * H2, half * H2 + H2), slice(H2 - half * H2, HD - half * H2)
                        last = nc.vector.tensor_tensor(out[:, :, own], heads[:, :, other],
                                                       sin[:, j, own].unsqueeze(1).to_broadcast([P, 2 * NH, H2]),
                                                       ALU.mult)
                    last.then_inc(prod_done, 1)

            def split(b, p, blocks):
                for n in blocks:
                    dve.wait_ge(hi_done, NB * b + n + 1)
                    dve.wait_ge(lo_done, NB * b + max(n - 1, 0))
                    nc.vector.tensor_tensor(rest[:, n % 2, :], psT[:, n % 2, :], parts[p][:, 0, n, :],
                                            ALU.subtract).then_inc(rest_done, 1)

            def round_(i, last=False):
                for p in range(2):
                    b = 2 * i + p
                    for j in range(J):
                        if not (last and p == 1):
                            rotate(b + 1, [j])
                        split(b, p, [j])
                        if j == 0 and not last:
                            moments(b + 2)
                        if j == 1 and not last:
                            normalize(b + 2)

            for b in range(2):
                moments(b)
                normalize(b)
            rotate(0, range(J))
            round_(0)
            with dve.Fori(1, rounds - 1) as i:
                round_(i)
            round_(rounds - 1, last=True)

        @block.gpsimd
        def _(pool):
            def add_rotated(b, p, tiles):
                for j in tiles:
                    pool.wait_ge(prod_done, J * b + j + 1)
                    if j == 0 and not (isinstance(b, int) and b < 2):
                        pool.wait_ge(rT_done, NB * (b - 1))
                    nc.gpsimd.tensor_tensor(rot[p][:, j, :], by_cos[:, j % 2, :], by_sin[:, j % 2, :],
                                            ALU.add).then_inc(rot_done, 1)

            def low_parts(b, p, blocks):
                for n in blocks:
                    pool.wait_ge(mid_done, NB * b + n + 1)
                    nc.gpsimd.tensor_tensor(parts[p][:, 2, n, :], rest[:, n % 2, :], parts[p][:, 1, n, :],
                                            ALU.subtract).then_inc(lo_done, 1)

            def round_(i, last=False):
                for p in range(2):
                    b = 2 * i + p
                    for j in range(J):
                        if not (last and p == 1):
                            add_rotated(b + 1, 1 - p, [j])
                        if j == 1 and not last:
                            ln.rsqrt(nc, k, pool, b + 2)
                        low_parts(b, p, [j])

            for b in range(2):
                ln.rsqrt(nc, k, pool, b)
            add_rotated(0, 0, range(J))
            round_(0)
            with pool.Fori(1, rounds - 1) as i:
                round_(i)
            round_(rounds - 1, last=True)

        @block.tensor
        def _(pe):
            def transpose_h(b):
                pe.wait_ge(z_done, b + 1)
                pe.wait_ge(hT_done, b)
                to_channels(nc, k, psA, z).then_inc(zT_done, 1)

            def project(b, p, tiles):
                for j in tiles:
                    if j == 0:
                        pe.wait_ge(hT_done, b + 1)
                    tok = slice(j * P, (j + 1) * P)
                    pe.wait_ge(prod_done, J * b + max(j - 1, 0))
                    for cb in range(CB):
                        last = nc.tensor.matmul(psQK[:, j % 2, :], hT[p][:, cb, tok], w[:, cb, 0:2 * C],
                                                start=(cb == 0), stop=(cb == CB - 1))
                    last.then_inc(qk_done, 1)
                    pe.wait_ge(vcopy_done, J * b + max(j - 1, 0))
                    for cb in range(CB):
                        last = nc.tensor.matmul(psV[:, j % 2, :], hT[p][:, cb, tok], w[:, cb, 2 * C:3 * C],
                                                start=(cb == 0), stop=(cb == CB - 1))
                    last.then_inc(v_done, 1)

            def transpose_rotated(b, p, blocks):
                for n in blocks:
                    if n == 0:
                        pe.wait_ge(rot_done, J * b + J)
                    pe.wait_ge(rest_done, NB * b + max(n - 1, 0))
                    for j in range(J):
                        last = nc.tensor.transpose(psT[:, n % 2, j * P:(j + 1) * P], rot[p][:, j, n * P:(n + 1) * P],
                                                   k.ident[:])
                    last.then_inc(rT_done, 1)

            def round_(i, last=False):
                for p in range(2):
                    b = 2 * i + p
                    for j in range(J):
                        if not (last and p == 1):
                            project(b + 1, 1 - p, [j])
                        transpose_rotated(b, p, [j])
                        if j == 2 and not last:
                            transpose_h(b + 2)

            pe.wait_ge(weights, 48)
            transpose_h(0)
            transpose_h(1)
            project(0, 0, range(J))
            round_(0)
            with pe.Fori(1, rounds - 1) as i:
                round_(i)
            round_(rounds - 1, last=True)

        @block.scalar
        def _(act):
            def modulate(b, p):
                act.wait_ge(zT_done, b + 1)
                if not (isinstance(b, int) and b < 2):
                    act.wait_ge(v_done, J * (b - 1))
                for cb in range(CB):
                    last = nc.scalar.activation(hT[p][:, cb, :], psA[:, cb, :], ACT.Identity,
                                                scale=k.mod[:, 1, CA * CB + cb, bass.ds(b, 1)],
                                                bias=k.mod[:, 1, SA * CB + cb, bass.ds(b, 1)])
                last.then_inc(hT_done, 1)

            def copy_v(b, i, p, tiles):
                for j in tiles:
                    if j == 0 and not (isinstance(i, int) and i == 0):
                        act.wait_ge(v_stored[p], 16 * i)
                    act.wait_ge(v_done, J * b + j + 1)
                    nc.scalar.activation(v[p][:, j, :], psV[:, j % 2, :], ACT.Copy).then_inc(vcopy_done, 1)

            def split(b, i, p, blocks):
                for n in blocks:
                    if n == 0 and not (isinstance(i, int) and i == 0):
                        act.wait_ge(parts_stored[p], 16 * i)
                    act.wait_ge(rT_done, NB * b + n + 1)
                    nc.scalar.activation(parts[p][:, 0, n, :], psT[:, n % 2, :], ACT.Copy).then_inc(hi_done, 1)
                    act.wait_ge(rest_done, NB * b + n + 1)
                    nc.scalar.activation(parts[p][:, 1, n, :], rest[:, n % 2, :], ACT.Copy).then_inc(mid_done, 1)

            def round_(i, last=False):
                for p in range(2):
                    b = 2 * i + p
                    for j in range(J):
                        if not (last and p == 1):
                            copy_v(b + 1, i + p, 1 - p, [j])
                        split(b, i, p, [j])
                        if j == 2 and not last:
                            modulate(b + 2, p)

            modulate(0, 0)
            modulate(1, 1)
            copy_v(0, 0, 0, range(J))
            round_(0)
            with act.Fori(1, rounds - 1) as i:
                round_(i)
            round_(rounds - 1, last=True)


def attention_phase(nc, k, tag, causal):
    with ExitStack() as ctx:
        sb = lambda n, s, t=F32: ctx.enter_context(nc.sbuf_tensor(f"{tag}_{n}", s, t))
        sem = lambda n: nc.alloc_semaphore(f"{tag}_{n}")
        ps = lambda n, s: ctx.enter_context(nc.psum_tensor(f"{tag}_{n}", s, F32))
        B = k.B
        half_B = B // 2
        U = NH // G4 * J
        GR = NH // G4
        Q_PARTS, K_PARTS = (0, 0, 1, 0, 2, 1), (0, 1, 0, 2, 0, 1)
        LOADS = len(Q_PARTS) + len(K_PARTS)
        KX = KS + 2
        VW = 2 * HD
        SLOTS = 3
        qs = [sb(f"qs{i}", [P, NH, T], BF16) for i in range(2)]
        ks = [sb(f"ks{i}", [P, NH, T], BF16) for i in range(2)]
        vd = [sb(f"vd{i}", [P, J, C]) for i in range(2)]
        vp = [sb(f"vp{i}", [P, J, NH, VW]) for i in range(2)]
        pT = sb("pT", [P, 2, G4, T])
        mx = sb("mx", [P, J, NH])
        mrow = sb("mrow", [NH, 2, T], BF16)
        o_sb = sb("o_sb", [P, T])
        rec = sb("rec", [P, J, G4])
        att = sb("att", [P, J, C])
        one = sb("one", [P, 1])
        psS = ps("psS", [P, SLOTS, T])
        psT = ps("psT", [P, 2, 2, T])
        psO = ps("psO", [P, T])
        stack_loaded = [[sem(f"stack_loaded{i}_{g}") for g in range(GR)] for i in range(2)]
        v_loaded = [sem(f"v_loaded{i}") for i in range(2)]
        m_loaded = [sem(f"m_loaded{i}") for i in range(2)]
        ones_done, k_ones, v_exp = sem("ones_done"), sem("k_ones"), sem("v_exp")
        s_done, max_done, mT_done, mhi_done, mrow_done = (sem("s_done"), sem("max_done"), sem("mT_done"),
                                                          sem("mhi_done"), sem("mrow_done"))
        st_done, exp_done, pv_done = sem("st_done"), sem("exp_done"), sem("pv_done")
        evac_done, oT_done, rec_done, att_done = sem("evac_done"), sem("oT_done"), sem("rec_done"), sem("att_done")
        att_stored = sem("att_stored")
        block = ctx.enter_context(nc.Block())

        SPREAD = U - 2 if causal else U - 1
        OUT_AFTER = {J + 2: 0, 2 * J + 2: 1, U - 1: 2}
        tiles_of = lambda u: range(NH * J * min(u, SPREAD) // SPREAD, NH * J * min(u + 1, SPREAD) // SPREAD)

        def schedule(last):
            order = []
            for u in range(U):
                order += [("S", n) for n in tiles_of(u) if not last]
                order += [("M", 0)] if u == SPREAD and not last else []
                order += [("O", OUT_AFTER[u])] if u in OUT_AFTER else []
            return order + [("O", GR - 1)]

        BEFORE = [("S", n) for n in range(NH * J)] + [("M", 0)]
        STEP, LAST_STEP = schedule(False), schedule(True)
        assert len(STEP) % SLOTS == 0

        def bank(b, last, what):
            if isinstance(b, int) and b == -1:
                return BEFORE.index(what) % SLOTS
            return (len(BEFORE) + (LAST_STEP if last else STEP).index(what)) % SLOTS

        def wait_for_bank(pe, b, last, what):
            before = isinstance(b, int) and b == -1
            at = (BEFORE if before else LAST_STEP if last else STEP).index(what) - SLOTS
            if at < 0 and before:
                return
            if at >= 0:
                (kind, n), of = (BEFORE if before else LAST_STEP if last else STEP)[at], b
            else:
                (kind, n), of = (BEFORE if isinstance(b, int) and b == 0 else STEP)[at], b - 1
            if kind == "S":
                pe.wait_ge(max_done, J * NH * (of + 1) + n + 1)
            elif kind == "M":
                pe.wait_ge(mrow_done, of + 2)
            else:
                pe.wait_ge(att_done, GR * of + n + 1)

        first_q = lambda kt: kt * P if causal else 0
        seen = lambda qt: (qt + 1) * P if causal else T

        def load_stack(engine, b, p, g, stack):
            dst, first, which = (qs[p], 0, Q_PARTS) if stack == "q" else (ks[p], CB, K_PARTS)
            for n, part in enumerate(which):
                src = k.parts_dram[b, part, first:first + CB].rearrange("n p t -> (n p) t")
                src = src[g * G4 * HD:(g + 1) * G4 * HD].rearrange("(h e) t -> e h t", e=HD)
                engine.dma_start(dst[n * HD:(n + 1) * HD, g * G4:(g + 1) * G4, :], src).then_inc(stack_loaded[p][g], 16)

        @block.sync
        def _(sp):
            def load_group(b, p, g):
                for stack in ("q", "k"):
                    load_stack(sp, b, p, g, stack)

            def load_v(b, p):
                sp.dma_start(vd[p][:], k.v_dram[b]).then_inc(v_loaded[p], 16)

            def load_maxima(b, p):
                sp.wait_ge(mrow_done, b + 1)
                for n in range(2):
                    sp.dma_start(qs[p][KS + n:KS + n + 1, :, :].rearrange("o h t -> o (h t)"), mrow[:, n, :]
                                 ).then_inc(m_loaded[p], 16)

            def store(b):
                sp.wait_ge(att_done, GR * b + GR)
                sp.dma_start(k.att_dram[b], att[:]).then_inc(att_stored, 16)

            def step(b, p, last_two=False, last=False):
                for g in range(GR):
                    if g == GR - 1 and not last:
                        load_maxima(b + 1, 1 - p)
                    if not last_two:
                        sp.wait_ge(pv_done, U * b + J * (g + 1))
                        load_group(b + 2, p, g)
                if not last_two:
                    sp.wait_ge(v_exp, b + 1)
                    load_v(b + 2, p)
                store(b)

            for g in range(GR):
                load_stack(sp, 0, 0, g, "q")
            load_v(0, 0)
            for g in range(GR):
                load_group(1, 1, g)
            load_v(1, 1)
            load_maxima(0, 0)
            step(0, 0)
            step(1, 1)
            with sp.Fori(1, half_B - 1) as i:
                for p in range(2):
                    step(2 * i + p, p)
            step(B - 2, 0, last_two=True)
            step(B - 1, 1, last_two=True, last=True)
            sp.wait_ge(att_stored, 16 * B)

        @block.tensor
        def _(pe):
            def scores_by_queries(b, i, p, n):
                h, qt = divmod(n, J)
                if n % (G4 * J) == 0:
                    pe.wait_ge(stack_loaded[p][h // G4], 16 * LOADS * (i + 1))
                wait_for_bank(pe, b - 1, False, ("S", n))
                m = bank(b - 1, False, ("S", n))
                out = psS[:, m, 0:seen(qt)]
                last = nc.tensor.matmul(out, qs[p][0:KS, h, qt * P:(qt + 1) * P], ks[p][0:KS, h, 0:seen(qt)],
                                        start=True, stop=not causal)
                if causal:
                    last = nc.tensor.matmul(psS[:, m, qt * P:(qt + 1) * P], k.ident_bf[:], k.mask_bf[:],
                                            start=False, stop=True)
                last.then_inc(s_done, 1)

            def transpose_maxima(b):
                pe.wait_ge(max_done, J * NH * (b + 1))
                wait_for_bank(pe, b - 1, False, ("M", 0))
                m = bank(b - 1, False, ("M", 0))
                for j in range(J):
                    last = nc.tensor.transpose(psS[0:NH, m, j * P:(j + 1) * P], mx[:, j, :], k.ident[:])
                last.then_inc(mT_done, 1)

            def scores_by_keys(b, p, u, pr):
                g, kt = divmod(u, J)
                pe.wait_ge(exp_done, 2 * U * b + max(2 * u + pr - 1, 0))
                for n in range(2):
                    h = G4 * g + 2 * pr + n
                    last = nc.tensor.matmul(psT[:, pr, n, first_q(kt):T], ks[p][0:KX, h, kt * P:(kt + 1) * P],
                                            qs[p][0:KX, h, first_q(kt):T], start=True, stop=not causal)
                    if causal:
                        last = nc.tensor.matmul(psT[:, pr, n, kt * P:(kt + 1) * P], k.mask_bf[:], k.ident_bf[:],
                                                start=False, stop=True)
                last.then_inc(st_done, 1)

            def values(b, p, u, heads):
                g, kt = divmod(u, J)
                if heads[0] == 0:
                    pe.wait_ge(exp_done, 2 * U * b + 2 * u + 2)
                    if u == 0:
                        pe.wait_ge(v_exp, b + 1)
                    if kt == 0:
                        pe.wait_ge(evac_done, GR * b + g)
                for n in heads:
                    last = nc.tensor.matmul(psO[VW * n:VW * (n + 1), first_q(kt):T], vp[p][:, kt, G4 * g + n, :],
                                            pT[:, u % 2, n, first_q(kt):T], start=(kt == 0), stop=(kt == J - 1))
                if heads[-1] == G4 - 1:
                    last.then_inc(pv_done, 1)

            def transpose_outputs(b, g, last_step):
                pe.wait_ge(evac_done, GR * b + g + 1)
                wait_for_bank(pe, b, last_step, ("O", g))
                m = bank(b, last_step, ("O", g))
                for j in range(J):
                    last = nc.tensor.transpose(psS[:, m, j * P:(j + 1) * P], o_sb[:, j * P:(j + 1) * P], k.ident[:])
                last.then_inc(oT_done, 1)

            VALUES_OF = {2: (0, 1), 3: (2, 3)}
            PARTS = 2 + len(VALUES_OF)
            made = lambda part, all_: min((0, 2, 3, 4, all_)[part], all_)

            def step(b, i, p, last=False):
                for u in range(U):
                    ahead = [] if last else list(tiles_of(u))
                    if u == 0:
                        pe.wait_ge(m_loaded[p], 32 * (i + 1))
                    for part in range(PARTS):
                        if part < 2:
                            scores_by_keys(b, p, u, part)
                        elif u > 0:
                            values(b, p, u - 1, VALUES_OF[part])
                        for n in ahead[made(part, len(ahead)):made(part + 1, len(ahead))]:
                            scores_by_queries(b + 1, i + p, 1 - p, n)
                        if part == 1 and u == SPREAD and not last:
                            transpose_maxima(b + 1)
                    if u in OUT_AFTER:
                        transpose_outputs(b, OUT_AFTER[u], last)
                values(b, p, U - 1, range(G4))
                transpose_outputs(b, GR - 1, last)

            for n in range(NH * J):
                scores_by_queries(0, 0, 0, n)
            transpose_maxima(0)
            pe.wait_ge(k_ones, 2)
            step(0, 0, 0)
            step(1, 0, 1)
            with pe.Fori(1, half_B - 1) as i:
                for p in range(2):
                    step(2 * i + p, i, p)
            step(B - 2, half_B - 1, 0)
            step(B - 1, half_B - 1, 1, last=True)

        @block.scalar
        def _(act):
            def exponentials(b, u, pairs):
                kt = u % J
                for pr in pairs:
                    act.wait_ge(st_done, 2 * U * b + 2 * u + pr + 1)
                    if pr == 0:
                        act.wait_ge(pv_done, U * b + max(u - 1, 0))
                    nc.scalar.activation(pT[:, u % 2, 2 * pr:2 * pr + 2, first_q(kt):T], psT[:, pr, :, first_q(kt):T],
                                         ACT.Exp, scale=HD ** -0.5).then_inc(exp_done, 1)

            def read_outputs(b, g):
                act.wait_ge(pv_done, U * b + J * (g + 1))
                act.wait_ge(oT_done, GR * b + g)
                nc.scalar.activation(o_sb[:], psO[:], ACT.Copy).then_inc(evac_done, 1)

            def negate_maxima(b, i, p):
                if i is not None:
                    act.wait_ge(m_loaded[p], 32 * (i + 1))
                act.wait_ge(mT_done, b + 1)
                nc.scalar.activation(mrow[:, 0, :], psS[0:NH, bank(b - 1, False, ("M", 0)), :], ACT.Copy, scale=-1.0).then_inc(mhi_done, 1)

            def step(b, i, p, last=False):
                for u in range(U):
                    exponentials(b, u, (0,))
                    if u == SPREAD and not last:
                        negate_maxima(b + 1, i, p)
                    exponentials(b, u, (1,))
                    if u % J == 0 and u > 0:
                        read_outputs(b, u // J - 1)
                read_outputs(b, GR - 1)

            for g in range(GR):
                load_stack(act, 0, 0, g, "k")
            negate_maxima(0, None, None)
            step(0, 0, 0)
            step(1, 0, 1)
            with act.Fori(1, half_B - 1) as i:
                for p in range(2):
                    step(2 * i + p, i, p)
            step(B - 2, half_B - 1, 0)
            step(B - 1, half_B - 1, 1, last=True)

        @block.vector
        def _(dve):
            def maxima(b, tiles):
                for n in tiles:
                    h, qt = divmod(n, J)
                    if n == 0:
                        dve.wait_ge(mT_done, b)
                    dve.wait_ge(s_done, J * NH * b + n + 1)
                    nc.vector.reduce_max(mx[:, qt, h:h + 1], psS[:, bank(b - 1, False, ("S", n)), 0:seen(qt)], axis=AX.X
                                         ).then_inc(max_done, 1)

            def second_part(b):
                dve.wait_ge(mhi_done, b + 1)
                nc.vector.scalar_tensor_tensor(mrow[:, 1, :], psS[0:NH, bank(b - 1, False, ("M", 0)), :], -1.0, mrow[:, 0, :],
                                               ALU.mult, ALU.subtract).then_inc(mrow_done, 1)

            def normalize(b, g, last_step):
                heads = psS[:, bank(b, last_step, ("O", g)), :].rearrange("p (j h e) -> p j h e", j=J, e=VW)
                dve.wait_ge(oT_done, GR * b + g + 1)
                if not (isinstance(b, int) and b == g == 0):
                    dve.wait_ge(att_done, GR * b + g)
                nc.vector.reciprocal(rec[:], heads[:, :, :, HD]).then_inc(rec_done, 1)
                dve.wait_ge(rec_done, GR * b + g + 1)
                if g == 0:
                    dve.wait_ge(att_stored, 16 * b)
                out = att[:].rearrange("p j (h e) -> p j h e", e=HD)[:, :, G4 * g:G4 * (g + 1), :]
                nc.vector.tensor_tensor(out, heads[:, :, :, 0:HD], rec[:].unsqueeze(3).to_broadcast([P, J, G4, HD]),
                                        ALU.mult).then_inc(att_done, 1)

            def step(b, last=False):
                for u in range(U):
                    if not last:
                        maxima(b + 1, tiles_of(u))
                    if u == SPREAD and not last:
                        second_part(b + 1)
                    if u in OUT_AFTER:
                        normalize(b, OUT_AFTER[u], last)
                normalize(b, GR - 1, last)

            maxima(0, range(NH * J))
            second_part(0)
            step(0)
            step(1)
            with dve.Fori(1, half_B - 1) as i:
                for p in range(2):
                    step(2 * i + p)
            step(B - 2)
            step(B - 1, last=True)

        @block.gpsimd
        def _(pool):
            def expand_v(b, i, p):
                pool.wait_ge(v_loaded[p], 16 * (i + 1))
                heads = vd[p][:].rearrange("p j (h e) -> p j h e", e=HD)
                nc.gpsimd.tensor_tensor(vp[p][:, :, :, 0:HD], heads, one[:].unsqueeze(2).unsqueeze(3).to_broadcast(
                    [P, J, NH, HD]), ALU.mult).then_inc(v_exp, 1)

            def step(b, i, p, last=False):
                if not last:
                    pool.wait_ge(pv_done, U * b)
                    expand_v(b + 1, i + p, 1 - p)

            for p in range(2):
                nc.gpsimd.memset(vp[p][:, :, :, HD:VW], 1.0)
            nc.gpsimd.memset(one[:], 1.0).then_inc(ones_done, 1)
            pool.wait_ge(ones_done, 1)
            for p in range(2):
                nc.gpsimd.memset(ks[p][KS:KX, :, :], 1.0).then_inc(k_ones, 1)
                pool.wait_ge(k_ones, p + 1)
            expand_v(0, 0, 0)
            step(0, 0, 0)
            step(1, 0, 1)
            with pool.Fori(1, half_B - 1) as i:
                for p in range(2):
                    step(2 * i + p, i, p)
            step(B - 2, half_B - 1, 0)
            step(B - 1, half_B - 1, 1, last=True)


def output_and_qkv_phase(nc, k, d):
    with ExitStack() as ctx:
        sb = lambda n, s, t=F32: ctx.enter_context(nc.sbuf_tensor("mid_" + n, s, t))
        sem = lambda n: nc.alloc_semaphore("mid_" + n)
        ps = lambda n, s: ctx.enter_context(nc.psum_tensor("mid_" + n, s, F32))
        B = k.B
        NB = 2 * CB
        wo, wq, wk, wv = sb("wo", [P, CB, C]), sb("wq", [P, CB, C]), sb("wk", [P, CB, C]), sb("wv", [P, CB, C])
        bv = sb("bv", [P, C])
        gate = sb("gate", [P, C])
        att = sb("att", [P, J, C])
        aT = sb("aT", [P, CB, T])
        y = sb("y", [P, J, C])
        z = sb("z", [P, J, C])
        hT = [sb(f"hT{i}", [P, CB, T]) for i in range(2)]
        rest = sb("rest", [P, 2, T])
        parts = [sb(f"parts{i}", [P, 3, NB, T], BF16) for i in range(2)]
        v = [sb(f"v{i}", [P, J, C]) for i in range(2)]
        ln = Norm(nc, ctx, "mid_ln")
        psA, psY, psV = ps("psA", [P, CB, T]), ps("psY", [P, J, C]), ps("psV", [P, J, C])
        psQ = ps("psQ", [P, 2, T])
        weights, gate_loaded, att_loaded = sem("weights"), sem("gate_loaded"), sem("att_loaded")
        aT_ps, aT_done, y_done, yg_done, x_done = sem("aT_ps"), sem("aT_done"), sem("y_done"), sem("yg_done"), sem("x_done")
        z_done, zT_done, hT_done, q_done = sem("z_done"), sem("zT_done"), sem("hT_done"), sem("q_done")
        hi_done, rest_done, mid_done, lo_done = sem("hi_done"), sem("rest_done"), sem("mid_done"), sem("lo_done")
        v_done, vb_done = sem("v_done"), sem("vb_done")
        v_stored = [sem(f"v_stored{i}") for i in range(2)]
        parts_stored = [sem(f"parts_stored{i}") for i in range(2)]
        block = ctx.enter_context(nc.Block())
        rounds = B // 2
        bias = lambda n: col(k, "bq" if n < CB else "bk", n % CB)

        @block.sync
        def _(sp):
            for ap, src in ((wo, "w_out"), (wq, "Wq"), (wk, "Wk"), (wv, "Wv")):
                sp.dma_start(ap[:], d[src].rearrange("(k p) n -> p k n", p=P)).then_inc(weights, 16)
            sp.dma_start(bv[:], d["rows"][ROWS.index("bv")].partition_broadcast(P)).then_inc(weights, 16)

            def load(b):
                if not (isinstance(b, int) and b == 0):
                    sp.wait_ge(yg_done, b)
                sp.dma_start(gate[:], k.mrows_dram[2, b].partition_broadcast(P)).then_inc(gate_loaded, 16)
                sp.dma_start(att[:], k.att_dram[b]).then_inc(att_loaded, 16)

            def store(b, p):
                sp.wait_ge(vb_done, b + 1)
                sp.dma_start(k.v_dram[b], v[p][:]).then_inc(v_stored[p], 16)
                sp.wait_ge(mid_done, NB * b + NB)
                sp.wait_ge(lo_done, NB * b + NB)
                sp.dma_start(k.parts_dram[b].rearrange("s n p t -> p s n t"), parts[p][:]).then_inc(parts_stored[p], 16)

            load(0)
            load(1)
            load(2)
            with sp.Fori(0, rounds - 2) as i:
                for p in range(2):
                    load(2 * i + p + 3)
                    store(2 * i + p, p)
            load(B - 1)
            store(B - 4, 0)
            store(B - 3, 1)
            store(B - 2, 0)
            store(B - 1, 1)
            for p in range(2):
                sp.wait_ge(v_stored[p], 16 * rounds)
                sp.wait_ge(parts_stored[p], 16 * rounds)

        @block.tensor
        def _(pe):
            def transpose_attention(b):
                pe.wait_ge(att_loaded, 16 * b + 16)
                if not (isinstance(b, int) and b == 0):
                    pe.wait_ge(aT_done, b)
                if not (isinstance(b, int) and b < 2):
                    pe.wait_ge(hT_done, b)
                to_channels(nc, k, psA, att).then_inc(aT_ps, 1)

            def project_out(b):
                pe.wait_ge(aT_done, b + 1)
                if not (isinstance(b, int) and b == 0):
                    pe.wait_ge(yg_done, b)
                for j in range(J):
                    for cb in range(CB):
                        last = nc.tensor.matmul(psY[:, j, :], aT[:, cb, j * P:(j + 1) * P], wo[:, cb, :],
                                                start=(cb == 0), stop=(cb == CB - 1))
                last.then_inc(y_done, 1)

            def transpose_h(b):
                pe.wait_ge(z_done, b + 1)
                pe.wait_ge(aT_done, min(b + 1, 2) if isinstance(b, int) else b + 1)
                to_channels(nc, k, psA, z).then_inc(zT_done, 1)

            def project_v(b, p):
                pe.wait_ge(hT_done, b + 1)
                if not (isinstance(b, int) and b == 0):
                    pe.wait_ge(vb_done, b)
                for j in range(J):
                    for cb in range(CB):
                        last = nc.tensor.matmul(psV[:, j, :], hT[p][:, cb, j * P:(j + 1) * P], wv[:, cb, :],
                                                start=(cb == 0), stop=(cb == CB - 1))
                last.then_inc(v_done, 1)

            def project_qk(b, p, blocks):
                for n in blocks:
                    w = wq if n < CB else wk
                    pe.wait_ge(rest_done, NB * b + max(n - 1, 0))
                    for cb in range(CB):
                        last = nc.tensor.matmul(psQ[:, n % 2, :], w[:, cb, (n % CB) * P:(n % CB + 1) * P],
                                                hT[p][:, cb, :], start=(cb == 0), stop=(cb == CB - 1))
                    last.then_inc(q_done, 1)

            def round_(i, last=False):
                for p in range(2):
                    b = 2 * i + p
                    project_v(b, p)
                    if not (last and p == 1):
                        transpose_h(b + 1)
                    project_qk(b, p, [0])
                    if not last:
                        transpose_attention(b + 2)
                    project_qk(b, p, [1])
                    if not last:
                        project_out(b + 2)
                    project_qk(b, p, [2, 3])

            pe.wait_ge(weights, 80)
            transpose_attention(0)
            project_out(0)
            transpose_attention(1)
            project_out(1)
            transpose_h(0)
            round_(0)
            with pe.Fori(1, rounds - 1) as i:
                round_(i)
            round_(rounds - 1, last=True)

        @block.scalar
        def _(act):
            def copy_attention(b):
                act.wait_ge(aT_ps, b + 1)
                if not (isinstance(b, int) and b == 0):
                    act.wait_ge(y_done, b)
                nc.scalar.activation(aT[:], psA[:], ACT.Copy).then_inc(aT_done, 1)

            def modulate(b, p):
                act.wait_ge(zT_done, b + 1)
                if not (isinstance(b, int) and b < 2):
                    act.wait_ge(v_done, b - 1)
                    act.wait_ge(q_done, NB * (b - 1))
                for cb in range(CB):
                    last = nc.scalar.activation(hT[p][:, cb, :], psA[:, cb, :], ACT.Identity,
                                                scale=k.mod[:, 1, CBM * CB + cb, bass.ds(b, 1)],
                                                bias=k.mod[:, 1, SB * CB + cb, bass.ds(b, 1)])
                last.then_inc(hT_done, 1)

            def split(b, i, p, blocks):
                for n in blocks:
                    if n == 0 and not (isinstance(i, int) and i == 0):
                        act.wait_ge(parts_stored[p], 16 * i)
                    act.wait_ge(q_done, NB * b + n + 1)
                    nc.scalar.activation(parts[p][:, 0, n, :], psQ[:, n % 2, :], ACT.Identity, bias=bias(n)
                                         ).then_inc(hi_done, 1)
                    act.wait_ge(rest_done, NB * b + n + 1)
                    nc.scalar.activation(parts[p][:, 1, n, :], rest[:, n % 2, :], ACT.Copy).then_inc(mid_done, 1)

            def round_(i, last=False):
                for p in range(2):
                    b = 2 * i + p
                    if not (last and p == 1):
                        modulate(b + 1, 1 - p)
                    split(b, i, p, [0])
                    if not last:
                        copy_attention(b + 2)
                    split(b, i, p, range(1, NB))

            copy_attention(0)
            copy_attention(1)
            modulate(0, 0)
            round_(0)
            with act.Fori(1, rounds - 1) as i:
                round_(i)
            round_(rounds - 1, last=True)

        @block.vector
        def _(dve):
            def residual(b):
                dve.wait_ge(y_done, b + 1)
                dve.wait_ge(gate_loaded, 16 * b + 16)
                if not (isinstance(b, int) and b == 0):
                    dve.wait_ge(x_done, b)
                nc.vector.tensor_tensor(y[:], psY[:], over_tiles(gate[:]), ALU.mult).then_inc(yg_done, 1)
                dve.wait_ge(yg_done, b + 1)
                xb = k.x[:, bass.ds(b * J, J), :]
                nc.vector.tensor_tensor(xb, xb, y[:], ALU.add).then_inc(x_done, 1)
                dve.wait_ge(x_done, b + 1)
                nc.vector.memset(ln.pause[:], 0.0)
                ln.moments(nc, dve, lambda j: k.x[:, b * J + j, :], b)

            def normalize(b):
                if not (isinstance(b, int) and b == 0):
                    dve.wait_ge(zT_done, b)
                ln.apply(nc, dve, z, lambda j: k.x[:, b * J + j, :], b).then_inc(z_done, 1)

            def add_bias(b, i, p):
                dve.wait_ge(v_done, b + 1)
                if not (isinstance(i, int) and i == 0):
                    dve.wait_ge(v_stored[p], 16 * i)
                nc.vector.tensor_tensor(v[p][:], psV[:], over_tiles(bv[:]), ALU.add).then_inc(vb_done, 1)

            def split(b, p, blocks):
                for n in blocks:
                    dve.wait_ge(hi_done, NB * b + n + 1)
                    dve.wait_ge(lo_done, NB * b + max(n - 1, 0))
                    nc.vector.scalar_tensor_tensor(rest[:, n % 2, :], psQ[:, n % 2, :], bias(n), parts[p][:, 0, n, :],
                                                   ALU.add, ALU.subtract).then_inc(rest_done, 1)

            def round_(i, last=False):
                for p in range(2):
                    b = 2 * i + p
                    add_bias(b, i, p)
                    split(b, p, [0, 1])
                    if not last:
                        residual(b + 2)
                    split(b, p, [2])
                    if not last:
                        normalize(b + 2)
                    split(b, p, [3])

            dve.wait_ge(weights, 80)
            residual(0)
            normalize(0)
            residual(1)
            normalize(1)
            round_(0)
            with dve.Fori(1, rounds - 1) as i:
                round_(i)
            round_(rounds - 1, last=True)

        @block.gpsimd
        def _(pool):
            def low_parts(b, p, blocks):
                for n in blocks:
                    pool.wait_ge(mid_done, NB * b + n + 1)
                    nc.gpsimd.tensor_tensor(parts[p][:, 2, n, :], rest[:, n % 2, :], parts[p][:, 1, n, :],
                                            ALU.subtract).then_inc(lo_done, 1)

            def round_(i, last=False):
                for p in range(2):
                    b = 2 * i + p
                    low_parts(b, p, [0, 1])
                    if not last:
                        ln.rsqrt(nc, k, pool, b + 2)
                    low_parts(b, p, [2, 3])

            ln.rsqrt(nc, k, pool, 0)
            ln.rsqrt(nc, k, pool, 1)
            round_(0)
            with pool.Fori(1, rounds - 1) as i:
                round_(i)
            round_(rounds - 1, last=True)


ROW_X1, ROW_X, ROW_GATE, ROW_ID, ROW = 0, C, 2 * C, 3 * C, 3 * C + 4
I32 = mybir.dt.int32


def route_phase(nc, k, d):
    with ExitStack() as ctx:
        sb = lambda n, s, t=F32: ctx.enter_context(nc.sbuf_tensor("rou_" + n, s, t))
        sem = lambda n: nc.alloc_semaphore("rou_" + n)
        ps = lambda n, s: ctx.enter_context(nc.psum_tensor("rou_" + n, s, F32))
        B = k.B
        wo = sb("wo", [P, CB, C])
        rowb = {n: sb(f"rowb_{n}", [P, C]) for n in ("bo", "l1_ln1_g", "l1_ln1_b", "router_w")}
        before, ones = sb("before", [P, P]), sb("ones", [P, P])
        experts = sb("experts", [P, NE])
        ids = sb("ids", [P, B * J], I32)
        mrow = [sb(f"mrow{i}", [P, 3, C]) for i in range(2)]
        att = sb("att", [P, J, C])
        aT = sb("aT", [P, CB, T])
        shift = sb("shift", [1, 2, C])
        z = [sb(f"z{i}", [P, J, C]) for i in range(2)]
        rows = [sb(f"rows_out{i}", [P, J, ROW]) for i in range(2)]
        junk = sb("junk", [P, J, C])
        key, key_f, above = sb("key", [P, J]), sb("key_f", [P, J]), sb("above", [P, J])
        key_i, expert_i, expert_f = sb("key_i", [P, J], I32), sb("expert_i", [P, J], I32), sb("expert_f", [P, J])
        member = sb("member", [P, J, NE], BF16)
        before_bf, ones_bf = sb("before_bf", [P, P], BF16), sb("ones_bf", [P, P], BF16)
        place = sb("place", [P, J, NE])
        slot = sb("slot", [P, J])
        slot_i = [sb(f"slot_i{i}", [P, J], I32) for i in range(2)]
        pool_pause = sb("pool_pause", [P, 2])
        nxt = k.next_row
        minus_mean = sb("minus_mean", [P, J])
        act_pause = sb("act_pause", [P, 2])
        mean_done = sem("mean_done")
        ln0, ln1 = Norm(nc, ctx, "rou_ln0"), Norm(nc, ctx, "rou_ln1")
        psA, psY = ps("psA", [P, CB, T]), ps("psY", [P, J, C])
        psR = ps("psR", [P, T])
        PREFIX, TOTAL = psR[:, 0:J * NE], psR[:, J * NE:(J + 1) * NE]
        weights, att_loaded, init = sem("weights"), sem("att_loaded"), sem("init")
        mrow_loaded = [sem(f"mrow_loaded{i}") for i in range(2)]
        scattered = [sem(f"scattered{i}") for i in range(2)]
        aT_ps, aT_done, y_done = sem("aT_ps"), sem("aT_done"), sem("y_done")
        z_done, shift_done, src_done = sem("z_done"), sem("shift_done"), sem("src_done")
        t_done, z1g_done, x1_done = sem("t_done"), sem("z1g_done"), sem("x1_done")
        copied, member_done = sem("copied"), sem("member_done")
        key_step, slot_step = sem("key_step"), sem("slot_step")
        ranks_done, slot_done = sem("ranks_done"), sem("slot_done")
        block = ctx.enter_context(nc.Block())
        KEY_STEPS, SLOT_STEPS = 7, 3
        assert B // 2 > NE + 1
        rounds = B // 2

        @block.sync
        def _(sp):
            sp.dma_start(wo[:], d["Wo"].rearrange("(k p) n -> p k n", p=P)).then_inc(weights, 16)
            for n, ap in rowb.items():
                sp.dma_start(ap[:], d["rows"][ROWS.index(n)].partition_broadcast(P)).then_inc(weights, 16)
            for ap, n in ((before, "before"), (experts, "experts"), (ids, "ids")):
                sp.dma_start(ap[:], d[n]).then_inc(weights, 16)

            def load_attention(b):
                sp.dma_start(att[:], k.att_dram[b]).then_inc(att_loaded, 16)

            def load_rows(b, p):
                for n, row in enumerate((4, 5, 3)):
                    sp.dma_start(mrow[p][:, n, :], k.mrows_dram[row, b].partition_broadcast(P)
                                 ).then_inc(mrow_loaded[p], 16)

            def step(b, p):
                sp.wait_ge(aT_ps, b + 2)
                load_attention(b + 2)
                sp.wait_ge(copied, b + 1)
                sp.wait_ge(src_done, b + 1)
                sp.wait_ge(shift_done, b + 1)
                load_rows(b + 2, p)

            load_attention(0)
            for p in range(2):
                load_rows(p, p)
            sp.wait_ge(aT_ps, 1)
            load_attention(1)
            with sp.Fori(0, NE) as i:
                for p in range(2):
                    step(2 * i + p, p)
                for w, n in ((k.moe_w1, "moe_W1"), (k.moe_w2, "moe_W2")):
                    sp.dma_start(w[:, bass.ds(i, 1)].rearrange("p o k f -> p (o k) f"),
                                 d[n][bass.ds(i, 1)].rearrange("o (k p) f -> p (o k) f", p=P)).then_inc(k.moe_loaded, 16)
            with sp.Fori(NE, rounds - 1) as i:
                for p in range(2):
                    step(2 * i + p, p)

        @block.tensor
        def _(pe):
            def project_out(b, p):
                pe.wait_ge(att_loaded, 16 * b + 16)
                pe.wait_ge(aT_done, b)
                to_channels(nc, k, psA, att).then_inc(aT_ps, 1)
                pe.wait_ge(aT_done, b + 1)
                pe.wait_ge(t_done, b)
                for j in range(J):
                    for cb in range(CB):
                        last = nc.tensor.matmul(psY[:, j, :], aT[:, cb, j * P:(j + 1) * P], wo[:, cb, :],
                                                start=(cb == 0), stop=False)
                    if j == 0:
                        pe.wait_ge(shift_done, b + 1)
                    last = nc.tensor.matmul(psY[:, j, :], ones[0:1, :], shift[0:1, p, :], start=False, stop=True)
                last.then_inc(y_done, 1)

            def count(b):
                pe.wait_ge(member_done, b + 1)
                pe.wait_ge(slot_done, b)
                for j in range(J):
                    out = PREFIX[:, j * NE:(j + 1) * NE]
                    nc.tensor.matmul(out, before_bf[:], member[:, j, :], start=True, stop=(j == 0))
                    for earlier in range(j):
                        nc.tensor.matmul(out, ones_bf[:], member[:, earlier, :], start=False, stop=(earlier == j - 1))
                for j in range(J):
                    last = nc.tensor.matmul(TOTAL, ones_bf[:], member[:, j, :], start=(j == 0), stop=(j == J - 1))
                last.then_inc(ranks_done, 1)

            pe.wait_ge(weights, 128)
            pe.wait_ge(init, 1)
            def round_(i, last=False):
                for p in range(2):
                    count(2 * i + p)
                    if not last:
                        project_out(2 * i + p + 2, p)

            project_out(0, 0)
            project_out(1, 1)
            round_(0)
            with pe.Fori(1, rounds - 1) as i:
                round_(i)
            round_(rounds - 1, last=True)

        @block.scalar
        def _(act):
            def copy_attention(b):
                act.wait_ge(aT_ps, b + 1)
                act.wait_ge(y_done, b)
                nc.scalar.activation(aT[:], psA[:], ACT.Copy).then_inc(aT_done, 1)

            def fill_rows(b, i, p):
                act.wait_ge(mrow_loaded[p], 48 * (i + 1))
                if not (isinstance(i, int) and i == 0):
                    act.wait_ge(scattered[p], 64 * i)
                nc.scalar.activation(rows[p][:, :, ROW_GATE:ROW_GATE + C], over_tiles(mrow[p][:, 2, :]), ACT.Copy)
                nc.scalar.activation(rows[p][:, :, ROW_X:ROW_X + C], k.x[:, bass.ds(b * J, J), :], ACT.Copy
                                     ).then_inc(copied, 1)

            def source_normalize(b, p):
                if not (isinstance(b, int) and b < 2):
                    act.wait_ge(x1_done, b - 1)
                act.wait_ge(mean_done, b + 1)
                nc.scalar.activation(act_pause[:, p:p + 1], minus_mean[:, 0:1], ACT.Copy)
                for j in range(J):
                    last = nc.scalar.activation(z[p][:, j, :], k.x[:, b * J + j, :], ACT.Identity,
                                                scale=ln0.rstd[:, j:j + 1], bias=minus_mean[:, j:j + 1])
                last.then_inc(z_done, 1)

            def round_(i, last=False):
                for p in range(2):
                    if not (last and p == 1):
                        fill_rows(2 * i + p + 1, i + p, 1 - p)
                    if not last:
                        copy_attention(2 * i + p + 2)
                        source_normalize(2 * i + p + 2, p)

            source_normalize(0, 0)
            copy_attention(0)
            fill_rows(0, 0, 0)
            source_normalize(1, 1)
            copy_attention(1)
            round_(0)
            with act.Fori(1, rounds - 1) as i:
                round_(i)
            round_(rounds - 1, last=True)

        @block.gpsimd
        def _(pool):
            def source(b, i, p):
                pool.wait_ge(mrow_loaded[p], 48 * (i + 1))
                pool.wait_ge(z_done, b + 1)
                nc.gpsimd.tensor_tensor(z[p][:], z[p][:], over_tiles(mrow[p][:, 0, :]), ALU.mult).then_inc(src_done, 1)

            def scatter(b, p):
                pool.wait_ge(slot_done, b + 1)
                pool.wait_ge(copied, b + 1)
                nc.gpsimd.tensor_tensor(pool_pause[:, p:p + 1], k.eps[:, 0:1], k.eps[:, 0:1], ALU.add)
                for j in range(J):
                    nc.gpsimd.indirect_dma_start(k.rows_dram, bass.IndirectOffsetOnAxis(ap=slot_i[p][:, j:j + 1], axis=0),
                                                 rows[p][:, j, :], None).then_inc(scattered[p], 16)

            def round_(i, last=False):
                for p in range(2):
                    b = 2 * i + p
                    if not last:
                        ln0.rsqrt(nc, k, pool, b + 2)
                    if not (last and p == 1):
                        ln1.rsqrt(nc, k, pool, b + 1)
                    scatter(b, p)
                    if not last:
                        source(b + 2, i + 1, p)

            nc.gpsimd.memset(ones[:], 1.0)
            for p in range(2):
                last = nc.gpsimd.memset(rows[p][:, :, ROW_ID:ROW], 0.0)
            last.then_inc(init, 1)
            pool.wait_ge(init, 1)
            ln0.rsqrt(nc, k, pool, 0)
            source(0, 0, 0)
            ln0.rsqrt(nc, k, pool, 1)
            ln1.rsqrt(nc, k, pool, 0)
            source(1, 0, 1)
            round_(0)
            with pool.Fori(1, rounds - 1) as i:
                round_(i)
            round_(rounds - 1, last=True)
            for p in range(2):
                pool.wait_ge(scattered[p], 64 * rounds)

        @block.vector
        def _(dve):
            def source_moments(b, i, p):
                dve.wait_ge(mrow_loaded[p], 48 * (i + 1))
                if not (isinstance(b, int) and b < 2):
                    dve.wait_ge(y_done, b - 1)
                nc.vector.tensor_tensor(shift[0:1, p, :], mrow[p][0:1, 1, :], rowb["bo"][0:1, :], ALU.add
                                        ).then_inc(shift_done, 1)
                ln0.moments(nc, dve, lambda j: k.x[:, b * J + j, :], b)

            def source_bias(b):
                dve.wait_ge(ln0.rstd_ready, b + 1)
                if not (isinstance(b, int) and b == 0):
                    dve.wait_ge(z_done, b)
                nc.vector.scalar_tensor_tensor(minus_mean[:], ln0.mv[:, :, 0], -1.0, ln0.rstd[:], ALU.mult, ALU.mult
                                               ).then_inc(mean_done, 1)

            def add_source(b, p):
                dve.wait_ge(y_done, b + 1)
                dve.wait_ge(src_done, b + 1)
                nc.vector.tensor_tensor(z[p][:], psY[:], z[p][:], ALU.add).then_inc(t_done, 1)
                dve.wait_ge(t_done, b + 1)
                nc.vector.memset(ln1.pause[:], 0.0)
                ln1.moments(nc, dve, lambda j: z[p][:, j, :], b)

            def normalize(b, i, p):
                dve.wait_ge(ln1.rstd_ready, b + 1)
                for j in range(J):
                    last = nc.vector.scalar_tensor_tensor(z[p][:, j, :], z[p][:, j, :], ln1.mv[:, j, 0:1],
                                                          rowb["l1_ln1_g"][:], ALU.subtract, ALU.mult)
                last.then_inc(z1g_done, 1)
                dve.wait_ge(z1g_done, b + 1)
                if not (isinstance(i, int) and i == 0):
                    dve.wait_ge(scattered[p], 64 * i)
                nc.vector.tensor_copy(rows[p][:, :, ROW_ID:ROW_ID + 1].bitcast(I32),
                                      ids[:, bass.ds(b * J, J)].unsqueeze(2))
                for j in range(J):
                    last = nc.vector.scalar_tensor_tensor(rows[p][:, j, ROW_X1:ROW_X1 + C], z[p][:, j, :],
                                                          ln1.rstd[:, j:j + 1], rowb["l1_ln1_b"][:], ALU.mult, ALU.add)
                last.then_inc(x1_done, 1)

            def choose(b, p):
                taken = [0]

                def follow(instruction):
                    taken[0] += 1
                    instruction.then_inc(key_step, 1)
                    dve.wait_ge(key_step, KEY_STEPS * b + taken[0])

                dve.wait_ge(x1_done, b + 1)
                for j in range(J):
                    instruction = nc.vector.tensor_tensor_reduce(
                        out=junk[:, j, :], in0=rows[p][:, j, ROW_X1:ROW_X1 + C], in1=rowb["router_w"][:], scale=1.0,
                        scalar=k.cols[:, COLS["router_b"][0]:COLS["router_b"][0] + 1], op0=ALU.mult, op1=ALU.add,
                        accum_out=key[:, j:j + 1])
                follow(instruction)
                follow(nc.vector.tensor_copy(key_i[:], key[:]))
                follow(nc.vector.tensor_copy(key_f[:], key_i[:]))
                follow(nc.vector.tensor_tensor(above[:], key_f[:], key[:], ALU.is_gt))
                follow(nc.vector.tensor_tensor(key_i[:], key_f[:], above[:], ALU.subtract))
                follow(nc.vector.tensor_scalar(expert_i[:], key_i[:], NE - 1, None, ALU.bitwise_and))
                follow(nc.vector.tensor_copy(expert_f[:], expert_i[:]))
                nc.vector.tensor_tensor(member[:], expert_f[:].unsqueeze(2).to_broadcast([P, J, NE]),
                                        experts[:].unsqueeze(1).to_broadcast([P, J, NE]), ALU.is_equal
                                        ).then_inc(member_done, 1)
                assert taken[0] == KEY_STEPS

            def place_rows(b, i, p):
                taken = [0]

                def follow(instruction):
                    taken[0] += 1
                    instruction.then_inc(slot_step, 1)
                    dve.wait_ge(slot_step, SLOT_STEPS * b + taken[0])

                dve.wait_ge(member_done, b + 1)
                dve.wait_ge(ranks_done, b + 1)
                follow(nc.vector.tensor_tensor(place[:], PREFIX.rearrange("p (j e) -> p j e", e=NE),
                                               nxt[:].unsqueeze(1).to_broadcast([P, J, NE]), ALU.add))
                follow(nc.vector.tensor_tensor(place[:], place[:], member[:], ALU.mult))
                nc.vector.tensor_tensor(nxt[:], nxt[:], TOTAL, ALU.add)
                follow(nc.vector.tensor_reduce(slot[:], place[:], op=ALU.add, axis=AX.X))
                if not (isinstance(i, int) and i == 0):
                    dve.wait_ge(scattered[p], 64 * i)
                nc.vector.tensor_copy(slot_i[p][:], slot[:]).then_inc(slot_done, 1)
                dve.wait_ge(slot_done, b + 1)
                nc.vector.memset(ln1.pause[:], 0.0)
                assert taken[0] == SLOT_STEPS

            def round_(i, last=False):
                for p in range(2):
                    b = 2 * i + p
                    if not last:
                        source_moments(b + 2, i + 1, p)
                    if not (last and p == 1):
                        add_source(b + 1, 1 - p)
                    place_rows(b, i, p)
                    if not last:
                        source_bias(b + 2)
                    if not (last and p == 1):
                        normalize(b + 1, i + p, 1 - p)
                        choose(b + 1, 1 - p)

            dve.wait_ge(weights, 128)
            dve.wait_ge(init, 1)
            nc.vector.tensor_copy(ones_bf[:], ones[:])
            nc.vector.tensor_copy(before_bf[:], before[:])
            nc.vector.tensor_scalar(nxt[:], experts[:], float(k.CAP), None, ALU.mult)
            source_moments(0, 0, 0)
            source_bias(0)
            source_moments(1, 0, 1)
            add_source(0, 0)
            source_bias(1)
            normalize(0, 0, 0)
            choose(0, 0)
            round_(0)
            with dve.Fori(1, rounds - 1) as i:
                round_(i)
            round_(rounds - 1, last=True)


def expert_phase(nc, k, d, out):
    with ExitStack() as ctx:
        sb = lambda n, s, t=F32: ctx.enter_context(nc.sbuf_tensor("exp_" + n, s, t))
        sem = lambda n: nc.alloc_semaphore("exp_" + n)
        ps = lambda n, s: ctx.enter_context(nc.psum_tensor("exp_" + n, s, F32))
        N = k.B * T
        NT = k.NT
        assert NT % RING == 0
        PADS = 2 * NE
        w1, w2 = k.moe_w1, k.moe_w2
        b1 = sb("b1", [P, NE, FF])
        b2 = sb("b2", [P, NE, C])
        rowb = {n: sb(f"rowb_{n}", [P, C]) for n in ("l1_ln2_g", "l1_ln2_b")}
        experts = sb("experts", [P, NE])
        lane = sb("lane", [P, 1])
        pad_ids = sb("pad_ids", [P, 1], I32)
        pad = sb("pad", [P, ROW])
        pad_row = sb("pad_row", [P, PADS])
        pad_slot = sb("pad_slot", [P, PADS], I32)
        number = sb("number", [1, NT])
        tiles_f, tiles_i = sb("tiles_f", [1, NE]), sb("tiles_i", [1, NE], I32)
        ends, jump = sb("ends", [1, NE]), sb("jump", [1, NE])
        reached = sb("reached", [1, NT])
        plan_e, plan_r = sb("plan_e", [1, NT]), sb("plan_r", [1, NT])
        expert_of, row_of = sb("expert_of", [1, NT], I32), sb("row_of", [1, NT], I32)
        rt = [sb(f"rt{i}", [P, ROW]) for i in range(RING)]
        x1T = [sb(f"x1T{i}", [P, CB, P]) for i in range(2)]
        hid = sb("hid", [P, FF])
        hidT = sb("hidT", [P, FB, P])
        t = [sb(f"t{i}", [P, C]) for i in range(RING)]
        stats, mv = sb("stats", [P, 6]), sb("mv", [P, 2, 2])
        pool_pause = sb("pool_pause", [P, 1])
        ve, rstd, pause = sb("ve", [P, 1]), sb("rstd", [P, 2]), sb("pause", [P, 1])
        psX, psH, psT = ps("psX", [P, CB, P]), ps("psH", [P, 2, T]), ps("psT", [P, FB, P])
        psY = ps("psY", [P, C])
        loaded, init, step, plan_done, padded = sem("loaded"), sem("init"), sem("step"), sem("plan_done"), sem("padded")
        plan_loaded, pads_ready = sem("plan_loaded"), sem("pads_ready")
        rt_loaded = [sem(f"rt_loaded{i}") for i in range(RING)]
        scattered = [sem(f"scattered{i}") for i in range(RING)]
        xT_ps, xT_done, hid_ps, hid_done = sem("xT_ps"), sem("xT_done"), sem("hid_ps"), sem("hid_done")
        hT_ps, hT_done, y_done, t_done = sem("hT_ps"), sem("hT_done"), sem("y_done"), sem("t_done")
        tb_done, stats_done, mv_done, ve_done = sem("tb_done"), sem("stats_done"), sem("mv_done"), sem("ve_done")
        rstd_done, zg_done, z_done, u_done = sem("rstd_done"), sem("zg_done"), sem("z_done"), sem("u_done")
        block = ctx.enter_context(nc.Block())
        rounds = NT // RING

        @block.sync
        def _(sp):
            for n, ap in (("experts", experts), ("lane", lane), ("pad_ids", pad_ids), ("number", number)):
                sp.dma_start(ap[:], d[n]).then_inc(plan_loaded, 16)
            for src, ap in (("moe_b1_rows", b1), ("moe_b2_rows", b2)):
                sp.dma_start(ap[:], d[src].partition_broadcast(P)).then_inc(loaded, 16)
            for n, ap in rowb.items():
                sp.dma_start(ap[:], d["rows"][ROWS.index(n)].partition_broadcast(P)).then_inc(loaded, 16)

            def load(c, i, p):
                row = sp.value_load(row_of[0:1, bass.ds(c, 1)], min_val=0, max_val=k.ROWS_ALL - P)
                if i is not None:
                    sp.wait_ge(scattered[p], 16 * i)
                sp.dma_start(rt[p][:], k.rows_dram[bass.ds(row, P), :]).then_inc(rt_loaded[p], 16)

            sp.wait_ge(plan_done, 1)
            sp.wait_ge(padded, 16 * PADS)
            for p in range(RING):
                load(p, None, p)
            with sp.Fori(1, rounds) as i:
                for p in range(RING):
                    load(RING * i + p, i, p)

        @block.vector
        def _(dve):
            taken = [0]

            def follow(instruction):
                taken[0] += 1
                instruction.then_inc(step, 1)
                dve.wait_ge(step, taken[0])

            dve.wait_ge(plan_loaded, 64)
            dve.wait_ge(init, 1)
            nc.vector.tensor_copy(pad[:, ROW_ID:ROW_ID + 1].bitcast(I32), pad_ids[:])
            for n in range(PADS):
                if n < NE:
                    last = nc.vector.tensor_tensor(pad_row[:, n:n + 1], lane[:], k.next_row[:, n:n + 1], ALU.add)
                else:
                    last = nc.vector.tensor_scalar(pad_row[:, n:n + 1], lane[:], float(NE * k.CAP + (n - NE) * P),
                                                   None, ALU.add)
            follow(last)
            nc.vector.tensor_copy(pad_slot[:], pad_row[:]).then_inc(pads_ready, 1)
            follow(nc.vector.tensor_scalar(tiles_f[:], experts[0:1, :], -float(k.CAP), float(P - 1), ALU.mult, ALU.add))
            follow(nc.vector.tensor_tensor(tiles_i[:], tiles_f[:], k.next_row[0:1, :], ALU.add))
            follow(nc.vector.tensor_scalar(tiles_i[:], tiles_i[:], 7, None, ALU.arith_shift_right))
            follow(nc.vector.tensor_copy(tiles_f[:], tiles_i[:]))
            follow(nc.vector.tensor_scalar(jump[:], tiles_f[:], -float(P), float(k.CAP), ALU.mult, ALU.add))
            follow(nc.vector.tensor_copy(ends[:], tiles_f[:]))
            for e in range(1, NE):
                follow(nc.vector.tensor_tensor(ends[:, e:e + 1], ends[:, e:e + 1], ends[:, e - 1:e], ALU.add))
            follow(nc.vector.tensor_scalar(plan_r[:], number[:], float(P), None, ALU.mult))
            follow(nc.vector.memset(plan_e[:], 0.0))
            for e in range(NE):
                follow(nc.vector.tensor_scalar(reached[:], number[:], ends[:, e:e + 1], None, ALU.is_ge))
                follow(nc.vector.tensor_tensor(plan_e[:], plan_e[:], reached[:], ALU.add))
                follow(nc.vector.scalar_tensor_tensor(plan_r[:], reached[:], jump[:, e:e + 1], plan_r[:],
                                                      ALU.mult, ALU.add))
            nc.vector.tensor_scalar(expert_of[:], plan_e[:], float(NE - 1), None, ALU.min)
            nc.vector.tensor_copy(row_of[:], plan_r[:]).then_inc(plan_done, 1)
            dve.wait_ge(plan_done, 1)

            def hidden_bias(c):
                e = dve.value_load(expert_of[0:1, bass.ds(c, 1)], min_val=0, max_val=NE - 1)
                for n in range(2):
                    dve.wait_ge(hid_ps, 2 * c + n + 1)
                    if n == 0:
                        dve.wait_ge(hT_ps, c)
                    nc.vector.tensor_tensor(hid[:, n * T:(n + 1) * T], psH[:, n, :],
                                            b1[:, bass.ds(e, 1), n * T:(n + 1) * T].rearrange("p o f -> p (o f)"),
                                            ALU.add).then_inc(hid_done, 1)

            def moments(c, p):
                e = dve.value_load(expert_of[0:1, bass.ds(c, 1)], min_val=0, max_val=NE - 1)
                dve.wait_ge(y_done, c + 1)
                nc.vector.tensor_tensor(t[p][:], psY[:], rt[p][:, ROW_X1:ROW_X1 + C], ALU.add).then_inc(t_done, 1)
                dve.wait_ge(t_done, c + 1)
                nc.vector.tensor_tensor(t[p][:], t[p][:], b2[:, bass.ds(e, 1), :].rearrange("p o f -> p (o f)"),
                                        ALU.add).then_inc(tb_done, 1)
                dve.wait_ge(tb_done, c + 1)
                nc.vector.bn_stats(stats[:], t[p][:]).then_inc(stats_done, 1)
                dve.wait_ge(stats_done, c + 1)
                nc.vector.memset(pause[:], 0.0)
                nc.vector.bn_aggr(mv[:, p % 2, :], stats[:]).then_inc(mv_done, 1)

            def normalize(c, p):
                dve.wait_ge(rstd_done, c + 1)
                nc.vector.scalar_tensor_tensor(t[p][:], t[p][:], mv[:, p % 2, 0:1], rowb["l1_ln2_g"][:],
                                               ALU.subtract, ALU.mult).then_inc(zg_done, 1)
                dve.wait_ge(zg_done, c + 1)
                nc.vector.scalar_tensor_tensor(t[p][:], t[p][:], rstd[:, p % 2:p % 2 + 1], rowb["l1_ln2_b"][:],
                                               ALU.mult, ALU.add).then_inc(z_done, 1)

            def round_(i, first=False, last=False):
                for p in range(RING):
                    c = RING * i + p
                    if not (first and p == 0):
                        normalize(c - 1, (p - 1) % RING)
                    if not (last and p == RING - 1):
                        hidden_bias(c + 1)
                    moments(c, p)

            dve.wait_ge(loaded, 64)
            hidden_bias(0)
            round_(0, first=True)
            with dve.Fori(1, rounds - 1) as i:
                round_(i)
            round_(rounds - 1, last=True)
            normalize(NT - 1, RING - 1)

        @block.tensor
        def _(pe):
            def expert(c):
                return pe.value_load(expert_of[0:1, bass.ds(c, 1)], min_val=0, max_val=NE - 1)

            def transpose_x(c, i, p):
                pe.wait_ge(rt_loaded[p], 16 * (i + 1))
                pe.wait_ge(xT_done, c)
                for cb in range(CB):
                    last = nc.tensor.transpose(psX[:, cb, :], rt[p][:, ROW_X1 + cb * P:ROW_X1 + (cb + 1) * P],
                                               k.ident[:])
                last.then_inc(xT_ps, 1)

            def hidden(c, p, e):
                pe.wait_ge(xT_done, c + 1)
                for n in range(2):
                    pe.wait_ge(hid_done, 2 * c)
                    for cb in range(CB):
                        last = nc.tensor.matmul(psH[:, n, :], x1T[p][:, cb, :],
                                                w1[:, bass.ds(e, 1), cb, n * T:(n + 1) * T].rearrange("p o f -> p (o f)"),
                                                start=(cb == 0), stop=(cb == CB - 1))
                    last.then_inc(hid_ps, 1)

            def transpose_hidden(c):
                pe.wait_ge(hid_done, 2 * c + 2)
                pe.wait_ge(hT_done, c)
                for f in range(FB):
                    last = nc.tensor.transpose(psT[:, f, :], hid[:, f * P:(f + 1) * P], k.ident[:])
                last.then_inc(hT_ps, 1)

            def output(c, e):
                pe.wait_ge(hT_done, c + 1)
                pe.wait_ge(t_done, c)
                for f in range(FB):
                    last = nc.tensor.matmul(psY[:], hidT[:, f, :],
                                            w2[:, bass.ds(e, 1), f, :].rearrange("p o f -> p (o f)"),
                                            start=(f == 0), stop=(f == FB - 1))
                last.then_inc(y_done, 1)

            def round_(i, last=False):
                for p in range(RING):
                    c = RING * i + p
                    if not (last and p == RING - 1):
                        hidden(c + 1, (p + 1) % 2, expert(c + 1))
                    if not (last and p >= RING - 2):
                        transpose_x(c + 2, i + (p + 2) // RING, (p + 2) % RING)
                    output(c, expert(c))
                    if not (last and p == RING - 1):
                        transpose_hidden(c + 1)

            pe.wait_ge(plan_done, 1)
            pe.wait_ge(k.moe_loaded, 32 * NE)
            transpose_x(0, 0, 0)
            hidden(0, 0, expert(0))
            transpose_hidden(0)
            transpose_x(1, 0, 1)
            round_(0)
            with pe.Fori(1, rounds - 1) as i:
                round_(i)
            round_(rounds - 1, last=True)

        @block.scalar
        def _(act):
            def copy_x(c, p):
                act.wait_ge(xT_ps, c + 1)
                act.wait_ge(hid_ps, 2 * c)
                nc.scalar.activation(x1T[p][:], psX[:], ACT.Copy).then_inc(xT_done, 1)

            def relu(c):
                act.wait_ge(hT_ps, c + 1)
                act.wait_ge(y_done, c)
                nc.scalar.activation(hidT[:], psT[:], ACT.Relu).then_inc(hT_done, 1)

            def round_(i, last=False):
                for p in range(RING):
                    c = RING * i + p
                    if not (last and p >= RING - 2):
                        copy_x(c + 2, p % 2)
                    if not (last and p == RING - 1):
                        relu(c + 1)

            copy_x(0, 0)
            relu(0)
            copy_x(1, 1)
            round_(0)
            with act.Fori(1, rounds - 1) as i:
                round_(i)
            round_(rounds - 1, last=True)

        @block.gpsimd
        def _(pool):
            def rsqrt(c, p):
                pool.wait_ge(mv_done, c + 1)
                nc.gpsimd.tensor_tensor(ve[:], mv[:, p % 2, 1:2], k.eps[:, 0:1], ALU.add).then_inc(ve_done, 1)
                pool.wait_ge(ve_done, c + 1)
                nc.gpsimd.tensor_tensor(rstd[:, p % 2:p % 2 + 1], ve[:], k.minus_half[:, 0:1], ALU.pow
                                        ).then_inc(rstd_done, 1)

            def finish(c, p):
                pool.wait_ge(z_done, c + 1)
                nc.gpsimd.tensor_tensor(t[p][:], t[p][:], rt[p][:, ROW_GATE:ROW_GATE + C], ALU.mult).then_inc(u_done, 1)
                pool.wait_ge(u_done, 2 * c + 1)
                nc.gpsimd.tensor_tensor(t[p][:], t[p][:], rt[p][:, ROW_X:ROW_X + C], ALU.add).then_inc(u_done, 1)
                pool.wait_ge(u_done, 2 * c + 2)
                nc.gpsimd.tensor_tensor(pool_pause[:], k.eps[:, 0:1], k.eps[:, 0:1], ALU.add)
                nc.gpsimd.indirect_dma_start(out, bass.IndirectOffsetOnAxis(
                    ap=rt[p][:, ROW_ID:ROW_ID + 1].bitcast(mybir.dt.uint32), axis=0), t[p][:], None,
                    bounds_check=last_token, oob_is_err=False).then_inc(scattered[p], 16)

            def round_(i, last=False):
                for p in range(RING):
                    finish(RING * i + p, p)
                    if not (last and p == RING - 1):
                        rsqrt(RING * i + p + 1, p + 1)

            last_token = nc.gpsimd.to_reg(N - 1)
            nc.gpsimd.memset(pad[:], 0.0).then_inc(init, 1)
            pool.wait_ge(pads_ready, 1)
            for n in range(PADS):
                nc.gpsimd.indirect_dma_start(k.rows_dram, bass.IndirectOffsetOnAxis(ap=pad_slot[:, n:n + 1], axis=0),
                                             pad[:], None).then_inc(padded, 16)
            rsqrt(0, 0)
            round_(0)
            with pool.Fori(1, rounds - 1) as i:
                round_(i)
            round_(rounds - 1, last=True)
            for p in range(RING):
                pool.wait_ge(scattered[p], 16 * rounds)


def cleared(nc):
    return nc.cleanup_on_exit()


def build(nc, d, out, B, upto="all"):
    k = Core()
    k.B = B
    with ExitStack() as ctx:
        sb = lambda n, s, t=F32: ctx.enter_context(nc.sbuf_tensor(n, s, t))
        k.x = sb("x_res", [P, B * J, C])
        k.mod = sb("mod", [P, 2, 12, B])
        k.cols = sb("cols_sb", [P, NCOLS])
        k.ident = sb("ident_sb", [P, P])
        k.ident_bf = sb("ident_bf", [P, P], BF16)
        k.mask_bf = sb("mask_bf", [P, P], BF16)
        k.half = sb("half", [P, T])
        k.eps = sb("eps", [P, J])
        k.minus_half = sb("minus_half", [P, J])
        k.mrows_dram = nc.dram_tensor("mrows", (len(MROWS), B, C), F32, kind="Internal").ap()
        init = ctx.enter_context(nc.semaphore("consts"))
        with nc.Block() as block:
            @block.gpsimd
            def _(pool):
                nc.gpsimd.memset(k.eps[:], EPS)
                nc.gpsimd.memset(k.minus_half[:], -0.5).then_inc(init, 1)
                pool.wait_ge(init, 1)
        with cleared(nc):
            setup_phase(nc, k, d)
        k.parts_dram = nc.dram_tensor("parts_dram", (B, 3, 2 * CB, P, T), BF16, kind="Internal").ap()
        k.att_dram = nc.dram_tensor("att_dram", (B, P, J, C), F32, kind="Internal").ap()
        k.v_dram = nc.dram_tensor("v_dram", (B, P, J, C), F32, kind="Internal").ap()
        with cleared(nc):
            retention_phase(nc, k, d)
        if upto != "A":
            with cleared(nc):
                channel_mix_phase(nc, k, d)
        if upto not in "AB":
            with cleared(nc):
                rotary_qkv_phase(nc, k, d)
            with cleared(nc):
                attention_phase(nc, k, "causal", True)
            with cleared(nc):
                output_and_qkv_phase(nc, k, d)
        if upto == "all":
            with cleared(nc):
                attention_phase(nc, k, "full", False)
            k.CAP = B * T + P
            k.ROWS_ALL = NE * k.CAP + NE * P
            k.NT = B * J + NE
            k.rows_dram = nc.dram_tensor("rows_dram", (k.ROWS_ALL, ROW), F32, kind="Internal").ap()
            k.next_row = sb("next_row", [P, NE])
            k.moe_w1 = sb("moe_w1", [P, NE, CB, FF])
            k.moe_w2 = sb("moe_w2", [P, NE, FB, C])
            k.moe_loaded = ctx.enter_context(nc.semaphore("moe_loaded"))
            with cleared(nc):
                route_phase(nc, k, d)
            with cleared(nc):
                expert_phase(nc, k, d, out.rearrange("n p c -> (n p) c"))
            return
        stored = ctx.enter_context(nc.semaphore("x_stored"))
        with nc.Block() as block:
            @block.sync
            def _(sp):
                sp.dma_start(out.rearrange("n p c -> p n c"), k.x[:]).then_inc(stored, 16)
                sp.wait_ge(stored, 16)


def lay_out(inp):
    import numpy as np
    f = lambda n: np.asarray(inp[n])
    B = f("L0_c").shape[0]
    columns = lambda v: np.asarray(v).reshape(-1, P).T
    A, R, E = "L0_attn_", "L0_ffn_", "L1_ffn_"
    cols = {"b_ret": f(A + "b_ret"), "ln1_scale": f(A + "ln1_scale"), "ln1_bias": f(A + "ln1_bias"), "b1": f(A + "b1"),
            "mu_r": f(R + "mu_r"), "mu_k": f(R + "mu_k"), "bq": f(E + "bq"), "bk": f(E + "bk"),
            "l1_ln1_g": f(E + "ln1_g"), "l1_ln1_b": f(E + "ln1_b"),
            "router_b": np.broadcast_to(f(E + "router_b"), (P,))}
    rows = {"ln1_scale": f(A + "ln1_scale"), "ln1_bias": f(A + "ln1_bias"), "b2": f(A + "b2"),
            "ln2_scale": f(A + "ln2_scale"), "ln2_bias": f(A + "ln2_bias"), "bv": f(E + "bv"), "bo": f(E + "bo"),
            "l1_ln1_g": f(E + "ln1_g"), "l1_ln1_b": f(E + "ln1_b"), "router_w": f(E + "router_w")[:, 0],
            "l1_ln2_g": f(E + "ln2_g"), "l1_ln2_b": f(E + "ln2_b")}
    angle = np.arange(T, dtype=np.float32)[:, None] / np.power(
        np.float32(10000.0), np.arange(0, HD, 2, dtype=np.float32)[None, :] / np.float32(HD))
    angle = angle.astype(np.float32).reshape(J, P, HD // 2).transpose(1, 0, 2)
    cos = np.concatenate([np.cos(angle), np.cos(angle)], axis=2)
    sin = np.concatenate([-np.sin(angle), np.sin(angle)], axis=2)
    arrays = {
        "x": f("L0_attn_x").reshape(B * J, P, C),
        "cT0": f("L0_c").T, "cT1": f("L1_c").T, "wmod0": f("L0_wmod"), "wmod1": f("L1_wmod"),
        "cols": np.concatenate([columns(cols[n]) for n in COLS], axis=1),
        "rows": np.stack([rows[n] for n in ROWS]),
        "mask": np.triu(np.full((P, P), -1e9, np.float32), 1),
        "w_out": f("L1_attn_w_out"), "Wq": f(E + "Wq"), "Wk": f(E + "Wk"), "Wv": f(E + "Wv"), "Wo": f(E + "Wo"),
        "moe_W1": f(E + "W1"), "moe_W2": f(E + "W2"), "moe_b1_rows": f(E + "b1"), "moe_b2_rows": f(E + "b2"),
        "before": np.triu(np.ones((P, P), np.float32), 1),
        "experts": np.broadcast_to(np.arange(NE, dtype=np.float32), (P, NE)),
        "ids": np.arange(B * T, dtype=np.int32).reshape(B * J, P).T,
        "lane": np.arange(P, dtype=np.float32)[:, None],
        "pad_ids": (B * T + np.arange(P, dtype=np.int32))[:, None],
        "number": np.arange(B * J + NE, dtype=np.float32)[None, :],
        "ident": np.eye(P, dtype=np.float32),
        "W_rT": f(R + "W_r").T, "W_kT": f(R + "W_k").T, "W_vT": f(R + "W_v").T,
        "w_qkv": f("L1_attn_w_qkv"), "cos": cos, "sin": sin,
        "W_ret": f(A + "W_ret"), "W1": f(A + "W1"), "W2": f(A + "W2"),
    }
    return {n: np.ascontiguousarray(a) for n, a in arrays.items()}


def kernel(**inputs):
    import numpy as np
    import concourse.bacc as bacc
    from concourse.bass_utils import run_bass_kernel_spmd

    arrays = lay_out(inputs)
    B = arrays["cT0"].shape[1]
    nc = bacc.Bacc("TRN2", target_bir_lowering=False, num_devices=1)
    d = {n: nc.dram_tensor(f"in_{n}", a.shape, mybir.dt.from_np(a.dtype), kind="ExternalInput").ap()
         for n, a in arrays.items()}
    out = nc.dram_tensor("out", (B * J, P, C), F32, kind="ExternalOutput").ap()
    build(nc, d, out, B)
    result = run_bass_kernel_spmd(nc, [{f"in_{n}": a for n, a in arrays.items()}], core_ids=[0])
    return result.results[0]["out"].reshape(B, T, C)
```
